# Optimizing a Trainium2 kernel written in Bass

```python
import numpy as np
import jax
import jax.numpy as jnp

def _softmax(x, axis=-1):
    return jax.nn.softmax(x, axis=axis)

def _gelu(x):
    return jax.nn.gelu(x, approximate=True)

def _silu(x):
    return jax.nn.silu(x)

def _sigmoid(x):
    return jax.nn.sigmoid(x)

def _layernorm(x, axis=-1, eps=1e-05):
    m = jnp.mean(x, axis=axis, keepdims=True)
    v = jnp.var(x, axis=axis, keepdims=True)
    return (x - m) / jnp.sqrt(v + eps)

def _scatter_add(tgt, idx, src, axis=0):
    return tgt.at[idx].add(src)

def _segment_sum(src, seg, n):
    return jax.ops.segment_sum(src, seg, n)
kernel_name = 'mk_gnn_resnorm_d4_gnn_r32_164f5d'

def setup_inputs(seed: int=0):
    np.random.seed(seed)
    _w = jnp.asarray

    def _rec_inputs():
        import jax
        import jax.numpy as jnp
        _gk = jax.random.key(seed)
        x = -0.0003713 + 1 * jax.random.normal(jax.random.fold_in(_gk, 1), (3125, 256), jnp.float32)
        _s = jax.random.randint(jax.random.fold_in(_gk, 2), (25000,), 0, 3125, jnp.int32)
        _d = jax.random.randint(jax.random.fold_in(_gk, 3), (25000,), 0, 3125, jnp.int32)
        _loop = jnp.arange(3125, dtype=jnp.int32)
        src = jnp.concatenate([_s, _d, _loop])
        dst = jnp.concatenate([_d, _s, _loop])
        _o = jnp.argsort(dst, stable=True)
        src = src[_o]
        dst = dst[_o]
        edge_attr_4 = jax.random.uniform(jax.random.fold_in(_gk, 11), (53125, 4), jnp.float32, 0.0, 0.999999)
        return (x, src, dst, edge_attr_4)
    x, src, dst, edge_attr_4 = _rec_inputs()

    def _L0_gnn_setup():
        import jax, jax.numpy as jnp
        import numpy as np
        N_NODES = 50000
        N_EDGES = 10000
        HIDDEN = 256
        N_LAYERS = 5
        BN_EPS = 1e-05

        def _mpnn(x, edge_index, edge_attr, mlp_w, mlp_b, ew1, ew2, bn_g, bn_b):
            n = x.shape[0]
            row, col = (edge_index[0], edge_index[1])
            deg = jax.ops.segment_sum(jnp.ones((edge_index.shape[1],), x.dtype), col, num_segments=n)
            dinv = jnp.where(deg > 0, deg ** (-0.5), 0.0)
            norm = dinv[row] * dinv[col]
            h = x
            for l in range(N_LAYERS):
                edge_fea = jnp.concatenate([edge_attr[:, 3:] @ ew1[l], edge_attr[:, 0:3] @ ew2[l]], axis=-1)
                msg = norm[:, None] * (h[row] + edge_fea)
                agg = jax.ops.segment_sum(msg, col, num_segments=n)
                h = jax.nn.relu(jnp.concatenate([h, agg], axis=1) @ mlp_w[l] + mlp_b[l])
                mu = h.mean(axis=0)
                var = h.var(axis=0)
                h = (h - mu) * jax.lax.rsqrt(var + BN_EPS) * bn_g[l] + bn_b[l]
                if l != N_LAYERS - 1:
                    h = jax.nn.relu(h)
            return h
        key = jax.random.key(seed)
        ks = jax.random.split(key, 8)
        x = jax.random.normal(ks[0], (N_NODES, HIDDEN), dtype=jnp.float32)
        edge_index = jax.random.randint(ks[1], (2, N_EDGES), 0, N_NODES, dtype=jnp.int64)
        edge_attr = jax.random.uniform(ks[2], (N_EDGES, 4), dtype=jnp.float32)
        mlp_w = jax.random.normal(ks[3], (N_LAYERS, 2 * HIDDEN, HIDDEN), dtype=jnp.float32) * (1.0 / np.sqrt(2 * HIDDEN))
        mlp_b = jnp.zeros((N_LAYERS, HIDDEN), dtype=jnp.float32)
        ew1 = jax.random.normal(ks[4], (N_LAYERS, 1, HIDDEN // 2), dtype=jnp.float32)
        ew2 = jax.random.normal(ks[5], (N_LAYERS, 3, HIDDEN // 2), dtype=jnp.float32) * (1.0 / np.sqrt(3.0))
        bn_g = jnp.ones((N_LAYERS, HIDDEN), dtype=jnp.float32)
        bn_b = jnp.zeros((N_LAYERS, HIDDEN), dtype=jnp.float32)
        return {'x': x, 'edge_index': edge_index, 'edge_attr': edge_attr, 'mlp_w': mlp_w, 'mlp_b': mlp_b, 'ew1': ew1, 'ew2': ew2, 'bn_g': bn_g, 'bn_b': bn_b}
    _L0_gnn_all = _L0_gnn_setup()
    _L0_gnn_in = {k: v for k, v in _L0_gnn_all.items() if k in ('mlp_w', 'mlp_b', 'ew1', 'ew2', 'bn_g', 'bn_b')}
    del _L0_gnn_all

    def _L1_gnn_setup():
        import jax, jax.numpy as jnp
        import numpy as np
        N_NODES = 3125
        IN_FEATS = 256
        OUT_FEATS = 256
        N_EDGES = 100000
        key = jax.random.key(seed)
        k1, k2, k3, k4 = jax.random.split(key, 4)
        x = jax.random.normal(k1, (N_NODES, IN_FEATS), dtype=jnp.float32)
        edge_index = jax.random.randint(k2, (2, N_EDGES), 0, N_NODES, dtype=jnp.int64)
        scale = 1.0 / np.sqrt(IN_FEATS)
        W = jax.random.uniform(k3, (IN_FEATS, OUT_FEATS), dtype=jnp.float32, minval=-scale, maxval=scale)
        b = jax.random.uniform(k4, (OUT_FEATS,), dtype=jnp.float32, minval=-scale, maxval=scale)
        return {'x': x, 'edge_index': edge_index, 'W': W, 'b': b}
    _L1_gnn_all = _L1_gnn_setup()
    _L1_gnn_in = {k: v for k, v in _L1_gnn_all.items() if k in ('W', 'b')}
    del _L1_gnn_all

    def _L2_gnn_setup():
        import jax, jax.numpy as jnp
        import numpy as np
        N_NODES = 10000
        N_EDGES = 10000
        C = 256

        def gcn_conv(x, edge_index, W, b, num_nodes):
            src = edge_index[0]
            dst = edge_index[1]
            loop = jnp.arange(num_nodes, dtype=edge_index.dtype)
            src = jnp.concatenate([src, loop])
            dst = jnp.concatenate([dst, loop])
            ones = jnp.ones(src.shape[0], dtype=x.dtype)
            deg = jax.ops.segment_sum(ones, dst, num_segments=num_nodes)
            dinv = jnp.where(deg > 0, jax.lax.rsqrt(deg), 0.0)
            norm = dinv[src] * dinv[dst]
            h = x @ W
            msg = h[src] * norm[:, None]
            out = jax.ops.segment_sum(msg, dst, num_segments=num_nodes)
            return out + b

        def gcn_block(x, edge_index, W, b, num_nodes):
            z = gcn_conv(x, edge_index, W, b, num_nodes)
            z = jax.nn.relu(z)
            return x + z
        key = jax.random.key(seed)
        k1, k2, k3, k4 = jax.random.split(key, 4)
        x = jax.random.normal(k1, (N_NODES, C), dtype=jnp.float32)
        edge_index = jax.random.randint(k2, (2, N_EDGES), 0, N_NODES, dtype=jnp.int64)
        s = 1.0 / np.sqrt(C)
        W1 = jax.random.uniform(k3, (C, C), jnp.float32, -s, s)
        b1 = jnp.zeros((C,), jnp.float32)
        W2 = jax.random.uniform(k4, (C, C), jnp.float32, -s, s)
        b2 = jnp.zeros((C,), jnp.float32)
        return {'x': x, 'edge_index': edge_index, 'W1': W1, 'b1': b1, 'W2': W2, 'b2': b2}
    _L2_gnn_all = _L2_gnn_setup()
    _L2_gnn_in = {k: v for k, v in _L2_gnn_all.items() if k in ('W1', 'b1', 'W2', 'b2')}
    del _L2_gnn_all

    def _L3_gnn_setup():
        import jax, jax.numpy as jnp
        import numpy as np
        N_NODES = 3125
        N_EDGES = 50000
        D_IN = 256
        D_OUT = 256
        key = jax.random.key(seed)
        k1, k2, k3, k4 = jax.random.split(key, 4)
        x = jax.random.normal(k1, (N_NODES, D_IN), dtype=jnp.float32)
        edge_index = jax.random.randint(k2, (2, N_EDGES), 0, N_NODES, dtype=jnp.int64)
        W = jax.random.normal(k3, (D_OUT, D_IN), dtype=jnp.float32) * (1.0 / np.sqrt(D_IN))
        b = jax.random.normal(k4, (D_OUT,), dtype=jnp.float32) * 0.01
        return {'x': x, 'edge_index': edge_index, 'W': W, 'b': b}
    _L3_gnn_all = _L3_gnn_setup()
    _L3_gnn_in = {k: v for k, v in _L3_gnn_all.items() if k in ('W', 'b')}
    del _L3_gnn_all
    return {'x': x, 'src': src, 'dst': dst, 'edge_attr_4': edge_attr_4, 'L0_gnn_mlp_w': _L0_gnn_in['mlp_w'], 'L0_gnn_mlp_b': _L0_gnn_in['mlp_b'], 'L0_gnn_ew1': _L0_gnn_in['ew1'], 'L0_gnn_ew2': _L0_gnn_in['ew2'], 'L0_gnn_bn_g': _L0_gnn_in['bn_g'], 'L0_gnn_bn_b': _L0_gnn_in['bn_b'], 'L1_gnn_W': _L1_gnn_in['W'], 'L1_gnn_b': _L1_gnn_in['b'], 'L2_gnn_W1': _L2_gnn_in['W1'], 'L2_gnn_b1': _L2_gnn_in['b1'], 'L2_gnn_W2': _L2_gnn_in['W2'], 'L2_gnn_b2': _L2_gnn_in['b2'], 'L3_gnn_W': _L3_gnn_in['W'], 'L3_gnn_b': _L3_gnn_in['b']}

def reference(x, src, dst, edge_attr_4, L0_gnn_mlp_w, L0_gnn_mlp_b, L0_gnn_ew1, L0_gnn_ew2, L0_gnn_bn_g, L0_gnn_bn_b, L1_gnn_W, L1_gnn_b, L2_gnn_W1, L2_gnn_b1, L2_gnn_W2, L2_gnn_b2, L3_gnn_W, L3_gnn_b):
    import jax
    import jax.numpy as jnp

    def _L0_gnn_ref(x, edge_index, edge_attr, mlp_w, mlp_b, ew1, ew2, bn_g, bn_b):
        import jax, jax.numpy as jnp
        import numpy as np
        N_NODES = 50000
        N_EDGES = 10000
        HIDDEN = 256
        N_LAYERS = 5
        BN_EPS = 1e-05

        def _mpnn(x, edge_index, edge_attr, mlp_w, mlp_b, ew1, ew2, bn_g, bn_b):
            n = x.shape[0]
            row, col = (edge_index[0], edge_index[1])
            deg = jax.ops.segment_sum(jnp.ones((edge_index.shape[1],), x.dtype), col, num_segments=n)
            dinv = jnp.where(deg > 0, deg ** (-0.5), 0.0)
            norm = dinv[row] * dinv[col]
            h = x
            for l in range(N_LAYERS):
                edge_fea = jnp.concatenate([edge_attr[:, 3:] @ ew1[l], edge_attr[:, 0:3] @ ew2[l]], axis=-1)
                msg = norm[:, None] * (h[row] + edge_fea)
                agg = jax.ops.segment_sum(msg, col, num_segments=n)
                h = jax.nn.relu(jnp.concatenate([h, agg], axis=1) @ mlp_w[l] + mlp_b[l])
                mu = h.mean(axis=0)
                var = h.var(axis=0)
                h = (h - mu) * jax.lax.rsqrt(var + BN_EPS) * bn_g[l] + bn_b[l]
                if l != N_LAYERS - 1:
                    h = jax.nn.relu(h)
            return h
        return _mpnn(x, edge_index, edge_attr, mlp_w, mlp_b, ew1, ew2, bn_g, bn_b)

    def _L1_gnn_ref(x, edge_index, W, b):
        import jax, jax.numpy as jnp
        import numpy as np
        N_NODES = 3125
        IN_FEATS = 256
        OUT_FEATS = 256
        N_EDGES = 100000
        n = x.shape[0]
        row = edge_index[0]
        col = edge_index[1]
        h = x @ W + b
        agg = jax.ops.segment_sum(h[col], row, num_segments=n)
        deg = jax.ops.segment_sum(jnp.ones((edge_index.shape[1],), dtype=h.dtype), row, num_segments=n)
        inv_deg = jnp.where(deg > 0, 1.0 / jnp.where(deg > 0, deg, 1.0), 0.0)
        return agg * inv_deg[:, None]

    def _L2_gnn_ref(x, edge_index, W1, b1, W2, b2):
        import jax, jax.numpy as jnp
        import numpy as np
        N_NODES = 10000
        N_EDGES = 10000
        C = 256

        def gcn_conv(x, edge_index, W, b, num_nodes):
            src = edge_index[0]
            dst = edge_index[1]
            loop = jnp.arange(num_nodes, dtype=edge_index.dtype)
            src = jnp.concatenate([src, loop])
            dst = jnp.concatenate([dst, loop])
            ones = jnp.ones(src.shape[0], dtype=x.dtype)
            deg = jax.ops.segment_sum(ones, dst, num_segments=num_nodes)
            dinv = jnp.where(deg > 0, jax.lax.rsqrt(deg), 0.0)
            norm = dinv[src] * dinv[dst]
            h = x @ W
            msg = h[src] * norm[:, None]
            out = jax.ops.segment_sum(msg, dst, num_segments=num_nodes)
            return out + b

        def gcn_block(x, edge_index, W, b, num_nodes):
            z = gcn_conv(x, edge_index, W, b, num_nodes)
            z = jax.nn.relu(z)
            return x + z
        n = x.shape[0]
        x = gcn_block(x, edge_index, W1, b1, n)
        x = gcn_block(x, edge_index, W2, b2, n)
        return x

    def _L3_gnn_ref(x, edge_index, W, b):
        import jax, jax.numpy as jnp
        import numpy as np
        N_NODES = 3125
        N_EDGES = 50000
        D_IN = 256
        D_OUT = 256
        h = jnp.einsum('nd,od->no', x, W) + b
        row, col = (edge_index[0], edge_index[1])
        msgs = h[col]
        out = jax.ops.segment_sum(msgs, row, num_segments=h.shape[0])
        return out
    edge_index = jnp.stack([src, dst])
    x = _layernorm(x + _L0_gnn_ref(x, edge_index, edge_attr_4, L0_gnn_mlp_w, L0_gnn_mlp_b, L0_gnn_ew1, L0_gnn_ew2, L0_gnn_bn_g, L0_gnn_bn_b), axis=-1)
    x = _layernorm(x + _L1_gnn_ref(x, edge_index, L1_gnn_W, L1_gnn_b), axis=-1)
    x = _layernorm(x + _L2_gnn_ref(x, edge_index, L2_gnn_W1, L2_gnn_b1, L2_gnn_W2, L2_gnn_b2), axis=-1)
    x = _layernorm(x + _L3_gnn_ref(x, edge_index, L3_gnn_W, L3_gnn_b), axis=-1)
    return x

_drawn_inputs = setup_inputs


def setup_inputs(seed=0):
    import zlib

    import numpy as np

    out = dict(_drawn_inputs(seed))
    spreads = {'L0_gnn_mlp_b': (0.0, 0.1),
     'L0_gnn_bn_g': (1.0, 0.2),
     'L0_gnn_bn_b': (0.0, 0.1),
     'L2_gnn_b1': (0.0, 0.1),
     'L2_gnn_b2': (0.0, 0.1)}
    factors = {}
    for name, (base, spread) in spreads.items():
        noise = np.random.default_rng([zlib.crc32(name.encode()), seed]).standard_normal(out[name].shape)
        drawn = base * np.exp(spread * noise) if base else spread * noise
        out[name] = jnp.asarray(drawn.astype(out[name].dtype))
    for name, factor in factors.items():
        out[name] = (out[name] * factor).astype(out[name].dtype)
    return out
```

```python
import concourse.bass as bass
from concourse import mybir
from contextlib import ExitStack

P = 128
N = 3125
F = 256
E = 53125
LAYERS = 5
EPS = 1e-5

NB = -(-N // P)
NR = NB * P
TAIL = N - (NB - 1) * P
CH = 7
CW = 448
NPAD = CH * CW
LASTW = N - (CH - 1) * CW
SUBS = 4
SW = CW // SUBS
GB = 5
NG = NB // GB
GW = GB * P
CF = NB * CW

EC = -(-E // P)
ELAST = E - (P - 1) * EC
EB = 8
WD = 16
NW = NPAD // WD
NWH = [P, NW - P]
KW = 3
NK = KW * NW
COPIES = 8
FLD = 5
ROWE = P * FLD
CPR = 1 + EC + 4
GAP = CPR * P - EC * P - WD
ROUNDS = -(-E // (KW * P))
TURNS = SUBS * NG
GWIN = 4
CSTEP = CW // (WD * GWIN)
STEPS = CH * CSTEP
HC = NB * WD

START1, START2, START16 = 1, 2, 16

S_BN = 256.0
S_LN = 2048.0
S_TAB = 4096.0

INPUTS = ["x", "src", "dst", "edge_attr_4", "L0_gnn_mlp_w", "L0_gnn_mlp_b", "L0_gnn_ew1", "L0_gnn_ew2",
          "L0_gnn_bn_g", "L0_gnn_bn_b", "L1_gnn_W", "L1_gnn_b", "L2_gnn_W1", "L2_gnn_b1", "L2_gnn_W2",
          "L2_gnn_b2", "L3_gnn_W", "L3_gnn_b"]


class Steps:

    def __init__(self, eng, sem):
        self.eng, self.sem, self.n = eng, sem, 0

    def __call__(self, ins):
        ins.then_inc(self.sem, 1)
        self.n = self.n + 1
        self.eng.wait_ge(self.sem, self.n)


def build(nc, x, src, dst, attr, mlp_w, mlp_b, ew1, ew2, bn_g, bn_b, w_1, b_1, w_21, b_21, w_22, b_22,
          w_3, b_3, out):
    f32, f16, bf16, i32 = mybir.dt.float32, mybir.dt.float16, mybir.dt.bfloat16, mybir.dt.int32
    ALU = mybir.AluOpType
    ACT = mybir.ActivationFunctionType
    AX = mybir.AxisListType
    ds = bass.ds

    def flat(ap, offset, dims):
        return bass.AP(ap.tensor, offset, dims)

    ctx = ExitStack()
    with ctx:
        def sb(name, shape, dt):
            return ctx.enter_context(nc.sbuf_tensor(name, shape, dt))

        def sem(name):
            return ctx.enter_context(nc.semaphore(name))

        def dram(name, shape, dt):
            return nc.dram_tensor(name, shape, dt).ap()

        slo_row = dram("slo_row", (P, EC), f16)
        table = dram("edge_table", (COPIES * CPR, ROWE), f32)
        adj_dram = dram("adj_dram", (NR, NR), f16)
        adjT_dram = dram("adjT_dram", (NR, NR), f16)
        dinv_row = dram("dinv_row", (NR,), f32)
        dinv2_row = dram("dinv2_row", (NR,), f32)
        dout_row = dram("dout_row", (NR,), f32)
        edge_sum = dram("edge_sum", (12, NPAD), f32)
        hT = dram("hT", (2, P, NR), f32)
        rawT = dram("rawT", (2, P, NR), f32)
        xs = [dram(f"x{i}", (NR, F), f32) for i in range(1, 5)]

        adj = sb("adj", [P, CH * CF], f16)
        work = sb("work", [P, 12672], f32)
        adj32 = adj[:, :].bitcast(f32)

        def cut(base, at, n, dt=f32):
            v = base[:, at:at + n]
            return v if dt == f32 else v.bitcast(dt)

        slo_bc = cut(adj32, 0, 26624, f16)
        oh_hi = cut(adj32, 26624, 5200, f16).rearrange("p (e b) -> p e b", b=NB)
        src_i = cut(adj32, 31824, EC, i32)
        dst_i = cut(adj32, 32240, EC, i32)
        dlo_i = cut(adj32, 32656, EC, i32)
        dhi_i = cut(adj32, 33072, EC, i32)
        slo_i = cut(adj32, 33488, EC, i32)
        shi_i = cut(adj32, 33904, EC, i32)
        dlo_f = cut(adj32, 34320, EC)
        dhi_h = cut(adj32, 34736, EC // 2, f16)
        slo_h = cut(adj32, 34944, EC // 2, f16)
        shi_h = cut(adj32, 35152, EC // 2, f16)
        cmp_h = cut(adj32, 35360, NW * 26 // 2, f16).rearrange("p (w g) -> p w g", g=26)
        degs = cut(adj32, 37908, 600).rearrange("p (i t b) -> p i t b", t=2, b=NB)
        att = cut(work, 0, 4 * EC).rearrange("p (e k) -> p e k", k=4)
        tab = cut(work, 1664, FLD * EC).rearrange("p (e k) -> p e k", k=FLD)
        sent = cut(work, 3744, GAP * FLD).rearrange("p (e k) -> p e k", k=FLD)
        hring = cut(work, 6864, 1024, f16).rearrange("p (s c) -> p s c", c=P)
        sel = [cut(work, 7888 + 400 * i, 400) for i in range(2)]
        dinvs = cut(work, 8688, EC)
        part = cut(work, 9104, NW)
        dwl_i = cut(work, 9300, 26, i32)
        dwl_h = cut(work, 9326, 13, f16)
        zeros = cut(work, 9340, 800)
        win = [cut(work, 0, KW * ROWE), cut(work, 1920, KW * ROWE)]
        ring1 = cut(work, 0, 768, f16).rearrange("p (s c) -> p s c", c=P)
        ring2 = cut(work, 768, 2400, f16).rearrange("p (s c) -> p s c", c=HC)
        ringd = cut(work, 3168, 96, bf16).rearrange("p (k w c) -> p k w c", k=KW, c=WD)
        es_out = cut(work, 3264, CW)
        key_i = cut(work, 3840, NK, i32)
        fa_i = cut(work, 4428, NK, i32)
        fb_i = cut(work, 5016, NK, i32)
        mask = cut(work, 5604, NK)
        slom = cut(work, 6192, NK)
        key2 = cut(work, 6780, NK)
        dlom = cut(work, 7368, NK)
        v3 = cut(work, 7956, 6 * NK, bf16).rearrange("p (e c) -> p e c", c=12)
        rest1 = cut(work, 3840, NK)
        rest2 = cut(work, 4428, NK)
        iot_i = cut(work, 11484, HC, i32)
        iot = cut(work, 11884, HC // 2, f16)
        ones_f = cut(work, 12084, P)
        ones_h = cut(work, 12212, 64, f16)
        zero_h = cut(work, 12276, 64, f16)
        parts = cut(work, 0, 6400, f16).rearrange("p (t b f) -> p t b f", t=2, f=F)
        rbuf = [cut(work, 6400 + 1280 * i, 1280) for i in range(2)]
        agg = cut(work, 8960, 2 * CW).rearrange("p (h n) -> p h n", h=2)
        nraw = cut(work, 9856, 2 * CW).rearrange("p (h n) -> p h n", h=2)
        wl = cut(work, 10752, 4 * F).rearrange("p (k n) -> p k n", k=4)
        bc = cut(work, 11776, CW)
        es = cut(work, 12224, CW)
        turn = [cut(work, 6400 + 1280 * i + 2 * CW, GW // 2, f16) for i in range(2)]
        xgrp = cut(work, 8960, GB * F)
        wd = cut(work, 9856, 2 * F).rearrange("p (h n) -> p h n", h=2)
        bias = cut(work, 10368, F)
        xr2 = cut(work, 10624, SUBS * F).rearrange("p (s f) -> p s f", f=F)
        tmp = cut(work, 11648, SUBS * F).rearrange("p (s f) -> p s f", f=F)
        wt = cut(work, 10624, 2 * F).rearrange("p (h n) -> p h n", h=2)

        pidx = sb("pidx", [P, 1], f32)
        pidx_i = sb("pidx_i", [P, 1], i32)
        ident = sb("ident", [P, P], f32)
        ident_h = sb("ident_h", [P, P], f16)
        dtab = sb("dtab", [P, 2, NB], f16)
        scl = sb("scl", [P, 2, NB], f32)
        idx = sb("idx", [P, 2 * KW], i32)
        starts = sb("starts", [P, 2, 4], i32)
        flag_f = sb("flag_f", [P, 2], f32)
        flag = sb("flag", [P, 1], i32)
        dop = sb("dop", [P, CH + 1, NB], f32)
        fcol = sb("fcol", [P, 3, LAYERS, 2], f32)
        ewt = sb("ewt", [12, F], f32)
        stats = sb("stats", [P, 2, CH, 6], f32)
        mv = sb("mv", [P, 2, 2], f32)
        bnsc = sb("bnsc", [P, 4, 2], f32)
        nrow = sb("nrow", [SW, 4, CH * SUBS], f32)
        ln_st = sb("ln_st", [P, GB, 6], f32)
        ln_mv = sb("ln_mv", [P, GB, 2], f32)
        ln_r = sb("ln_r", [P, 2, GB], f32)

        ps = ctx.enter_context(nc.psum_tensor("ps", [P, 8 * 512], f32))

        def bank(i, n=1):
            return ps[:, 512 * i:512 * (i + n)]

        acc = [[bank(2 * t + h)[:, 0:CW] for h in range(2)] for t in range(2)]
        lin = bank(4, 2)
        lin_h = [bank(4)[:, 0:CW], bank(5)[:, 0:CW]]
        lin_s = lin.rearrange("p (s f) -> p s f", f=F)
        turn_ps = [bank(6 + t)[0:SW, 0:GW // 2].bitcast(f16) for t in range(2)]
        ptr = [bank(0, 3), bank(3, 3)]

        def adj_chunk(c):
            return adj[:, ds(c * CF, CF)].rearrange("p (b n) -> p b n", n=CW)

        (consts_i, consts, zeros_set, zero_stored, edges_loaded, fields_done, slo_stored, slo_loaded,
         hist_ready, hist_used, deg_done, root_in, root_out, onehot_t, tab_ready, sel_ready, sel_used,
         table_done, table_stored, part_ready, starts_ready, idx_ready, rows_stored,
         built, flag_ready, captured, cap_summed, adj_stored, dout_part, dout_ready, dout_stored,
         rows_loaded, dve_step, pool_step, es_zeroed, vec_step, pad_step, settled, es_free, adj_turned, adj_turned_out, turn_even, turn_odd) = [sem(n) for n in (
             "consts_i consts zeros_set zero_stored edges_loaded fields_done slo_stored slo_loaded "
             "hist_ready hist_used deg_done root_in root_out onehot_t tab_ready sel_ready sel_used "
             "table_done table_stored part_ready starts_ready idx_ready rows_stored "
             "built flag_ready captured cap_summed adj_stored dout_part dout_ready dout_stored "
             "rows_loaded dve_step pool_step es_zeroed vec_step pad_step settled es_free adj_turned adj_turned_out turn_even turn_odd").split()]

        def settle(eng):
            eng.sem_inc(settled, 1)

        class Build:

            def __init__(self, way):
                self.gathered = sem(f"gathered_{way}")
                self.turned = sem(f"turned_{way}")
                self.turned_used = sem(f"turned_used_{way}")
                self.ring_ready = sem(f"ring_ready_{way}")
                self.ring_used = sem(f"ring_used_{way}")
                self.sums_done = sem(f"sums_done_{way}")
                self.win_kept = sem(f"win_kept_{way}")
                self.sums_kept = sem(f"sums_kept_{way}")
                self.es_stored = sem(f"es_stored_{way}")

        fast, slow = Build("fast"), Build("slow")

        (parts_hi, parts_lo, agg_evac, spmm_done, lin_done, lin_evac, hT_even, hT_odd, w_loaded, bc_loaded,
         es_loaded, raw_stored, stats_done, var_ready, std_ready, bn_ready, grp_even, grp_odd, norm_done,
         turned_grp, hT_stored, xT_done, fcol_loaded, x_loaded, op_loaded, eye_added, y_ready, x_stored,
         wt_done, wt_kept, bias_loaded, xr_even, xr_odd, xr2_loaded, ln_var, ln_std, pad_set, ln_rows) = [sem(n) for n in (
             "parts_hi parts_lo agg_evac spmm_done lin_done lin_evac hT_even hT_odd w_loaded bc_loaded "
             "es_loaded raw_stored stats_done var_ready std_ready bn_ready grp_even grp_odd norm_done "
             "turned_grp hT_stored xT_done fcol_loaded x_loaded op_loaded eye_added y_ready x_stored "
             "wt_done wt_kept bias_loaded xr_even xr_odd xr2_loaded ln_var ln_std pad_set ln_rows").split()]
        turn_stored = [turn_even, turn_odd]
        hT_loaded, grp_loaded, xr_loaded = [hT_even, hT_odd], [grp_even, grp_odd], [xr_even, xr_odd]

        block = ctx.enter_context(nc.Block())

        @block.gpsimd
        def _(pool):
            nc.gpsimd.iota(iot_i, pattern=[[1, HC]], base=0, channel_multiplier=0).then_inc(consts_i, 1)
            nc.gpsimd.iota(pidx_i[:, :], pattern=[[0, 1]], base=0, channel_multiplier=1).then_inc(consts_i, 1)
            nc.gpsimd.memset(zeros, 0.0).then_inc(zeros_set, 1)

            def gather(b, base):
                for h in range(2):
                    for k in range(KW):
                        nc.gpsimd.indirect_dma_start(
                            win[h][0:NWH[h], k * ROWE:(k + 1) * ROWE], None, table,
                            bass.IndirectOffsetOnAxis(ap=idx[0:NWH[h], h * KW + k:h * KW + k + 1], axis=0),
                        ).then_inc(b.gathered, 16)

            pool.wait_ge(idx_ready, 1)
            pool.wait_ge(table_stored, 16 * (2 * COPIES + 1))
            gather(fast, 0)

            pool.wait_ge(flag_ready, 1)
            general = pool.value_load(flag[0:1, 0:1], min_val=0, max_val=1)
            with pool.If(general):
                pool.wait_ge(es_zeroed, 16 * CH)
                with pool.Fori(0, ROUNDS) as r:
                    pool.wait_ge(idx_ready, r + 2)
                    settle(pool)
                    gather(slow, r)
                    with pool.Fori(0, CH) as c:
                        pool.wait_ge(slow.sums_kept, START1 + (r * CH + c + 1) * CSTEP)
                        pool.dma_start(edge_sum[:, ds(c * CW, CW)], es_out[0:12, :],
                                       accum_op=ALU.add).then_inc(slow.es_stored, 16)
                        pool.wait_ge(slow.es_stored, 16 * (r * CH + c + 1))
                        pool.sem_inc(es_free, 1)
            with pool.Else():
                pool.nop()

            def eye(c, b, at, p0, w):
                v = adj_chunk(c)[:, ds(b, 1), at:at + w].rearrange("p b n -> p (b n)")
                return nc.gpsimd.tensor_tensor(v, v, ident_h[:, p0:p0 + w], ALU.add)

            def eyes(c, j, t):
                if t == 0:
                    at = [(0, 0, P), (P, 0, P), (2 * P, 0, P), (3 * P, 0, CW - 3 * P)]
                    bs = [7 * j, 7 * j + 1, 7 * j + 2, 7 * j + 3]
                else:
                    at = [(0, 64, 64), (64, 0, P), (192, 0, P), (320, 0, P)]
                    bs = [7 * j + 3, 7 * j + 4, 7 * j + 5, 7 * j + 6]
                pool.wait_ge(op_loaded, 16 * (CH + c + 1))
                for b, (a, p0, w) in zip(bs, at):
                    last = eye(c, b, a, p0, w)
                last.then_inc(eye_added, 1)

            with pool.Fori(0, CH // 2) as j:
                for t in range(2):
                    eyes(2 * j + t, j, t)
            eyes(CH - 1, CH // 2, 0)

        @block.sync
        def _(sp):
            sp.wait_ge(zeros_set, 2)
            full = (P - 1) * EC
            sp.dma_start(src_i[0:P - 1, :], src[0:full].rearrange("(p e) -> p e", e=EC)).then_inc(edges_loaded, 16)
            sp.dma_start(dst_i[0:P - 1, :], dst[0:full].rearrange("(p e) -> p e", e=EC)).then_inc(edges_loaded, 16)
            sp.dma_start(src_i[P - 1:P, 0:ELAST], src[full:E].rearrange("(p e) -> p e", p=1)).then_inc(edges_loaded, 16)
            sp.dma_start(dst_i[P - 1:P, 0:ELAST], dst[full:E].rearrange("(p e) -> p e", p=1)).then_inc(edges_loaded, 16)
            sp.dma_start(att[0:P - 1, :, :], attr[0:full, :].rearrange("(p e) k -> p e k", e=EC)).then_inc(edges_loaded, 16)
            sp.dma_start(att[P - 1:P, 0:ELAST, :], attr[full:E, :].rearrange("(p e) k -> p e k", p=1)).then_inc(edges_loaded, 16)
            zh = zeros.bitcast(f16).rearrange("p (b n) -> p b n", b=NB)
            zf = zeros[:, 0:F]
            sp.dma_start(adj_dram[:, NPAD:NR].rearrange("(b p) n -> p b n", p=P), zh[:, :, 0:NR - NPAD]).then_inc(zero_stored, 16)
            sp.dma_start(rawT[:, :, NPAD:NR].rearrange("h p n -> p h n"),
                         zf[:, 0:128].rearrange("p (h n) -> p h n", h=2)).then_inc(zero_stored, 16)
            sp.dma_start(adjT_dram[NPAD:NR, :].rearrange("r (x c) -> (r x) c", x=2),
                         zeros.bitcast(f16)).then_inc(zero_stored, 16)
            for t in xs[1:]:
                sp.dma_start(t[NPAD:NR, :], zf[0:NR - NPAD, :]).then_inc(zero_stored, 16)
            sp.dma_start(fcol[:, 0, :, :], mlp_b.rearrange("l (h p) -> p (l h)", p=P), allow_slow_non_contiguous=True).then_inc(fcol_loaded, 16)
            sp.dma_start(fcol[:, 1, :, :], bn_g.rearrange("l (h p) -> p (l h)", p=P), allow_slow_non_contiguous=True).then_inc(fcol_loaded, 16)
            sp.dma_start(fcol[:, 2, :, :], bn_b.rearrange("l (h p) -> p (l h)", p=P), allow_slow_non_contiguous=True).then_inc(fcol_loaded, 16)
            sp.wait_ge(fields_done, 1)
            sp.dma_start(slo_row, slo_h).then_inc(slo_stored, 16)
            sp.wait_ge(slo_stored, 16)
            q = P * EC // 4
            for i in range(4):
                sp.dma_start(slo_bc[:, i * q:(i + 1) * q], flat(slo_row, i * q, [[0, P], [1, q]])).then_inc(slo_loaded, 16)
            sp.wait_ge(deg_done, 1)
            for t, row in enumerate((dinv_row, dinv2_row)):
                sp.dma_start(row.rearrange("(b p) -> p b", p=P), degs[:, 5, t, :], allow_slow_non_contiguous=True).then_inc(rows_stored, 16)
            sp.wait_ge(table_done, 1)
            for j in range(COPIES):
                at = (j * CPR * P + P - WD * j) * FLD
                sp.dma_start(flat(table, at, [[EC * FLD, P], [1, EC * FLD]]),
                             tab.rearrange("p e k -> p (e k)")).then_inc(table_stored, 16)
                sp.dma_start(flat(table, at + P * EC * FLD, [[GAP * FLD, 1], [1, GAP * FLD]]),
                             sent[0:1, :, :].rearrange("p e k -> p (e k)")).then_inc(table_stored, 16)
            sp.dma_start(table[0:1, :], sent[0:1, 0:P, :].rearrange("p e k -> p (e k)")).then_inc(table_stored, 16)
            for c in range(CH):
                sp.wait_ge(fast.sums_kept, START1 + (c + 1) * CSTEP)
                sp.dma_start(edge_sum[:, c * CW:(c + 1) * CW], es_out[0:12, :]).then_inc(fast.es_stored, 16)
            sp.wait_ge(flag_ready, 1)
            general = sp.value_load(flag[0:1, 0:1], min_val=0, max_val=1)
            with sp.If(general):
                sp.wait_ge(fast.es_stored, START16 + 16 * CH)
                sp.wait_ge(zeros_set, 3)
                for c in range(CH):
                    sp.dma_start(edge_sum[:, c * CW:(c + 1) * CW], es_out[0:12, :]).then_inc(es_zeroed, 16)
            with sp.Else():
                sp.nop()

            sp.wait_ge(built, 1)
            sp.wait_ge(fast.es_stored, START16 + 16 * CH)
            for c in range(CH):
                sp.dma_start(adj_dram[:, c * CW:(c + 1) * CW].rearrange("(b p) n -> p b n", p=P),
                             adj_chunk(c)).then_inc(adj_stored, 16)
            sp.wait_ge(adj_stored, 16 * CH)
            sp.wait_ge(rows_stored, 32)
            sp.wait_ge(zero_stored, 16 * 6)

            for g in range(NG):
                if g >= 2:
                    sp.wait_ge(turned_grp, g - 1)
                    sp.wait_ge(parts_hi, g - 1)
                    sp.wait_ge(parts_lo, g - 1)
                v = rbuf[g % 2].rearrange("p (b f) -> p b f", f=F)
                if g < NG - 1:
                    sp.dma_start(v, x[g * GW:(g + 1) * GW, :].rearrange("(b p) f -> p b f", p=P)).then_inc(grp_loaded[g % 2], 16)
                else:
                    sp.wait_ge(pad_set, 1)
                    sp.dma_start(v[:, 0:GB - 1, :], x[g * GW:(NB - 1) * P, :].rearrange("(b p) f -> p b f", p=P)).then_inc(grp_loaded[0], 16)
                    sp.dma_start(v[0:TAIL, GB - 1, :], x[(NB - 1) * P:N, :]).then_inc(grp_loaded[0], 16)
                if g >= 1:
                    sp.wait_ge(xT_done, g)
                    sp.dma_start(hT[:, :, (g - 1) * GW:g * GW].rearrange("h p n -> p h n"),
                                 xgrp.rearrange("p (h n) -> p h n", h=2)).then_inc(hT_stored, 16)
            sp.wait_ge(xT_done, NG)
            sp.dma_start(hT[:, :, (NG - 1) * GW:NR].rearrange("h p n -> p h n"),
                         xgrp.rearrange("p (h n) -> p h n", h=2)).then_inc(hT_stored, 16)

            def load_weights(l):
                sp.wait_ge(lin_done, START1 + CH * l + 1)
                sp.dma_start(wl, mlp_w[ds(l, 1), :, :].rearrange("l (k p) n -> p (l k) n", p=P)).then_inc(w_loaded, 16)
                for i in range(3):
                    sp.dma_start(ewt[4 * i:4 * i + 3, P:F], ew2[ds(l, 1), :, :].rearrange("l k n -> (l k) n")).then_inc(w_loaded, 16)
                    sp.dma_start(ewt[4 * i + 3:4 * i + 4, 0:P], ew1[ds(l, 1), :, :].rearrange("l k n -> (l k) n")).then_inc(w_loaded, 16)

            LAST = LAYERS - 1

            def store_raw(g, c):
                sp.wait_ge(lin_evac, START2 + 2 * g + 2)
                sp.dma_start(rawT[:, :, ds(c * CW, CW)].rearrange("h p n -> p h n"), nraw).then_inc(raw_stored, 16)

            def load_reverse(c):
                sp.dma_start(adj_chunk(c), adjT_dram[:, ds(c * CW, CW)].rearrange("(b p) n -> p b n", p=P)).then_inc(op_loaded, 16)
                sp.wait_ge(op_loaded, 16 * c + 16)
                settle(sp)

            def chunk(l, c, t, j, first):
                g = CH * l + c
                sp.wait_ge(agg_evac, START2 + 2 * g + 2)
                sp.dma_start(bc, flat(dinv_row, c * CW, [[0, P], [1, CW]])).then_inc(bc_loaded, 16)
                sp.wait_ge(spmm_done, START2 + 2 * g)
                sp.dma_start(es[0:12, :], edge_sum[:, ds(c * CW, CW)]).then_inc(es_loaded, 16)
                sp.wait_ge(lin_done, START1 + g)
                sp.dma_start(rbuf[t][:, 0:2 * CW].rearrange("p (h n) -> p h n", h=2),
                             hT[:, :, ds(c * CW, CW)].rearrange("h p n -> p h n")).then_inc(hT_loaded[t], 16)
                if not first:
                    store_raw(g - 1, c - 1)
                    if l is LAST:
                        load_reverse(c - 1)

            def products(l):
                load_weights(l)
                sp.wait_ge(hT_stored, 16 * NG * (l + 1))
                settle(sp)
                sp.wait_ge(parts_lo, NG * (l + 1))
                sp.wait_ge(parts_hi, NG * (l + 1))
                chunk(l, 0, 0, 0, True)
                with sp.Fori(0, CH // 2) as j:
                    chunk(l, 2 * j + 1, 1, j, False)
                    chunk(l, 2 * j + 2, 0, j + 1, False)
                store_raw(CH * l + CH - 1, CH - 1)
                if l is LAST:
                    load_reverse(CH - 1)
                sp.wait_ge(raw_stored, START16 + 16 * CH * (l + 1))
                for t in range(2):
                    sp.wait_ge(turn_stored[t], START16 + 16 * CH * TURNS // 2)

            def load_raw_group(l, g):
                if g >= 2:
                    sp.wait_ge(turned_grp, NG * (l + 1) + g - 1)
                    if l is not LAST:
                        settle(sp)
                        sp.wait_ge(hT_stored, 16 * (NG * (l + 1) + g - 1))
                sp.dma_start(rbuf[g % 2].rearrange("p (h n) -> p h n", h=2),
                             rawT[:, :, g * GW:(g + 1) * GW].rearrange("h p n -> p h n")).then_inc(grp_loaded[g % 2], 16)

            with sp.Fori(0, LAYERS - 1) as l:
                products(l)
                for g in range(NG):
                    load_raw_group(l, g)
                    if g >= 1:
                        sp.wait_ge(norm_done, NG * l + g)
                        sp.dma_start(hT[:, :, (g - 1) * GW:g * GW].rearrange("h p n -> p h n"),
                                     rbuf[(g - 1) % 2].rearrange("p (h n) -> p h n", h=2)).then_inc(hT_stored, 16)
                sp.wait_ge(norm_done, NG * l + NG)
                sp.dma_start(hT[:, :, (NG - 1) * GW:NR].rearrange("h p n -> p h n"),
                             rbuf[(NG - 1) % 2].rearrange("p (h n) -> p h n", h=2)).then_inc(hT_stored, 16)
            products(LAST)

            sp.wait_ge(stats_done, START1 + CH * LAYERS)
            for g in range(NG):
                load_raw_group(LAST, g)
                v = xgrp.rearrange("p (b f) -> p b f", f=F)
                if g >= 1:
                    sp.wait_ge(y_ready, g)
                    sp.wait_ge(parts_hi, NG * LAYERS + g)
                    sp.dma_start(xs[0][(g - 1) * GW:g * GW, :].rearrange("(b p) f -> p b f", p=P), v).then_inc(x_stored, 16)
                    sp.wait_ge(x_stored, 16 * g)
                if g < NG - 1:
                    sp.dma_start(v, x[g * GW:(g + 1) * GW, :].rearrange("(b p) f -> p b f", p=P)).then_inc(x_loaded, 16)
                else:
                    sp.wait_ge(pad_set, 2)
                    sp.dma_start(v[:, 0:GB - 1, :], x[g * GW:(NB - 1) * P, :].rearrange("(b p) f -> p b f", p=P)).then_inc(x_loaded, 16)
                    sp.dma_start(v[0:TAIL, GB - 1, :], x[(NB - 1) * P:N, :]).then_inc(x_loaded, 16)
            sp.wait_ge(y_ready, NG)
            sp.dma_start(xs[0][(NG - 1) * GW:NR, :].rearrange("(b p) f -> p b f", p=P),
                         xgrp.rearrange("p (b f) -> p b f", f=F)).then_inc(x_stored, 16)
            sp.wait_ge(x_stored, 16 * NG)

            sp.wait_ge(dout_ready, 1)
            sp.dma_start(dout_row.rearrange("(b p) -> p b", p=P), dop[:, CH, :], allow_slow_non_contiguous=True).then_inc(dout_stored, 16)
            sp.wait_ge(dout_stored, 16)
            sp.dma_start(nrow[:, 2, :], dout_row[0:NPAD].rearrange("(s p) -> p s", p=SW), allow_slow_non_contiguous=True).then_inc(rows_loaded, 16)
            sp.dma_start(nrow[:, 3, :], dinv2_row[0:NPAD].rearrange("(s p) -> p s", p=SW), allow_slow_non_contiguous=True).then_inc(rows_loaded, 16)

            for ph, (w, b) in enumerate(((w_1, b_1), (w_21, b_21), (w_22, b_22), (w_3, b_3))):
                base = CH * (LAYERS + ph)
                sp.wait_ge(lin_done, START1 + base + 1)
                if ph:
                    sp.wait_ge(y_ready, NG + CH * ph)
                    sp.wait_ge(x_stored, 16 * (NG + CH * ph))
                sp.dma_start(wt if ph == 3 else wd, w.rearrange("(h p) n -> p h n", p=P)).then_inc(bias_loaded, 16)
                sp.dma_start(bias[0:SW, :], flat(b, 0, [[0, SW], [1, F]])).then_inc(bias_loaded, 16)
                if ph:
                    for g in range(NG):
                        if g >= 2:
                            sp.wait_ge(parts_hi, NG * (LAYERS + ph) + g - 1)
                            sp.wait_ge(parts_lo, NG * (LAYERS + ph) + g - 1)
                        sp.dma_start(rbuf[g % 2].rearrange("p (b f) -> p b f", f=F),
                                     xs[ph][g * GW:(g + 1) * GW, :].rearrange("(b p) f -> p b f", p=P)).then_inc(grp_loaded[g % 2], 16)
                    sp.wait_ge(parts_hi, NG * (LAYERS + ph + 1))
                    sp.wait_ge(parts_lo, NG * (LAYERS + ph + 1))
                sp.wait_ge(parts_hi, NG * (LAYERS + 1))

                def load_x(c, t, ph=ph):
                    sp.dma_start(rbuf[t][0:SW, 0:SUBS * F].rearrange("p (s f) -> p s f", f=F),
                                 xs[ph][ds(c * CW, CW), :].rearrange("(s p) f -> p s f", p=SW)).then_inc(xr_loaded[t], 16)

                def store_y(c, t, ph=ph, base=base):
                    sp.wait_ge(y_ready, NG + CH * ph + c + 1)
                    v = rbuf[t][0:SW, 0:SUBS * F].rearrange("p (s f) -> p s f", f=F)
                    if ph < 3:
                        sp.dma_start(xs[ph + 1][ds(c * CW, CW), :].rearrange("(s p) f -> p s f", p=SW), v).then_inc(x_stored, 16)
                    elif isinstance(c, int) and c == CH - 1:
                        at = c * CW + (SUBS - 1) * SW
                        sp.dma_start(out[c * CW:at, :].rearrange("(s p) f -> p s f", p=SW), v[:, 0:SUBS - 1, :]).then_inc(x_stored, 16)
                        sp.dma_start(out[at:N, :], v[0:N - at, SUBS - 1, :]).then_inc(x_stored, 16)
                    else:
                        sp.dma_start(out[ds(c * CW, CW), :].rearrange("(s p) f -> p s f", p=SW), v).then_inc(x_stored, 16)

                def dense(c, t, first, ph=ph, base=base):
                    if ph == 2:
                        sp.wait_ge(y_ready, NG + CH * ph + c)
                        sp.dma_start(xr2[0:SW, :, :], xs[1][ds(c * CW, CW), :].rearrange("(s p) f -> p s f", p=SW)).then_inc(xr2_loaded, 16)
                    if not first:
                        store_y(c - 1, 1 - t)
                        sp.wait_ge(x_stored, 16 * (NG + CH * ph) + 16 * c)
                    if not (isinstance(c, int) and c == CH - 1):
                        load_x(c + 1, 1 - t)
                    if ph in (0, 2):
                        sp.wait_ge(spmm_done, START2 + 2 * (base + c) + 2)
                        if ph == 0:
                            sp.dma_start(adj_chunk(c), adj_dram[:, ds(c * CW, CW)].rearrange("(b p) n -> p b n", p=P)).then_inc(op_loaded, 16)
                        else:
                            sp.dma_start(adj_chunk(c), adjT_dram[:, ds(c * CW, CW)].rearrange("(b p) n -> p b n", p=P)).then_inc(op_loaded, 16)
                        sp.wait_ge(op_loaded, 16 * (CH * (1 if ph == 0 else 2) + c + 1))
                        settle(sp)

                load_x(0, 0)
                dense(0, 0, True)
                with sp.Fori(0, CH // 2 - 1) as j:
                    dense(2 * j + 1, 1, False)
                    dense(2 * j + 2, 0, False)
                dense(CH - 2, 1, False)
                dense(CH - 1, 0, False)
                store_y(CH - 1, 0)
            sp.wait_ge(x_stored, 16 * (NG + 4 * CH + 1))

        @block.scalar
        def _(act):
            act.wait_ge(root_in, 1)
            nc.scalar.activation(degs[:, 2, :, :], degs[:, 1, :, :], ACT.Sqrt).then_inc(root_out, 1)

            with act.Fori(0, CH) as c:
                act.wait_ge(fast.es_stored, START16 + 16 * c)
                with act.Fori(0, CSTEP) as s:
                    w0 = (c * CSTEP + s) * GWIN
                    for u in range(GWIN):
                        act.wait_ge(fast.ring_used, GWIN + w0 + u + 1)
                        nc.scalar.activation(adj_chunk(c)[:, :, ds(s * (GWIN * WD) + u * WD, WD)],
                                             bank(u)[:, 0:HC].rearrange("p (b n) -> p b n", n=WD),
                                             ACT.Copy).then_inc(fast.win_kept, 1)
                    act.wait_ge(fast.sums_done, START1 + c * CSTEP + s + 1)
                    nc.scalar.activation(es_out[0:12, ds(s * (GWIN * WD), GWIN * WD)],
                                         bank(4)[0:12, 0:GWIN * WD], ACT.Copy).then_inc(fast.sums_kept, 1)

            def high(dst_part, src_rows, scale):
                return nc.scalar.activation(dst_part, src_rows, ACT.Identity, scale=scale)

            for g in range(NG):
                act.wait_ge(grp_loaded[g % 2], 16 * (g // 2 + 1) + 16 * (g == NG - 1))
                v = rbuf[g % 2].rearrange("p (b f) -> p b f", f=F)
                for b in range(GB):
                    last = high(parts[:, 0, g * GB + b, :], v[:, b, :], scl[:, 0, g * GB + b:g * GB + b + 1])
                last.then_inc(parts_hi, 1)
                act.wait_ge(turned_grp, g + 1)
                act.wait_ge(hT_stored, 16 * g)
                nc.scalar.activation(xgrp, ptr[g % 2][:, 0:GB * F], ACT.Copy).then_inc(xT_done, 1)

            def lin_out(l, c):
                g = CH * l + c
                act.wait_ge(lin_done, START1 + g + 2)
                act.wait_ge(raw_stored, START16 + 16 * g)
                act.wait_ge(stats_done, START1 + g)
                for h in range(2):
                    nc.scalar.activation(nraw[:, h, :], lin_h[h], ACT.Relu,
                                         bias=fcol[:, 0, ds(l, 1), h]).then_inc(lin_evac, 1)

            def turn_out(c):
                for m in range(TURNS):
                    t, (q, g) = m % 2, divmod(m, NG)
                    act.wait_ge(adj_turned, c * TURNS + m + 1)
                    act.wait_ge(turn_stored[t], START16 + 16 * (c * (TURNS // 2) + m // 2))
                    nc.scalar.activation(turn[t][0:SW, :], turn_ps[t], ACT.Copy).then_inc(adj_turned_out, 1)
                    act.wait_ge(adj_turned_out, 2 + c * TURNS + m + 1)
                    act.dma_start(adjT_dram[ds(c * CW + q * SW, SW), g * GW:(g + 1) * GW],
                                  turn[t][0:SW, :]).then_inc(turn_stored[t], 16)

            def chunks_out(l, turning=False):
                if turning:
                    turn_out(0)
                    with act.Fori(0, CH - 1) as c:
                        turn_out(c + 1)
                        lin_out(l, c)
                    lin_out(l, CH - 1)
                else:
                    with act.Fori(0, CH) as c:
                        lin_out(l, c)

            def normalize(l, g, func):
                k = g // 2 + 1
                act.wait_ge(grp_loaded[g % 2], 64 + 48 * l + 16 * k if g % 2 == 0 else 32 + 32 * l + 16 * k)
                v = rbuf[g % 2].rearrange("p (h n) -> p h n", h=2)
                for h in range(2):
                    last = nc.scalar.activation(v[:, h, :], v[:, h, :], func, bias=bnsc[:, 3, h:h + 1],
                                                scale=bnsc[:, 2, h:h + 1])
                last.then_inc(norm_done, 1)

            def turned_high(l, g):
                act.wait_ge(turned_grp, NG * (l + 1) + g + 1)
                for b in range(GB):
                    n = g * GB + b
                    last = high(parts[:, 0, n, :], ptr[g % 2][:, b * F:(b + 1) * F], scl[:, 0, n:n + 1])
                last.then_inc(parts_hi, 1)

            act.wait_ge(fcol_loaded, 48)
            def layer_out(l, turning=False):
                chunks_out(l, turning)
                act.wait_ge(var_ready, l + 1)
                nc.scalar.activation(bnsc[:, 1, :], bnsc[:, 0, :], ACT.Sqrt).then_inc(std_ready, 1)
                act.wait_ge(bn_ready, l + 1)
                for g in range(NG):
                    normalize(l, g, ACT.Relu)
                    if g >= 1:
                        turned_high(l, g - 1)
                turned_high(l, NG - 1)

            layer_out(0, turning=True)
            with act.Fori(1, LAYERS - 1) as l:
                layer_out(l)
            last_l = LAYERS - 1
            chunks_out(last_l)
            act.wait_ge(var_ready, LAYERS)
            nc.scalar.activation(bnsc[:, 1, :], bnsc[:, 0, :], ACT.Sqrt).then_inc(std_ready, 1)
            act.wait_ge(bn_ready, LAYERS)

            def ln_root(n, rows, nb):
                act.wait_ge(ln_var, n)
                nc.scalar.activation(ln_r[0:rows, 1, 0:nb], ln_r[0:rows, 0, 0:nb], ACT.Sqrt).then_inc(ln_std, 1)

            normalize(last_l, 0, ACT.Identity)
            for g in range(NG):
                if g + 1 < NG:
                    normalize(last_l, g + 1, ACT.Identity)
                ln_root(g + 1, P, GB)
                act.wait_ge(ln_rows, g + 1)
                for b in range(GB):
                    last = high(parts[:, 0, g * GB + b, :], xgrp[:, b * F:(b + 1) * F], S_LN)
                last.then_inc(parts_hi, 1)

            ln_n = NG
            for ph in range(4):
                if ph:
                    for g in range(NG):
                        base_g = [64 + 48 * LAYERS + 48 * (ph - 1), 32 + 32 * LAYERS + 32 * (ph - 1)][g % 2]
                        act.wait_ge(grp_loaded[g % 2], base_g + 16 * (g // 2 + 1))
                        for b in range(GB):
                            n = g * GB + b
                            last = high(parts[:, 0, n, :], rbuf[g % 2][:, b * F:(b + 1) * F],
                                        scl[:, 1, n:n + 1] if ph < 3 else S_LN)
                        last.then_inc(parts_hi, 1)
                scale = 1.0 if ph in (1, 2) else 1.0 / S_LN

                def agg_out(c, ph=ph, scale=scale):
                    g = CH * (LAYERS + ph) + c
                    act.wait_ge(lin_done, START1 + g + 1)
                    for h in range(2):
                        act.wait_ge(spmm_done, START2 + 2 * g + h + 1)
                        nc.scalar.activation(agg[:, h, :], acc_of(c)[h], ACT.Copy, scale=scale).then_inc(agg_evac, 1)

                def acc_of(c):
                    return acc[acc_t[0]]

                acc_t = [0]
                if ph == 0:
                    act.wait_ge(x_stored, 16 * NG)
                agg_out(0)
                with act.Fori(0, CH // 2) as j:
                    for t in range(2):
                        acc_t[0] = 1 - t
                        agg_out(2 * j + t + 1)
                        if ph != 1:
                            ln_root(ln_n + 2 * j + t + 1, SW, SUBS)
                if ph != 1:
                    ln_root(ln_n + CH, SW, SUBS)
                    ln_n += CH

        @block.vector
        def _(dve):
            V = nc.vector
            link = Steps(dve, dve_step)
            for b in (fast, slow):
                dve.sem_inc(b.ring_used, GWIN)
                dve.sem_inc(b.win_kept, GWIN)
                dve.sem_inc(b.sums_kept, START1)
                dve.sem_inc(b.sums_done, START1)
                dve.sem_inc(b.turned, START1)
            dve.sem_inc(fast.es_stored, START16)
            dve.sem_inc(es_free, START1)
            dve.sem_inc(hist_used, 2)
            dve.sem_inc(adj_turned_out, 2)
            dve.sem_inc(turn_even, START16)
            dve.sem_inc(turn_odd, START16)
            dve.sem_inc(sel_used, 2)
            dve.sem_inc(agg_evac, START2 + 2)
            dve.sem_inc(lin_done, START1 + 1)
            dve.sem_inc(spmm_done, START2)
            dve.sem_inc(lin_evac, START2)
            dve.sem_inc(raw_stored, START16)
            dve.sem_inc(stats_done, START1)
            V.memset(src_i, 0)
            V.memset(dst_i, 4095)
            V.memset(att.rearrange("p e k -> p (e k)"), 0.0).then_inc(zeros_set, 1)
            V.memset(ewt[:, :], 0.0)
            V.memset(sent.rearrange("p e k -> p (e k)"), 0.0)
            V.memset(ones_f, 1.0)
            V.memset(ones_h, 1.0)
            link(V.memset(zero_h, 0.0))
            V.memset(sent[:, :, 0], 4095.0)
            dve.wait_ge(consts_i, 2)
            V.tensor_copy(iot, iot_i)
            link(V.tensor_copy(pidx[:, :], pidx_i[:, :]))
            V.tensor_scalar(ident[:, :], iot[:, 0:P], pidx[:, 0:1], None, ALU.is_equal)
            V.tensor_scalar(ident_h[:, :], iot[:, 0:P], pidx[:, 0:1], None, ALU.is_equal).then_inc(consts, 1)

            dve.wait_ge(edges_loaded, 16 * 6)
            V.tensor_scalar(slo_i, src_i, P - 1, None, ALU.bitwise_and)
            V.tensor_scalar(shi_i, src_i, 7, None, ALU.logical_shift_right)
            V.tensor_scalar(dlo_i, dst_i, P - 1, None, ALU.bitwise_and)
            link(V.tensor_scalar(dhi_i, dst_i, 7, None, ALU.logical_shift_right))
            V.tensor_copy(slo_h, slo_i).then_inc(fields_done, 1)
            V.tensor_copy(shi_h, shi_i)
            V.tensor_copy(dlo_f, dlo_i)
            link(V.tensor_copy(dhi_h, dhi_i))

            def hi_onehot(hi):
                return V.tensor_tensor(oh_hi, hi.unsqueeze(2).broadcast_to((P, EC, NB)),
                                       iot[:, 0:NB].unsqueeze(1).broadcast_to((P, EC, NB)), ALU.is_equal)

            link(hi_onehot(dhi_h))
            with dve.Fori(0, EC // (2 * EB)) as i:
                for t in range(2):
                    dve.wait_ge(hist_used, 2 * i + t + 1)
                    for k in range(EB):
                        last = V.tensor_scalar(hring[:, t * EB + k, :], iot[:, 0:P],
                                               dlo_f[:, ds(i * (2 * EB) + t * EB + k, 1)], None, ALU.is_equal)
                    last.then_inc(hist_ready, 1)

            V.scalar_tensor_tensor(tab[:, :, 0], src_i, 4096.0, dst_i, ALU.mult, ALU.add)
            link(V.tensor_scalar(dwl_i, dst_i.rearrange("p (g x) -> p g x", x=WD)[:, :, WD - 1], 4, None,
                                 ALU.logical_shift_right))
            link(V.tensor_copy(dwl_h, dwl_i))
            link(V.tensor_tensor(cmp_h, iot[:, 0:NW].unsqueeze(2).broadcast_to((P, NW, 26)),
                                 dwl_h.unsqueeze(1).broadcast_to((P, NW, 26)), ALU.is_gt))
            V.tensor_reduce(part, cmp_h, AX.X, ALU.add).then_inc(part_ready, 1)
            link(V.memset(starts[:, :, :], 0))
            dve.wait_ge(starts_ready, 1)
            V.tensor_copy(starts[:, 0, 0:1], bank(5)[:, 32:33])
            link(V.tensor_copy(starts[0:NWH[1], 1, 0:1], bank(5)[0:NWH[1], 33:34]))
            V.tensor_scalar(starts[:, :, 1], starts[:, :, 0], COPIES - 1, None, ALU.bitwise_and)
            link(V.tensor_scalar(starts[:, :, 2], starts[:, :, 0], 3, None, ALU.logical_shift_right))
            link(V.scalar_tensor_tensor(starts[:, :, 3], starts[:, :, 1], float(CPR), starts[:, :, 2], ALU.mult, ALU.add))
            for k in range(KW):
                last = V.tensor_scalar(idx[:, :].rearrange("p (h k) -> p h k", k=KW)[:, :, k], starts[:, :, 3],
                                       float(1 + k), None, ALU.add)
            last.then_inc(idx_ready, 1)

            dve.wait_ge(slo_loaded, 64)
            q = P * EC // 4
            for i in range(4):
                last = V.tensor_scalar(slo_bc[:, i * q:(i + 1) * q], slo_bc[:, i * q:(i + 1) * q], pidx[:, 0:1],
                                       None, ALU.is_equal)
            last.then_inc(onehot_t, 1)

            dve.wait_ge(hist_used, 2 + EC // EB + 1)
            deg = bank(6)[:, 0:NB]
            V.tensor_scalar(degs[:, 0, 0, :], deg, 1.0, None, ALU.max)
            V.tensor_scalar(degs[:, 0, 1, :], deg, 1.0, None, ALU.add)
            V.tensor_scalar(degs[:, 4, 0, :], deg, 1.0, None, ALU.min)
            link(V.memset(degs[:, 4, 1, :], 1.0))
            V.reciprocal(degs[:, 1, :, :], degs[:, 0, :, :]).then_inc(root_in, 1)
            link(hi_onehot(shi_h))
            dve.wait_ge(root_out, 1)
            link(V.tensor_tensor(degs[:, 3, :, :], degs[:, 2, :, :], degs[:, 2, :, :], ALU.mult))
            link(V.tensor_tensor(degs[:, 3, :, :], degs[:, 3, :, :], degs[:, 0, :, :], ALU.mult))
            link(V.tensor_scalar(degs[:, 3, :, :], degs[:, 3, :, :], -0.5, 1.5, ALU.mult, ALU.add))
            link(V.tensor_tensor(degs[:, 3, :, :], degs[:, 3, :, :], degs[:, 2, :, :], ALU.mult))
            link(V.tensor_tensor(degs[:, 1, :, :], degs[:, 3, :, :], degs[:, 4, :, :], ALU.mult))
            V.tensor_scalar(degs[:, 5, :, :], degs[:, 1, :, :], 1.0 / S_BN, None, ALU.mult).then_inc(deg_done, 1)
            V.tensor_scalar(scl[:, :, :], degs[:, 1, :, :], S_BN, None, ALU.mult)
            link(V.tensor_scalar(degs[:, 2, 0, :], degs[:, 1, 0, :], S_TAB, None, ALU.mult))
            link(V.tensor_copy(dtab[:, 0, :], degs[:, 2, 0, :]))
            V.tensor_tensor(dtab[:, 1, :], degs[:, 2, 0, :], dtab[:, 0, :], ALU.subtract).then_inc(tab_ready, 1)

            n0 = link.n
            with dve.Fori(0, EC // (2 * EB)) as i:
                link.n = n0 + 4 * i
                for t in range(2):
                    e0 = i * (2 * EB) + t * EB
                    v = sel[t].rearrange("p (e a b) -> p e a b", a=2, b=NB)
                    dve.wait_ge(sel_ready, 2 * i + t + 1)
                    for a in range(2):
                        last = V.tensor_tensor(v[:, :, a, :], bank(6 + t)[:, 0:400].rearrange("p (e a b) -> p e a b", a=2, b=NB)[:, :, a, :],
                                               oh_hi[:, ds(e0, EB), :], ALU.mult)
                    link(last)
                    link(V.tensor_reduce(dinvs[:, ds(e0, EB)], sel[t].rearrange("p (e c) -> p e c", c=2 * NB), AX.X, ALU.add))
                    dve.sem_inc(sel_used, 1)
            link.n = n0 + 4 * (EC // (2 * EB))
            link(V.tensor_scalar(dinvs, dinvs, S_BN / S_TAB, None, ALU.mult))
            V.tensor_tensor(tab[:, :, 1:FLD], att, dinvs.unsqueeze(2).broadcast_to((P, EC, 4)), ALU.mult).then_inc(table_done, 1)

            def split(b, r, f):
                val = bank(2 * (f % 2), 2).rearrange("p (k w) -> p k w", w=2 * P)[:, 0:KW, 0:NW]
                v = [v3[:, :, 4 * a + f - 1].rearrange("p (k w) -> p k w", w=NW) for a in range(3)]
                q1, q2 = (x.rearrange("p (k w) -> p k w", w=NW) for x in (rest1, rest2))
                dve.wait_ge(b.turned, START1 + FLD * r + f + 1)
                link(V.tensor_copy(v[0], val))
                link(V.tensor_tensor(q1, val, v[0], ALU.subtract))
                dve.sem_inc(b.turned_used, 1)
                link(V.tensor_copy(v[1], q1))
                link(V.tensor_tensor(q2, q1, v[1], ALU.subtract))
                link(V.tensor_copy(v[2], q2))

            def fields(b, r):
                dve.wait_ge(b.turned, START1 + FLD * r + 1)
                k3 = [x.rearrange("p (k w) -> p k w", w=NW) for x in (key_i, fa_i, mask)]
                link(V.tensor_copy(k3[0], bank(0, 2).rearrange("p (k w) -> p k w", w=2 * P)[:, 0:KW, 0:NW]))
                dve.sem_inc(b.turned_used, 1)
                link(V.tensor_scalar(fa_i, key_i, 4, 255, ALU.logical_shift_right, ALU.bitwise_and))
                V.tensor_tensor(k3[2], k3[1], iot_i[:, 0:NW].unsqueeze(1).broadcast_to((P, KW, NW)), ALU.is_equal)
                link(V.tensor_scalar(fb_i, key_i, 19, None, ALU.logical_shift_right))
                link(V.tensor_scalar(fa_i, key_i, WD - 1, None, ALU.bitwise_and))
                V.scalar_tensor_tensor(key2, fb_i, float(WD), fa_i, ALU.mult, ALU.add)
                link(V.scalar_tensor_tensor(dlom, fa_i, 1.0, mask, ALU.add, ALU.mult))
                link(V.tensor_scalar(fb_i, key_i, 12, P - 1, ALU.logical_shift_right, ALU.bitwise_and))
                link(V.scalar_tensor_tensor(slom, fb_i, 1.0, mask, ALU.add, ALU.mult))

            def one_hots(b, r, w0, step):
                dve.wait_ge(b.sums_done, START1 + r * STEPS + step)
                d4 = dlom.rearrange("p (k w) -> p k w", w=NW)[:, :, ds(w0, GWIN)]
                V.tensor_tensor(ringd, d4.unsqueeze(3).broadcast_to((P, KW, GWIN, WD)),
                                iot[:, 1:WD + 1].unsqueeze(1).unsqueeze(1).broadcast_to((P, KW, GWIN, WD)), ALU.is_equal)
                for u in range(GWIN):
                    dve.wait_ge(b.ring_used, r * NW + w0 + u + 1)
                    for k in range(KW):
                        at = ds(w0 + (k * NW + u), 1)
                        V.tensor_scalar(ring1[:, KW * u + k, :], iot[:, 1:P + 1], slom[:, at], None, ALU.is_equal)
                        last = V.tensor_scalar(ring2[:, KW * u + k, :], iot[:, 0:HC], key2[:, at], None, ALU.is_equal)
                    last.then_inc(b.ring_ready, 1)

            dve.wait_ge(zero_stored, 16 * 6)
            dve.wait_ge(table_stored, 16 * (2 * COPIES + 1))
            n0 = link.n
            fields(fast, 0)
            V.tensor_reduce(flag_f[:, 0:1], mask, AX.X, ALU.add).then_inc(captured, 1)
            for f in range(1, FLD):
                split(fast, 0, f)
            round_steps = link.n - n0
            with dve.Fori(0, STEPS) as s:
                one_hots(fast, 0, s * GWIN, s)
            dve.wait_ge(cap_summed, 1)
            link(V.tensor_scalar(flag_f[:, 1:2], bank(7)[:, 0:1], float(E), None, ALU.is_equal))
            link(V.tensor_scalar(flag[:, :], flag_f[:, 1:2], -1.0, 1.0, ALU.mult, ALU.add))
            dve.sem_inc(flag_ready, 1)
            dve.wait_ge(fast.win_kept, GWIN + NW)
            general = dve.value_load(flag[0:1, 0:1], min_val=0, max_val=1)
            n0 = link.n
            with dve.If(general):
                dve.wait_ge(fast.es_stored, START16 + 16 * CH)
                link(V.memset(es_out, 0.0))
                dve.sem_inc(zeros_set, 1)
                for c in range(CH):
                    V.memset(adj[:, c * CF:(c + 1) * CF], 0.0)
                for h in range(2):
                    for k in range(KW):
                        V.memset(idx[:, KW * h + k:KW * h + k + 1], 1 + k - KW)
                n1 = link.n
                with dve.Fori(0, ROUNDS) as r:
                    link.n = n1 + r * (round_steps + 1)
                    dve.wait_ge(slow.turned, START1 + FLD * r)
                    link(V.tensor_scalar(idx[:, :], idx[:, :], float(KW), None, ALU.add))
                    dve.sem_inc(idx_ready, 1)
                    fields(slow, r)
                    for f in range(1, FLD):
                        split(slow, r, f)
                    settle(dve)
                    with dve.Fori(0, CH) as c:
                        with dve.Fori(0, CSTEP) as s:
                            step = c * CSTEP + s
                            one_hots(slow, r, step * GWIN, step)
                            for u in range(GWIN):
                                dve.wait_ge(slow.ring_used, r * NW + step * GWIN + (GWIN + u + 1))
                                v = adj_chunk(c)[:, :, ds(s * (GWIN * WD) + u * WD, WD)]
                                V.tensor_tensor(v, v, bank(u)[:, 0:HC].rearrange("p (b n) -> p b n", n=WD),
                                                ALU.add).then_inc(slow.win_kept, 1)
                            dve.wait_ge(slow.sums_done, START1 + r * STEPS + step + 1)
                            dve.wait_ge(es_free, START1 + r * CH + c)
                            V.tensor_copy(es_out[0:12, ds(s * (GWIN * WD), GWIN * WD)],
                                          bank(4)[0:12, 0:GWIN * WD]).then_inc(slow.sums_kept, 1)
                dve.wait_ge(slow.es_stored, 16 * CH * ROUNDS)
                dve.wait_ge(slow.win_kept, GWIN + NW * ROUNDS)
            with dve.Else():
                dve.nop()
            dve.sem_inc(built, 1)
            pad_link = Steps(dve, pad_step)

            def low(part_lo, rows, scale, part_hi):
                return V.scalar_tensor_tensor(part_lo, rows, scale, part_hi, ALU.mult, ALU.subtract)

            for g in range(NG):
                if g == NG - 1:
                    dve.wait_ge(turned_grp, g - 1)
                    dve.wait_ge(parts_hi, g - 1)
                    dve.wait_ge(parts_lo, g - 1)
                    pad_link(V.memset(rbuf[0][:, (GB - 1) * F:GB * F], 0.0))
                    dve.sem_inc(pad_set, 1)
                dve.wait_ge(parts_hi, g + 1)
                for b in range(GB):
                    n = g * GB + b
                    last = low(parts[:, 1, n, :], rbuf[g % 2][:, b * F:(b + 1) * F], scl[:, 0, n:n + 1], parts[:, 0, n, :])
                last.then_inc(parts_lo, 1)

            def agg_out(l, c, t):
                g = CH * l + c
                dve.wait_ge(bc_loaded, 16 * (g + 1))
                dve.wait_ge(lin_done, START1 + g + 1)
                for h in range(2):
                    dve.wait_ge(spmm_done, START2 + 2 * g + h + 1)
                    V.tensor_tensor(agg[:, h, :], acc[t][h], bc, ALU.mult).then_inc(agg_evac, 1)

            def chunk_stats(l, c, width):
                dve.wait_ge(lin_evac, START2 + 2 * (CH * l + c) + 2)
                for h in range(2):
                    last = V.bn_stats(stats[:, h, ds(c, 1), :].rearrange("p c s -> p (c s)"), nraw[:, h, 0:width])
                last.then_inc(stats_done, 1)

            def norm_factors(l, steps):
                for h in range(2):
                    last = V.bn_aggr(mv[:, h, :], stats[:, h, :, :].rearrange("p c s -> p (c s)"))
                steps(last)
                steps(V.tensor_scalar(bnsc[:, 0, :], mv[:, :, 1], EPS, None, ALU.add))
                steps(V.reciprocal(bnsc[:, 0, :], bnsc[:, 0, :]))
                dve.sem_inc(var_ready, 1)
                dve.wait_ge(std_ready, l + 1)
                g_l, b_l = (fcol[:, i, ds(l, 1), :].rearrange("p l h -> p (l h)") for i in (1, 2))
                steps(V.tensor_tensor(bnsc[:, 2, :], bnsc[:, 1, :], g_l, ALU.mult))
                steps(V.tensor_tensor(bnsc[:, 3, :], mv[:, :, 0], bnsc[:, 2, :], ALU.mult))
                steps(V.tensor_tensor(bnsc[:, 3, :], b_l, bnsc[:, 3, :], ALU.subtract))
                dve.sem_inc(bn_ready, 1)

            def row_sums(c):
                V.tensor_reduce(dop[:, ds(c, 1), :].rearrange("p c b -> p (c b)"), adj_chunk(c), AX.X, ALU.add).then_inc(dout_part, 1)

            def layer(l, degrees=False):
                agg_out(l, 0, 0)
                with dve.Fori(0, CH // 2) as j:
                    for t in range(2):
                        if degrees:
                            row_sums(2 * j + t)
                        agg_out(l, 2 * j + t + 1, 1 - t)
                        chunk_stats(l, 2 * j + t, CW)
                if degrees:
                    row_sums(CH - 1)
                chunk_stats(l, CH - 1, LASTW)
                dve.wait_ge(stats_done, START1 + CH * l + CH)
                settle(dve)
                norm_factors(l, link)

            dve.wait_ge(fcol_loaded, 48)
            link = Steps(dve, vec_step)

            def groups_low(l):
                for g in range(NG):
                    dve.wait_ge(parts_hi, NG * (l + 1) + g + 1)
                    for b in range(GB):
                        n = g * GB + b
                        last = low(parts[:, 1, n, :], ptr[g % 2][:, b * F:(b + 1) * F], scl[:, 0, n:n + 1], parts[:, 0, n, :])
                    last.then_inc(parts_lo, 1)

            layer(0, degrees=True)
            groups_low(0)
            dve.wait_ge(dout_part, CH)
            V.tensor_reduce(dop[:, CH, :], dop[:, 0:CH, :].rearrange("p c b -> p b c"), AX.X, ALU.add).then_inc(dout_ready, 1)
            per_layer = link.n
            with dve.Fori(1, LAYERS - 1) as l:
                link.n = per_layer * l
                layer(l)
                groups_low(l)
            link.n = per_layer * (LAYERS - 1)
            layer(LAYERS - 1)

            def layer_norm(v, rows, nb, n):
                for b in range(nb):
                    last = V.bn_stats(ln_st[0:rows, b, :], v[:, b, :])
                link(last)
                settle(dve)
                for b in range(nb):
                    last = V.bn_aggr(ln_mv[0:rows, b, :], ln_st[0:rows, b, :])
                link(last)
                link(V.tensor_scalar(ln_r[0:rows, 0, 0:nb], ln_mv[0:rows, 0:nb, 1], EPS, None, ALU.add))
                link(V.reciprocal(ln_r[0:rows, 0, 0:nb], ln_r[0:rows, 0, 0:nb]))
                dve.sem_inc(ln_var, 1)
                dve.wait_ge(ln_std, n)
                for b in range(nb):
                    last = V.tensor_scalar(v[:, b, :], v[:, b, :], ln_mv[0:rows, b, 0:1], ln_r[0:rows, 1, b:b + 1],
                                           ALU.subtract, ALU.mult)
                link(last)

            xg = xgrp.rearrange("p (b f) -> p b f", f=F)
            for g in range(NG):
                if g == NG - 1:
                    dve.wait_ge(x_stored, 16 * g)
                    link(V.memset(xg[:, GB - 1, :], 0.0))
                    dve.sem_inc(pad_set, 1)
                dve.wait_ge(turned_grp, NG * LAYERS + g + 1)
                dve.wait_ge(x_loaded, 16 * (g + 1) + 16 * (g == NG - 1))
                link(V.tensor_tensor(xgrp, ptr[g % 2][:, 0:GB * F], xgrp, ALU.add))
                layer_norm(xg, P, GB, g + 1)
                dve.sem_inc(ln_rows, 1)
                dve.wait_ge(parts_hi, NG * LAYERS + g + 1)
                for b in range(GB):
                    n = g * GB + b
                    last = low(parts[:, 1, n, :], xg[:, b, :], S_LN, parts[:, 0, n, :])
                link(last)
                dve.sem_inc(parts_lo, 1)
                dve.sem_inc(y_ready, 1)

            dve.wait_ge(rows_loaded, 32)
            link(V.tensor_scalar(nrow[:, 1, :], nrow[:, 2, :], 1.0, None, ALU.min))
            link(V.tensor_scalar(nrow[:, 0, :], nrow[:, 2, :], 1.0, None, ALU.max))
            link(V.reciprocal(nrow[:, 0, :], nrow[:, 0, :]))
            link(V.tensor_tensor(nrow[:, 0, :], nrow[:, 0, :], nrow[:, 1, :], ALU.mult))

            ln_n = NG
            for ph in range(4):
                if ph:
                    for g in range(NG):
                        dve.wait_ge(parts_hi, NG * (LAYERS + ph) + g + 1)
                        for b in range(GB):
                            n = g * GB + b
                            last = low(parts[:, 1, n, :], rbuf[g % 2][:, b * F:(b + 1) * F],
                                       scl[:, 1, n:n + 1] if ph < 3 else S_LN, parts[:, 0, n, :])
                        last.then_inc(parts_lo, 1)
                dve.wait_ge(bias_loaded, 32 * (ph + 1))
                if ph == 3:
                    dve.wait_ge(wt_done, 1)
                    link(V.tensor_copy(wd.rearrange("p h n -> p (h n)"), bank(6)))
                    dve.sem_inc(wt_kept, 1)
                row_bias = bias[0:SW, :]

                def rows_out(c, t, j, ph=ph):
                    g = CH * (LAYERS + ph) + c
                    k = [4, 3][t] * ph + j + 1
                    v = rbuf[t][0:SW, 0:SUBS * F].rearrange("p (s f) -> p s f", f=F)
                    dve.wait_ge(xr_loaded[t], 16 * k)
                    col = lambda i, s: nrow[:, i, ds(c * SUBS + s, 1)]
                    if ph in (0, 3):
                        for s in range(SUBS):
                            last = V.scalar_tensor_tensor(v[:, s, :], row_bias, col(1 if ph == 0 else 2, s), v[:, s, :], ALU.mult, ALU.add)
                        link(last)
                    dve.wait_ge(lin_done, START1 + g + 2)
                    for s in range(SUBS):
                        if ph == 0:
                            last = V.scalar_tensor_tensor(v[:, s, :], lin_s[0:SW, s, :], col(0, s), v[:, s, :], ALU.mult, ALU.add)
                        elif ph == 3:
                            last = V.tensor_tensor(v[:, s, :], lin_s[0:SW, s, :], v[:, s, :], ALU.add)
                        else:
                            last = V.scalar_tensor_tensor(tmp[0:SW, s, :], lin_s[0:SW, s, :], col(3, s), row_bias, ALU.mult, ALU.add)
                    link(last)
                    dve.sem_inc(lin_evac, 2)
                    if ph in (1, 2):
                        link(V.scalar_tensor_tensor(v, tmp[0:SW, :, :], 0.0, v, ALU.max, ALU.add))
                    if ph == 2:
                        dve.wait_ge(xr2_loaded, 16 * (c + 1))
                        link(V.tensor_tensor(v, v, xr2[0:SW, :, :], ALU.add))
                    if ph != 1:
                        layer_norm(v, SW, SUBS, ln_n + c + 1)
                    dve.sem_inc(y_ready, 1)

                per = [2 + 5, 2, 3 + 5, 2 + 5][ph]
                n0 = link.n
                with dve.Fori(0, CH // 2) as j:
                    for t in range(2):
                        link.n = n0 + per * (2 * j + t)
                        rows_out(2 * j + t, t, j)
                link.n = n0 + per * (CH - 1)
                rows_out(CH - 1, 0, CH // 2)
                assert link.n == n0 + per * CH
                if ph != 1:
                    ln_n += CH

        @block.tensor
        def _(pe):
            T = nc.tensor
            pe.wait_ge(consts, 1)
            deg = bank(6)[:, 0:NB]
            T.matmul(deg, zero_h, zero_h[:, 0:NB], start=True, stop=False)
            with pe.Fori(0, EC // (2 * EB)) as i:
                for t in range(2):
                    pe.wait_ge(hist_ready, 2 * i + t + 1)
                    for k in range(EB):
                        last = T.matmul(deg, hring[:, t * EB + k, :],
                                        oh_hi[:, ds(i * (2 * EB) + t * EB + k, 1), :].rearrange("p e b -> p (e b)"),
                                        start=False, stop=False)
                    last.then_inc(hist_used, 1)
            T.matmul(deg, zero_h, zero_h[:, 0:NB], start=False, stop=True).then_inc(hist_used, 1)
            pe.wait_ge(part_ready, 1)
            T.matmul(bank(5)[:, 32:33], part[:, 0:P], ones_f[:, 0:1], start=True, stop=True)
            T.matmul(bank(5)[0:NWH[1], 33:34], part[:, P:NW], ones_f[:, 0:1], start=True, stop=True).then_inc(starts_ready, 1)
            pe.wait_ge(onehot_t, 1)
            pe.wait_ge(tab_ready, 1)
            cols = slo_bc.rearrange("q (p e) -> q p e", e=EC)
            with pe.Fori(0, EC // (2 * EB)) as i:
                for t in range(2):
                    pe.wait_ge(sel_used, 2 * i + t + 1)
                    for k in range(EB):
                        last = T.matmul(bank(6 + t)[:, 50 * k:50 * k + 50],
                                        cols[:, :, ds(i * (2 * EB) + t * EB + k, 1)].rearrange("q p e -> q (p e)"),
                                        dtab[:, :, :].rearrange("p a b -> p (a b)"), start=True, stop=True)
                    last.then_inc(sel_ready, 1)

            def turn_fields(b, r):
                pe.wait_ge(b.gathered, 16 * 2 * KW * (r + 1))
                pe.wait_ge(b.win_kept, GWIN + NW * r)
                for f in range(FLD):
                    if f >= 2:
                        pe.wait_ge(b.turned_used, FLD * r + f - 1)
                    to = bank(2 * (f % 2), 2).rearrange("p (k w) -> p k w", w=2 * P)
                    for k in range(KW):
                        for h in range(2):
                            rows = win[h][0:NWH[h], k * ROWE:(k + 1) * ROWE].rearrange("w (e f) -> w e f", f=FLD)[:, :, f]
                            last = T.transpose(to[:, k, h * P:h * P + NWH[h]], rows, ident[0:NWH[h], 0:NWH[h]])
                    last.then_inc(b.turned, 1)

            def windows(b, r):
                with pe.Fori(0, STEPS) as s:
                    w0 = s * GWIN
                    for u in range(GWIN):
                        pe.wait_ge(b.ring_ready, r * NW + w0 + u + 1)
                        pe.wait_ge(b.win_kept, r * NW + w0 + u + 1)
                        for k in range(KW):
                            last = T.matmul(bank(u)[:, 0:HC], ring1[:, KW * u + k, :], ring2[:, KW * u + k, :],
                                            start=(k == 0), stop=(k == KW - 1))
                        last.then_inc(b.ring_used, 1)
                    pe.wait_ge(b.sums_kept, START1 + r * STEPS + s)
                    for u in range(GWIN):
                        for k in range(KW):
                            last = T.matmul(bank(4)[0:12, u * WD:(u + 1) * WD],
                                            v3[:, ds(w0 + (k * NW + u), 1), :].rearrange("p e c -> p (e c)"),
                                            ringd[:, k, u, :], start=(k == 0), stop=(k == KW - 1))
                    last.then_inc(b.sums_done, 1)

            turn_fields(fast, 0)
            pe.wait_ge(captured, 1)
            T.matmul(bank(7)[:, 0:1], ones_f, flag_f[:, 0:1], start=True, stop=True).then_inc(cap_summed, 1)
            windows(fast, 0)
            pe.wait_ge(flag_ready, 1)
            general = pe.value_load(flag[0:1, 0:1], min_val=0, max_val=1)
            with pe.If(general):
                with pe.Fori(0, ROUNDS) as r:
                    turn_fields(slow, r)
                    windows(slow, r)
            with pe.Else():
                pe.nop()

            pe.wait_ge(built, 1)
            for g in range(NG):
                pe.wait_ge(grp_loaded[g % 2], 16 * (g // 2 + 1) + 16 * (g == NG - 1))
                if g >= 2:
                    pe.wait_ge(xT_done, g - 1)
                for b in range(GB):
                    for h in range(2):
                        last = T.transpose(ptr[g % 2][:, h * GW + b * P:h * GW + (b + 1) * P],
                                           rbuf[g % 2][:, b * F + h * P:b * F + (h + 1) * P], ident[:, :])
                last.then_inc(turned_grp, 1)

            def turn_batch(c, m):
                q, g = divmod(m, NG)
                pe.wait_ge(adj_turned_out, c * TURNS + m + 1)
                for k in range(GB):
                    last = T.transpose(turn_ps[m % 2][:, k * P:(k + 1) * P],
                                       adj_chunk(c)[:, g * GB + k, q * SW:(q + 1) * SW], ident_h[:, :])
                last.then_inc(adj_turned, 1)

            def product(g, c, t, edges, turning=False):
                pe.wait_ge(agg_evac, START2 + 2 * g)
                for b in range(NB):
                    for a in range(2):
                        for h in range(2):
                            last = T.matmul(acc[t][h], parts[:, a, b, h * P:(h + 1) * P], adj_chunk(c)[:, b, :],
                                            start=(b == 0 and a == 0),
                                            stop=(not edges and b == NB - 1 and a == 1))
                            if not edges and b == NB - 1 and a == 1:
                                last.then_inc(spmm_done, 1)
                    if turning and b < TURNS:
                        turn_batch(c, b)
                if edges:
                    pe.wait_ge(es_loaded, 16 * (g + 1))
                    for h in range(2):
                        T.matmul(acc[t][h], ewt[:, h * P:(h + 1) * P], es[0:12, :], start=False,
                                 stop=True).then_inc(spmm_done, 1)

            def linear(l, c, t, j):
                g = CH * l + c
                pe.wait_ge(hT_loaded[t], 16 * ([4, 3][t] * l + j + 1))
                pe.wait_ge(agg_evac, START2 + 2 * g + 4)
                pe.wait_ge(lin_evac, START2 + 2 * g)
                hc = rbuf[t][:, 0:2 * CW].rearrange("p (h n) -> p h n", h=2)
                for h in range(2):
                    for k in range(4):
                        last = T.matmul(lin_h[h], wl[:, k, h * P:(h + 1) * P], hc[:, k, :] if k < 2 else agg[:, k - 2, :],
                                        start=(k == 0), stop=(k == 3))
                last.then_inc(lin_done, 1)

            def layer(l, turning=False):
                pe.wait_ge(parts_hi, NG * (l + 1))
                pe.wait_ge(parts_lo, NG * (l + 1))
                pe.wait_ge(w_loaded, 16 * 7 * (l + 1))
                product(CH * l, 0, 0, True, turning)
                with pe.Fori(0, CH // 2) as j:
                    for t in range(2):
                        product(CH * l + 2 * j + t + 1, 2 * j + t + 1, 1 - t, True, turning)
                        linear(l, 2 * j + t, t, j)
                linear(l, CH - 1, 0, CH // 2)

            def turn_groups(l):
                for g in range(NG):
                    pe.wait_ge(norm_done, NG * l + g + 1)
                    if g >= 2:
                        if l is LAST:
                            pe.wait_ge(ln_rows, g - 1)
                        else:
                            pe.wait_ge(parts_hi, NG * (l + 1) + g - 1)
                            pe.wait_ge(parts_lo, NG * (l + 1) + g - 1)
                    v = rbuf[g % 2].rearrange("p (h n) -> p h n", h=2)
                    for b in range(GB):
                        for h in range(2):
                            last = T.transpose(ptr[g % 2][:, b * F + h * P:b * F + (h + 1) * P],
                                               v[:, h, b * P:(b + 1) * P], ident[:, :])
                    last.then_inc(turned_grp, 1)

            LAST = LAYERS - 1
            layer(0, turning=True)
            turn_groups(0)
            with pe.Fori(1, LAYERS - 1) as l:
                layer(l)
                turn_groups(l)
            layer(LAST)
            turn_groups(LAST)

            for ph in range(4):
                base = CH * (LAYERS + ph)
                if ph == 3:
                    pe.wait_ge(bias_loaded, 32 * 4)
                    for k in range(2):
                        for h in range(2):
                            last = T.transpose(bank(6)[:, h * F + k * P:h * F + (k + 1) * P],
                                               wt[:, k, h * P:(h + 1) * P], ident[:, :])
                    last.then_inc(wt_done, 1)
                pe.wait_ge(parts_hi, NG * (LAYERS + ph + 1))
                pe.wait_ge(parts_lo, NG * (LAYERS + ph + 1))

                def chunk_product(c, t, ph=ph, base=base):
                    if ph == 0:
                        pe.wait_ge(op_loaded, 16 * (c + 1))
                    elif ph == 1:
                        pe.wait_ge(eye_added, c + 1)
                    elif ph == 3:
                        pe.wait_ge(op_loaded, 16 * (2 * CH + c + 1))
                    product(base + c, c, t, False)

                def chunk_linear(c, base=base):
                    g = base + c
                    pe.wait_ge(agg_evac, START2 + 2 * g + 4)
                    pe.wait_ge(lin_evac, START2 + 2 * g)
                    for s in range(SUBS):
                        for h in range(2):
                            last = T.matmul(lin_s[0:SW, s, :], agg[:, h, s * SW:(s + 1) * SW], wd[:, h, :],
                                            start=(h == 0), stop=(h == 1))
                    last.then_inc(lin_done, 1)

                chunk_product(0, 0)
                if ph == 3:
                    pe.wait_ge(wt_kept, 1)
                else:
                    pe.wait_ge(bias_loaded, 32 * (ph + 1))
                with pe.Fori(0, CH // 2) as j:
                    for t in range(2):
                        chunk_product(2 * j + t + 1, 1 - t)
                        chunk_linear(2 * j + t)
                chunk_linear(CH - 1)


def kernel(**inputs):
    import numpy as np
    import concourse.bacc as bacc
    from concourse.bass_utils import run_bass_kernel_spmd

    nc = bacc.Bacc("TRN2", target_bir_lowering=False, num_devices=1)
    arrays, args = {}, []
    for name in INPUTS:
        a = np.ascontiguousarray(inputs[name])
        arrays[f"in_{name}"] = a
        args.append(nc.dram_tensor(f"in_{name}", a.shape, mybir.dt.from_np(a.dtype), kind="ExternalInput").ap())
    args.append(nc.dram_tensor("out", (N, F), mybir.dt.float32, kind="ExternalOutput").ap())
    build(nc, *args)
    r = run_bass_kernel_spmd(nc, [arrays], core_ids=[0])
    return r.results[0]["out"]
```

```python
import concourse.bass as bass
from concourse import mybir
from contextlib import ExitStack

P = 128
N = 3125
F = 256
E = 53125
LAYERS = 5
EPS = 1e-5

NB = -(-N // P)
NR = NB * P
TAIL = N - (NB - 1) * P
CH = 7
CW = 448
NPAD = CH * CW
LASTW = N - (CH - 1) * CW
SUBS = 4
SW = CW // SUBS
GB = 5
NG = NB // GB
GW = GB * P
CF = NB * CW

EC = -(-E // P)
ELAST = E - (P - 1) * EC
EB = 8
HB = 4
SB = 16
WD = 16
NW = NPAD // WD
NWH = [P, NW - P]
KW = 3
NK = KW * NW
COPIES = 8
FLD = 5
ROWE = P * FLD
CPR = 1 + EC + 4
GAP = CPR * P - EC * P - WD
ROUNDS = -(-E // (KW * P))
TURNS = NG + 1
GWIN = 4
CSTEP = CW // (WD * GWIN)
STEPS = CH * CSTEP
HC = NB * WD

START1, START2, START16 = 1, 2, 16

S_BN = 256.0
S_LN = 2048.0
S_TAB = 4096.0

INPUTS = ["x", "src", "dst", "edge_attr_4", "L0_gnn_mlp_w", "L0_gnn_mlp_b", "L0_gnn_ew1", "L0_gnn_ew2",
          "L0_gnn_bn_g", "L0_gnn_bn_b", "L1_gnn_W", "L1_gnn_b", "L2_gnn_W1", "L2_gnn_b1", "L2_gnn_W2",
          "L2_gnn_b2", "L3_gnn_W", "L3_gnn_b"]


class Steps:

    def __init__(self, eng, sem):
        self.eng, self.sem, self.n = eng, sem, 0

    def __call__(self, ins):
        ins.then_inc(self.sem, 1)
        self.n = self.n + 1
        self.eng.wait_ge(self.sem, self.n)


def build(nc, x, src, dst, attr, mlp_w, mlp_b, ew1, ew2, bn_g, bn_b, w_1, b_1, w_21, b_21, w_22, b_22,
          w_3, b_3, out):
    f32, f16, bf16, i32 = mybir.dt.float32, mybir.dt.float16, mybir.dt.bfloat16, mybir.dt.int32
    ALU = mybir.AluOpType
    ACT = mybir.ActivationFunctionType
    AX = mybir.AxisListType
    ds = bass.ds

    def flat(ap, offset, dims):
        return bass.AP(ap.tensor, offset, dims)

    ctx = ExitStack()
    with ctx:
        def sb(name, shape, dt):
            return ctx.enter_context(nc.sbuf_tensor(name, shape, dt))

        def sem(name):
            return ctx.enter_context(nc.semaphore(name))

        def dram(name, shape, dt):
            return nc.dram_tensor(name, shape, dt).ap()

        slo_row = dram("slo_row", (P, EC), f16)
        table = dram("edge_table", (COPIES * CPR, ROWE), f32)
        adj_dram = dram("adj_dram", (NR, NR), f16)
        adjT_dram = dram("adjT_dram", (NR, NR), f16)
        dinv_row = dram("dinv_row", (NR,), f32)
        dinv2_row = dram("dinv2_row", (NR,), f32)
        dout_row = dram("dout_row", (NR,), f32)
        edge_sum = dram("edge_sum", (12, NPAD), f32)
        hT = dram("hT", (2, P, NR), f32)
        rawT = dram("rawT", (2, P, NR), f32)
        xs = [dram(f"x{i}", (NR, F), f32) for i in range(1, 5)]

        adj = sb("adj", [P, CH * CF], f16)
        work = sb("work", [P, 12672], f32)
        adj32 = adj[:, :].bitcast(f32)

        def cut(base, at, n, dt=f32):
            v = base[:, at:at + n]
            return v if dt == f32 else v.bitcast(dt)

        slo_bc = cut(adj32, 0, 26624, f16)
        oh_hi = cut(adj32, 26624, 5200, f16).rearrange("p (e b) -> p e b", b=NB)
        src_i = cut(adj32, 31824, EC, i32)
        dst_i = cut(adj32, 32240, EC, i32)
        dlo_i = cut(adj32, 32656, EC, i32)
        dhi_i = cut(adj32, 33072, EC, i32)
        slo_i = cut(adj32, 33488, EC, i32)
        shi_i = cut(adj32, 33904, EC, i32)
        dlo_f = cut(adj32, 34320, EC)
        dhi_h = cut(adj32, 34736, EC // 2, f16)
        slo_h = cut(adj32, 34944, EC // 2, f16)
        shi_h = cut(adj32, 35152, EC // 2, f16)
        cmp_h = cut(adj32, 35360, NW * 26 // 2, f16).rearrange("p (w g) -> p w g", g=26)
        degs = cut(adj32, 37908, 600).rearrange("p (i t b) -> p i t b", t=2, b=NB)
        att = cut(work, 0, 4 * EC).rearrange("p (e k) -> p e k", k=4)
        tab = cut(work, 1664, FLD * EC).rearrange("p (e k) -> p e k", k=FLD)
        sent = cut(work, 3744, GAP * FLD).rearrange("p (e k) -> p e k", k=FLD)
        hring = cut(work, 6864, HB * EB * P // 2, f16).rearrange("p (s c) -> p s c", c=P)
        sel = [cut(work, 7888 + SB * NB * i, SB * NB) for i in range(2)]
        dinvs = cut(work, 8688, EC)
        part = cut(work, 9104, NW)
        dwl_i = cut(work, 9300, 26, i32)
        dwl_h = cut(work, 9326, 13, f16)
        zeros = cut(work, 9340, 800)
        win = [cut(work, 0, KW * ROWE), cut(work, 1920, KW * ROWE)]
        ring1 = cut(work, 0, 768, f16).rearrange("p (s c) -> p s c", c=P)
        ring2 = cut(work, 768, 2400, f16).rearrange("p (s c) -> p s c", c=HC)
        ringd = cut(work, 3168, CSTEP * 96, bf16).rearrange("p (s k w c) -> p s k w c", s=CSTEP, k=KW, c=WD)
        key_i = cut(work, 3840, NK, i32)
        fa_i = cut(work, 4428, NK, i32)
        fb_i = cut(work, 5016, NK, i32)
        mask = cut(work, 5604, NK)
        slom = cut(work, 6192, NK)
        key2 = cut(work, 6780, NK)
        dlom = cut(work, 7368, NK)
        v3 = cut(work, 7956, 6 * NK, bf16).rearrange("p (e c) -> p e c", c=12)
        es_out = cut(work, 5016, CW)
        rest1 = cut(work, 3840, NK)
        rest2 = cut(work, 4428, NK)
        iot_i = cut(work, 11484, HC, i32)
        iot = cut(work, 11884, HC // 2, f16)
        ones_f = cut(work, 12084, P)
        ones_h = cut(work, 12212, 64, f16)
        zero_h = cut(work, 12276, 64, f16)
        dist = cut(work, 12340, GWIN * P // 2, f16).rearrange("p (u c) -> p u c", c=P)
        slom_neg = cut(work, 5600, NK + GWIN)
        parts = cut(work, 0, 6400, f16).rearrange("p (t b f) -> p t b f", t=2, f=F)
        rbuf = [cut(work, 6400 + 1280 * i, 1280) for i in range(2)]
        agg = cut(work, 8960, 2 * CW).rearrange("p (h n) -> p h n", h=2)
        nraw = cut(work, 9856, 2 * CW).rearrange("p (h n) -> p h n", h=2)
        wl = cut(work, 10752, 4 * F).rearrange("p (k n) -> p k n", k=4)
        bc = cut(work, 11776, CW)
        es = cut(work, 12224, CW)
        turn = [cut(work, 6400 + 1280 * i + 2 * CW, GW // 2, f16) for i in range(2)]
        xgrp = [cut(work, 8960, GB * F),
                cut(work, 10752, GB * F)]
        wd = cut(work, 9856, 2 * F).rearrange("p (h n) -> p h n", h=2)
        bias = cut(work, 10368, F)
        xr2 = cut(work, 10624, SUBS * F).rearrange("p (s f) -> p s f", f=F)
        tmp = cut(work, 11648, SUBS * F).rearrange("p (s f) -> p s f", f=F)
        wt = cut(work, 10624, 2 * F).rearrange("p (h n) -> p h n", h=2)

        pidx = sb("pidx", [P, 1], f32)
        pidx_neg = sb("pidx_neg", [P, 1], f32)
        pidx_i = sb("pidx_i", [P, 1], i32)
        ident = sb("ident", [P, P], f32)
        ident_h = sb("ident_h", [P, P], f16)
        dtab = sb("dtab", [P, 2, NB], f16)
        scl = sb("scl", [P, 2, NB], f32)
        idx = sb("idx", [P, 2 * KW], i32)
        starts = sb("starts", [P, 2, 4], i32)
        flag_f = sb("flag_f", [P, 2], f32)
        flag = sb("flag", [P, 1], i32)
        dop = sb("dop", [P, CH + 1, NB], f32)
        fcol = sb("fcol", [P, 3, LAYERS, 2], f32)
        ewt = sb("ewt", [12, F], f32)
        stats = sb("stats", [P, 2, CH, 6], f32)
        mv = sb("mv", [P, 2, 2], f32)
        bnsc = sb("bnsc", [P, 4, 2], f32)
        nrow = sb("nrow", [SW, 4, CH * SUBS], f32)
        ln_st = sb("ln_st", [P, GB, 6], f32)
        ln_mv = sb("ln_mv", [P, GB, 2], f32)
        ln_r = sb("ln_r", [P, 2, GB], f32)

        ps = ctx.enter_context(nc.psum_tensor("ps", [P, 8 * 512], f32))

        def bank(i, n=1):
            return ps[:, 512 * i:512 * (i + n)]

        acc = [[bank(2 * t + h)[:, 0:CW] for h in range(2)] for t in range(2)]
        lin = bank(4, 2)
        lin_h = [bank(4)[:, 0:CW], bank(5)[:, 0:CW]]
        lin_s = lin.rearrange("p (s f) -> p s f", f=F)
        turn_ps = [bank(6 + t)[0:SW, 0:GW // 2].bitcast(f16) for t in range(2)]
        ptr = [bank(2 + 3 * t, 3)[:, 0:GB * F] for t in range(2)]

        def adj_chunk(c):
            return adj[:, ds(c * CF, CF)].rearrange("p (b n) -> p b n", n=CW)

        (consts_i, consts, zeros_set, padded, attr_loaded, act_step, dist_ready, onehot_act, keys_ready, zero_stored, edges_loaded, fields_done, slo_stored, slo_loaded,
         hist_ready, hist_used, deg_done, root_in, root_out, onehot_t, tab_ready, sel_ready, sel_used,
         table_done, table_stored, part_ready, starts_ready, idx_ready, rows_stored,
         built, flag_ready, captured, cap_summed, adj_stored, adj_restored, dout_part, dout_ready, dout_stored,
         rows_loaded, dve_step, pool_step, es_zeroed, vec_step, pad_step, settled, es_free, adj_turned, adj_turned_out, turn_even, turn_odd) = [sem(n) for n in (
             "consts_i consts zeros_set padded attr_loaded act_step dist_ready onehot_act keys_ready zero_stored edges_loaded fields_done slo_stored slo_loaded "
             "hist_ready hist_used deg_done root_in root_out onehot_t tab_ready sel_ready sel_used "
             "table_done table_stored part_ready starts_ready idx_ready rows_stored "
             "built flag_ready captured cap_summed adj_stored adj_restored dout_part dout_ready dout_stored "
             "rows_loaded dve_step pool_step es_zeroed vec_step pad_step settled es_free adj_turned adj_turned_out turn_even turn_odd").split()]

        def settle(eng):
            eng.sem_inc(settled, 1)

        class Build:

            def __init__(self, way):
                self.gathered = sem(f"gathered_{way}")
                self.turned = sem(f"turned_{way}")
                self.turned_used = sem(f"turned_used_{way}")
                self.ring_ready = sem(f"ring_ready_{way}")
                self.ring_used = sem(f"ring_used_{way}")
                self.sums_done = sem(f"sums_done_{way}")
                self.win_kept = sem(f"win_kept_{way}")
                self.sums_kept = sem(f"sums_kept_{way}")
                self.es_stored = sem(f"es_stored_{way}")

        fast, slow = Build("fast"), Build("slow")

        (parts_hi, parts_lo, agg_evac, spmm_done, lin_done, lin_evac, hT_even, hT_odd, w_loaded, bc_loaded,
         es_loaded, raw_stored, stats_done, var_ready, std_ready, bn_ready, grp_even, grp_odd, norm_done,
         turned_grp, hT_stored, xT_done, fcol_loaded, x_even, x_odd, op_loaded, eye_added, y_ready, x_stored,
         wt_done, wt_kept, bias_loaded, xr_even, xr_odd, xr2_loaded, ln_var, ln_std, pad_set, ln_rows) = [sem(n) for n in (
             "parts_hi parts_lo agg_evac spmm_done lin_done lin_evac hT_even hT_odd w_loaded bc_loaded "
             "es_loaded raw_stored stats_done var_ready std_ready bn_ready grp_even grp_odd norm_done "
             "turned_grp hT_stored xT_done fcol_loaded x_even x_odd op_loaded eye_added y_ready x_stored "
             "wt_done wt_kept bias_loaded xr_even xr_odd xr2_loaded ln_var ln_std pad_set ln_rows").split()]
        turn_stored, x_loaded = [turn_even, turn_odd], [x_even, x_odd]
        hT_loaded, grp_loaded, xr_loaded = [hT_even, hT_odd], [grp_even, grp_odd], [xr_even, xr_odd]

        block = ctx.enter_context(nc.Block())

        @block.gpsimd
        def _(pool):
            nc.gpsimd.iota(iot_i, pattern=[[1, HC]], base=0, channel_multiplier=0).then_inc(consts_i, 1)
            nc.gpsimd.iota(pidx_i[:, :], pattern=[[0, 1]], base=0, channel_multiplier=1).then_inc(consts_i, 1)
            nc.gpsimd.memset(zeros, 0.0).then_inc(zeros_set, 1)

            def gather(b, base):
                for h in range(2):
                    for k in range(KW):
                        nc.gpsimd.indirect_dma_start(
                            win[h][0:NWH[h], k * ROWE:(k + 1) * ROWE], None, table,
                            bass.IndirectOffsetOnAxis(ap=idx[0:NWH[h], h * KW + k:h * KW + k + 1], axis=0),
                        ).then_inc(b.gathered, 16)

            pool.wait_ge(idx_ready, 1)
            pool.wait_ge(table_stored, 16 * (2 * COPIES + 1))
            gather(fast, 0)

            pool.wait_ge(flag_ready, 1)
            general = pool.value_load(flag[0:1, 0:1], min_val=0, max_val=1)
            with pool.If(general):
                pool.wait_ge(es_zeroed, 16 * CH)
                with pool.Fori(0, ROUNDS) as r:
                    pool.wait_ge(idx_ready, r + 2)
                    settle(pool)
                    gather(slow, r)
                    with pool.Fori(0, CH) as c:
                        pool.wait_ge(slow.sums_kept, START1 + (r * CH + c + 1))
                        pool.dma_start(edge_sum[:, ds(c * CW, CW)], es_out[0:12, :],
                                       accum_op=ALU.add).then_inc(slow.es_stored, 16)
                        pool.wait_ge(slow.es_stored, 16 * (r * CH + c + 1))
                        pool.sem_inc(es_free, 1)
            with pool.Else():
                pool.nop()

            def eye(c, b, at, p0, w):
                v = adj_chunk(c)[:, ds(b, 1), at:at + w].rearrange("p b n -> p (b n)")
                return nc.gpsimd.tensor_tensor(v, v, ident_h[:, p0:p0 + w], ALU.add)

            def eyes(c, j, t):
                if t == 0:
                    at = [(0, 0, P), (P, 0, P), (2 * P, 0, P), (3 * P, 0, CW - 3 * P)]
                    bs = [7 * j, 7 * j + 1, 7 * j + 2, 7 * j + 3]
                else:
                    at = [(0, 64, 64), (64, 0, P), (192, 0, P), (320, 0, P)]
                    bs = [7 * j + 3, 7 * j + 4, 7 * j + 5, 7 * j + 6]
                pool.wait_ge(op_loaded, 16 * (CH + c + 1))
                for b, (a, p0, w) in zip(bs, at):
                    last = eye(c, b, a, p0, w)
                last.then_inc(eye_added, 1)

            with pool.Fori(0, CH // 2) as j:
                for t in range(2):
                    eyes(2 * j + t, j, t)
            eyes(CH - 1, CH // 2, 0)

        @block.sync
        def _(sp):
            sp.wait_ge(padded, 1)
            full = (P - 1) * EC
            sp.dma_start(src_i[0:P - 1, :], src[0:full].rearrange("(p e) -> p e", e=EC)).then_inc(edges_loaded, 16)
            sp.dma_start(dst_i[0:P - 1, :], dst[0:full].rearrange("(p e) -> p e", e=EC)).then_inc(edges_loaded, 16)
            sp.dma_start(src_i[P - 1:P, 0:ELAST], src[full:E].rearrange("(p e) -> p e", p=1)).then_inc(edges_loaded, 16)
            sp.dma_start(dst_i[P - 1:P, 0:ELAST], dst[full:E].rearrange("(p e) -> p e", p=1)).then_inc(edges_loaded, 16)
            sp.wait_ge(padded, 2)
            sp.dma_start(att[0:P - 1, :, :], attr[0:full, :].rearrange("(p e) k -> p e k", e=EC)).then_inc(attr_loaded, 16)
            sp.dma_start(att[P - 1:P, 0:ELAST, :], attr[full:E, :].rearrange("(p e) k -> p e k", p=1)).then_inc(attr_loaded, 16)
            sp.wait_ge(zeros_set, 1)
            sp.wait_ge(fields_done, 1)
            sp.dma_start(slo_row, slo_h).then_inc(slo_stored, 16)
            sp.wait_ge(slo_stored, 16)
            q = P * EC // 4
            for i in range(4):
                sp.dma_start(slo_bc[:, i * q:(i + 1) * q], flat(slo_row, i * q, [[0, P], [1, q]])).then_inc(slo_loaded, 16)
            zh = zeros.bitcast(f16).rearrange("p (b n) -> p b n", b=NB)
            zf = zeros[:, 0:F]
            sp.dma_start(adj_dram[:, NPAD:NR].rearrange("(b p) n -> p b n", p=P), zh[:, :, 0:NR - NPAD]).then_inc(zero_stored, 16)
            sp.dma_start(rawT[:, :, NPAD:NR].rearrange("h p n -> p h n"),
                         zf[:, 0:128].rearrange("p (h n) -> p h n", h=2)).then_inc(zero_stored, 16)
            sp.dma_start(adjT_dram[NPAD:NR, :].rearrange("r (x c) -> (r x) c", x=2),
                         zeros.bitcast(f16)).then_inc(zero_stored, 16)
            for t in xs[1:]:
                sp.dma_start(t[NPAD:NR, :], zf[0:NR - NPAD, :]).then_inc(zero_stored, 16)
            sp.dma_start(fcol[:, 0, :, :], mlp_b.rearrange("l (h p) -> p (l h)", p=P), allow_slow_non_contiguous=True).then_inc(fcol_loaded, 16)
            sp.dma_start(fcol[:, 1, :, :], bn_g.rearrange("l (h p) -> p (l h)", p=P), allow_slow_non_contiguous=True).then_inc(fcol_loaded, 16)
            sp.dma_start(fcol[:, 2, :, :], bn_b.rearrange("l (h p) -> p (l h)", p=P), allow_slow_non_contiguous=True).then_inc(fcol_loaded, 16)
            sp.wait_ge(deg_done, 1)
            for t, row in enumerate((dinv_row, dinv2_row)):
                sp.dma_start(row.rearrange("(b p) -> p b", p=P), degs[:, 5, t, :], allow_slow_non_contiguous=True).then_inc(rows_stored, 16)
            sp.wait_ge(table_done, 1)
            for j in range(COPIES):
                at = (j * CPR * P + P - WD * j) * FLD
                sp.dma_start(flat(table, at, [[EC * FLD, P], [1, EC * FLD]]),
                             tab.rearrange("p e k -> p (e k)")).then_inc(table_stored, 16)
                sp.dma_start(flat(table, at + P * EC * FLD, [[GAP * FLD, 1], [1, GAP * FLD]]),
                             sent[0:1, :, :].rearrange("p e k -> p (e k)")).then_inc(table_stored, 16)
            sp.dma_start(table[0:1, :], sent[0:1, 0:P, :].rearrange("p e k -> p (e k)")).then_inc(table_stored, 16)
            def store_adj(c, done):
                sp.dma_start(adj_dram[:, c * CW:(c + 1) * CW].rearrange("(b p) n -> p b n", p=P),
                             adj_chunk(c)).then_inc(done, 16)

            for c in range(CH):
                sp.wait_ge(fast.sums_kept, START1 + c + 1)
                sp.dma_start(edge_sum[:, c * CW:(c + 1) * CW], es_out[0:12, :]).then_inc(fast.es_stored, 16)
                sp.wait_ge(fast.win_kept, GWIN + (c + 1) * CSTEP * GWIN)
                store_adj(c, adj_stored)
            sp.wait_ge(flag_ready, 1)
            general = sp.value_load(flag[0:1, 0:1], min_val=0, max_val=1)
            with sp.If(general):
                sp.wait_ge(fast.es_stored, START16 + 16 * CH)
                sp.wait_ge(zeros_set, 2)
                for c in range(CH):
                    sp.dma_start(edge_sum[:, c * CW:(c + 1) * CW], es_out[0:12, :]).then_inc(es_zeroed, 16)
                sp.wait_ge(built, 1)
                sp.wait_ge(adj_stored, 16 * CH)
                for c in range(CH):
                    store_adj(c, adj_restored)
                sp.wait_ge(adj_restored, 16 * CH)
            with sp.Else():
                sp.nop()

            sp.wait_ge(built, 1)
            sp.wait_ge(fast.es_stored, START16 + 16 * CH)
            sp.wait_ge(rows_stored, 32)
            sp.wait_ge(zero_stored, 16 * 6)

            for g in range(NG):
                if g >= 2:
                    sp.wait_ge(turned_grp, g - 1)
                    sp.wait_ge(parts_hi, g - 1)
                    sp.wait_ge(parts_lo, g - 1)
                v = rbuf[g % 2].rearrange("p (b f) -> p b f", f=F)
                if g < NG - 1:
                    sp.dma_start(v, x[g * GW:(g + 1) * GW, :].rearrange("(b p) f -> p b f", p=P)).then_inc(grp_loaded[g % 2], 16)
                else:
                    sp.wait_ge(pad_set, 1)
                    sp.dma_start(v[:, 0:GB - 1, :], x[g * GW:(NB - 1) * P, :].rearrange("(b p) f -> p b f", p=P)).then_inc(grp_loaded[0], 16)
                    sp.dma_start(v[0:TAIL, GB - 1, :], x[(NB - 1) * P:N, :]).then_inc(grp_loaded[0], 16)
                if g >= 1:
                    sp.wait_ge(xT_done, g)
                    sp.dma_start(hT[:, :, (g - 1) * GW:g * GW].rearrange("h p n -> p h n"),
                                 xgrp[0].rearrange("p (h n) -> p h n", h=2)).then_inc(hT_stored, 16)
            sp.wait_ge(xT_done, NG)
            sp.dma_start(hT[:, :, (NG - 1) * GW:NR].rearrange("h p n -> p h n"),
                         xgrp[0].rearrange("p (h n) -> p h n", h=2)).then_inc(hT_stored, 16)

            def load_weights(l):
                sp.wait_ge(lin_done, START1 + CH * l + 1)
                sp.dma_start(wl, mlp_w[ds(l, 1), :, :].rearrange("l (k p) n -> p (l k) n", p=P)).then_inc(w_loaded, 16)
                for i in range(3):
                    sp.dma_start(ewt[4 * i:4 * i + 3, P:F], ew2[ds(l, 1), :, :].rearrange("l k n -> (l k) n")).then_inc(w_loaded, 16)
                    sp.dma_start(ewt[4 * i + 3:4 * i + 4, 0:P], ew1[ds(l, 1), :, :].rearrange("l k n -> (l k) n")).then_inc(w_loaded, 16)

            LAST = LAYERS - 1

            sp.wait_ge(adj_stored, 16 * CH)

            def store_raw(g, c):
                sp.wait_ge(lin_evac, START2 + 2 * g + 2)
                sp.dma_start(rawT[:, :, ds(c * CW, CW)].rearrange("h p n -> p h n"), nraw).then_inc(raw_stored, 16)

            def load_reverse(c):
                sp.dma_start(adj_chunk(c), adjT_dram[:, ds(c * CW, CW)].rearrange("(b p) n -> p b n", p=P)).then_inc(op_loaded, 16)

            def chunk(l, c, t, j, first):
                g = CH * l + c
                sp.wait_ge(agg_evac, START2 + 2 * g + 2)
                sp.dma_start(bc, flat(dinv_row, c * CW, [[0, P], [1, CW]])).then_inc(bc_loaded, 16)
                sp.wait_ge(spmm_done, START2 + 2 * g)
                sp.dma_start(es[0:12, :], edge_sum[:, ds(c * CW, CW)]).then_inc(es_loaded, 16)
                sp.wait_ge(lin_done, START1 + g)
                sp.dma_start(rbuf[t][:, 0:2 * CW].rearrange("p (h n) -> p h n", h=2),
                             hT[:, :, ds(c * CW, CW)].rearrange("h p n -> p h n")).then_inc(hT_loaded[t], 16)
                if not first:
                    store_raw(g - 1, c - 1)
                    if l is LAST:
                        load_reverse(c - 1)
                        sp.wait_ge(op_loaded, 16 * c)
                        settle(sp)

            def products(l):
                load_weights(l)
                sp.wait_ge(hT_stored, 16 * NG * (l + 1))
                settle(sp)
                sp.wait_ge(parts_lo, NG * (l + 1))
                sp.wait_ge(parts_hi, NG * (l + 1))
                chunk(l, 0, 0, 0, True)
                with sp.Fori(0, CH // 2) as j:
                    chunk(l, 2 * j + 1, 1, j, False)
                    chunk(l, 2 * j + 2, 0, j + 1, False)
                store_raw(CH * l + CH - 1, CH - 1)
                sp.wait_ge(raw_stored, START16 + 16 * CH * (l + 1))
                if l is not LAST:
                    for t in range(2):
                        sp.wait_ge(turn_stored[t], START16 + 16 * (CH - 1) * (TURNS // 2) * (l + 1))

            def load_raw_group(l, g):
                if g >= 2:
                    sp.wait_ge(turned_grp, NG * (l + 1) + g - 1)
                    if l is not LAST:
                        settle(sp)
                        sp.wait_ge(hT_stored, 16 * (NG * (l + 1) + g - 1))
                sp.dma_start(rbuf[g % 2].rearrange("p (h n) -> p h n", h=2),
                             rawT[:, :, g * GW:(g + 1) * GW].rearrange("h p n -> p h n")).then_inc(grp_loaded[g % 2], 16)

            with sp.Fori(0, LAYERS - 1) as l:
                products(l)
                for g in range(NG):
                    load_raw_group(l, g)
                    if g >= 1:
                        sp.wait_ge(norm_done, NG * l + g)
                        sp.dma_start(hT[:, :, (g - 1) * GW:g * GW].rearrange("h p n -> p h n"),
                                     rbuf[(g - 1) % 2].rearrange("p (h n) -> p h n", h=2)).then_inc(hT_stored, 16)
                sp.wait_ge(norm_done, NG * l + NG)
                sp.dma_start(hT[:, :, (NG - 1) * GW:NR].rearrange("h p n -> p h n"),
                             rbuf[(NG - 1) % 2].rearrange("p (h n) -> p h n", h=2)).then_inc(hT_stored, 16)
            products(LAST)

            sp.wait_ge(stats_done, START1 + CH * LAYERS)
            def load_x_group(g):
                v = xgrp[g % 2].rearrange("p (b f) -> p b f", f=F)
                if g < NG - 1:
                    sp.dma_start(v, x[g * GW:(g + 1) * GW, :].rearrange("(b p) f -> p b f", p=P)).then_inc(x_loaded[g % 2], 16)
                else:
                    sp.wait_ge(pad_set, 2)
                    sp.dma_start(v[:, 0:GB - 1, :], x[g * GW:(NB - 1) * P, :].rearrange("(b p) f -> p b f", p=P)).then_inc(x_loaded[g % 2], 16)
                    sp.dma_start(v[0:TAIL, GB - 1, :], x[(NB - 1) * P:N, :]).then_inc(x_loaded[g % 2], 16)

            for g in range(2):
                load_raw_group(LAST, g)
                load_x_group(g)
            load_reverse(CH - 1)
            for g in range(NG):
                if g + 2 < NG:
                    load_raw_group(LAST, g + 2)
                sp.wait_ge(y_ready, g + 1)
                sp.wait_ge(parts_hi, NG * LAYERS + g + 1)
                sp.dma_start(xs[0][g * GW:(g + 1) * GW, :].rearrange("(b p) f -> p b f", p=P),
                             xgrp[g % 2].rearrange("p (b f) -> p b f", f=F)).then_inc(x_stored, 16)
                sp.wait_ge(x_stored, 16 * (g + 1))
                if g + 2 < NG:
                    load_x_group(g + 2)

            sp.wait_ge(dout_ready, 1)
            sp.dma_start(dout_row.rearrange("(b p) -> p b", p=P), dop[:, CH, :], allow_slow_non_contiguous=True).then_inc(dout_stored, 16)
            sp.wait_ge(dout_stored, 16)
            sp.dma_start(nrow[:, 2, :], dout_row[0:NPAD].rearrange("(s p) -> p s", p=SW), allow_slow_non_contiguous=True).then_inc(rows_loaded, 16)
            sp.dma_start(nrow[:, 3, :], dinv2_row[0:NPAD].rearrange("(s p) -> p s", p=SW), allow_slow_non_contiguous=True).then_inc(rows_loaded, 16)

            for ph, (w, b) in enumerate(((w_1, b_1), (w_21, b_21), (w_22, b_22), (w_3, b_3))):
                base = CH * (LAYERS + ph)
                sp.wait_ge(lin_done, START1 + base + 1)
                if ph:
                    sp.wait_ge(y_ready, NG + CH * ph)
                    sp.wait_ge(x_stored, 16 * (NG + CH * ph))
                sp.dma_start(wt if ph == 3 else wd, w.rearrange("(h p) n -> p h n", p=P)).then_inc(bias_loaded, 16)
                sp.dma_start(bias[0:SW, :], flat(b, 0, [[0, SW], [1, F]])).then_inc(bias_loaded, 16)
                if ph:
                    for g in range(NG):
                        if g >= 2:
                            sp.wait_ge(parts_hi, NG * (LAYERS + ph) + g - 1)
                            sp.wait_ge(parts_lo, NG * (LAYERS + ph) + g - 1)
                        sp.dma_start(rbuf[g % 2].rearrange("p (b f) -> p b f", f=F),
                                     xs[ph][g * GW:(g + 1) * GW, :].rearrange("(b p) f -> p b f", p=P)).then_inc(grp_loaded[g % 2], 16)
                    sp.wait_ge(parts_hi, NG * (LAYERS + ph + 1))
                    sp.wait_ge(parts_lo, NG * (LAYERS + ph + 1))
                sp.wait_ge(parts_hi, NG * (LAYERS + 1))

                def load_x(c, t, ph=ph):
                    sp.dma_start(rbuf[t][0:SW, 0:SUBS * F].rearrange("p (s f) -> p s f", f=F),
                                 xs[ph][ds(c * CW, CW), :].rearrange("(s p) f -> p s f", p=SW)).then_inc(xr_loaded[t], 16)

                def store_y(c, t, ph=ph, base=base):
                    sp.wait_ge(y_ready, NG + CH * ph + c + 1)
                    v = rbuf[t][0:SW, 0:SUBS * F].rearrange("p (s f) -> p s f", f=F)
                    if ph < 3:
                        sp.dma_start(xs[ph + 1][ds(c * CW, CW), :].rearrange("(s p) f -> p s f", p=SW), v).then_inc(x_stored, 16)
                    elif isinstance(c, int) and c == CH - 1:
                        at = c * CW + (SUBS - 1) * SW
                        sp.dma_start(out[c * CW:at, :].rearrange("(s p) f -> p s f", p=SW), v[:, 0:SUBS - 1, :]).then_inc(x_stored, 16)
                        sp.dma_start(out[at:N, :], v[0:N - at, SUBS - 1, :]).then_inc(x_stored, 16)
                    else:
                        sp.dma_start(out[ds(c * CW, CW), :].rearrange("(s p) f -> p s f", p=SW), v).then_inc(x_stored, 16)

                def dense(c, t, first, ph=ph, base=base):
                    if ph == 2:
                        sp.wait_ge(y_ready, NG + CH * ph + c)
                        sp.dma_start(xr2[0:SW, :, :], xs[1][ds(c * CW, CW), :].rearrange("(s p) f -> p s f", p=SW)).then_inc(xr2_loaded, 16)
                    if not first:
                        store_y(c - 1, 1 - t)
                        sp.wait_ge(x_stored, 16 * (NG + CH * ph) + 16 * c)
                    if not (isinstance(c, int) and c == CH - 1):
                        load_x(c + 1, 1 - t)
                    if ph in (0, 2):
                        sp.wait_ge(spmm_done, START2 + 2 * (base + c) + 2)
                        if ph == 0:
                            sp.dma_start(adj_chunk(c), adj_dram[:, ds(c * CW, CW)].rearrange("(b p) n -> p b n", p=P)).then_inc(op_loaded, 16)
                        else:
                            sp.dma_start(adj_chunk(c), adjT_dram[:, ds(c * CW, CW)].rearrange("(b p) n -> p b n", p=P)).then_inc(op_loaded, 16)
                        sp.wait_ge(op_loaded, 16 * (CH * (1 if ph == 0 else 2) + c + 1))
                        settle(sp)

                load_x(0, 0)
                dense(0, 0, True)
                with sp.Fori(0, CH // 2 - 1) as j:
                    dense(2 * j + 1, 1, False)
                    dense(2 * j + 2, 0, False)
                dense(CH - 2, 1, False)
                dense(CH - 1, 0, False)
                store_y(CH - 1, 0)
            sp.wait_ge(x_stored, 16 * (NG + 4 * CH + 1))

        @block.scalar
        def _(act):
            act.wait_ge(consts, 1)
            act.wait_ge(slo_loaded, 64)
            q = P * EC // 4
            quarters = [slo_bc[:, i * q:(i + 1) * q] for i in range(2)]
            for v in quarters:
                nc.scalar.activation(v, v, ACT.Abs, bias=pidx_neg[:, 0:1]).then_inc(act_step, 1)
            for i, v in enumerate(quarters):
                act.wait_ge(act_step, i + 1)
                last = nc.scalar.activation(v, v, ACT.Relu, bias=ones_f[:, 0:1], scale=-1.0)
            last.then_inc(onehot_t, 1)

            act.wait_ge(root_in, 1)
            nc.scalar.activation(degs[:, 2, :, :], degs[:, 1, :, :], ACT.Sqrt).then_inc(root_out, 1)

            def last_block(w, u):
                nc.scalar.activation(dist[:, u, :], iot[:, 1:P + 1], ACT.Abs,
                                     bias=slom_neg[:, ds(w + (KW - 1) * NW, 1)]).then_inc(dist_ready, 1)
                act.wait_ge(dist_ready, w + 1)
                nc.scalar.activation(ring1[:, KW * u + KW - 1, :], dist[:, u, :], ACT.Relu,
                                     bias=ones_f[:, 0:1], scale=-1.0).then_inc(onehot_act, 1)

            act.wait_ge(keys_ready, 1)
            act.wait_ge(fast.turned, START1 + FLD)
            for u in range(GWIN):
                last_block(u, u)
            with act.Fori(0, CH) as c:
                with act.Fori(0, CSTEP) as s:
                    w0 = (c * CSTEP + s) * GWIN
                    for u in range(GWIN):
                        act.wait_ge(fast.ring_used, GWIN + w0 + u + 1)
                        nc.scalar.activation(adj_chunk(c)[:, :, ds(s * (GWIN * WD) + u * WD, WD)],
                                             bank(u)[:, 0:HC].rearrange("p (b n) -> p b n", n=WD),
                                             ACT.Copy).then_inc(fast.win_kept, 1)
                        last_block(w0 + (GWIN + u), u)
                act.wait_ge(fast.sums_done, CSTEP + (c + 1) * CSTEP)
                act.wait_ge(fast.es_stored, START16 + 16 * c)
                nc.scalar.activation(es_out[0:12, :], bank(4)[0:12, 0:CW], ACT.Copy).then_inc(fast.sums_kept, 1)

            def high(dst_part, src_rows, scale):
                return nc.scalar.activation(dst_part, src_rows, ACT.Identity, scale=scale)

            for g in range(NG):
                act.wait_ge(grp_loaded[g % 2], 16 * (g // 2 + 1) + 16 * (g == NG - 1))
                v = rbuf[g % 2].rearrange("p (b f) -> p b f", f=F)
                for b in range(GB):
                    last = high(parts[:, 0, g * GB + b, :], v[:, b, :], scl[:, 0, g * GB + b:g * GB + b + 1])
                last.then_inc(parts_hi, 1)
                act.wait_ge(turned_grp, g + 1)
                act.wait_ge(hT_stored, 16 * g)
                nc.scalar.activation(xgrp[0], ptr[g % 2], ACT.Copy).then_inc(xT_done, 1)

            def lin_out(l, c):
                g = CH * l + c
                act.wait_ge(lin_done, START1 + g + 2)
                act.wait_ge(raw_stored, START16 + 16 * g)
                act.wait_ge(stats_done, START1 + g)
                settle(act)
                for h in range(2):
                    nc.scalar.activation(nraw[:, h, :], lin_h[h], ACT.Relu,
                                         bias=fcol[:, 0, ds(l, 1), h]).then_inc(lin_evac, 1)

            def turn_out(l, k):
                for m in range(TURNS):
                    n, slot = (l * (CH - 1) + k) * TURNS + m, m % 2
                    act.wait_ge(adj_turned, n + 1)
                    act.wait_ge(turn_stored[slot], START16 + 16 * ((l * (CH - 1) + k) * (TURNS // 2) + m // 2))
                    nc.scalar.activation(turn[slot][0:SW, :], turn_ps[slot], ACT.Copy).then_inc(adj_turned_out, 1)
                    act.wait_ge(adj_turned_out, 2 + n + 1)
                    if m < NG:
                        to = adjT_dram[ds((k + 1) * CW + l * SW, SW), m * GW:(m + 1) * GW]
                    else:
                        to = adjT_dram[ds(l * SW, SW), ds(k * (4 * P), GW)]
                    act.dma_start(to, turn[slot][0:SW, :]).then_inc(turn_stored[slot], 16)

            def chunks_out(l, turning):
                if turning:
                    act.wait_ge(parts_hi, NG * (l + 1))
                    act.wait_ge(parts_lo, NG * (l + 1))
                    act.wait_ge(hT_stored, 16 * NG * (l + 1))
                    settle(act)
                with act.Fori(0, CH - 1) as k:
                    if turning:
                        turn_out(l, k)
                    lin_out(l, k)
                lin_out(l, CH - 1)

            def normalize(l, g, func):
                k = g // 2 + 1
                act.wait_ge(grp_loaded[g % 2], 64 + 48 * l + 16 * k if g % 2 == 0 else 32 + 32 * l + 16 * k)
                v = rbuf[g % 2].rearrange("p (h n) -> p h n", h=2)
                for h in range(2):
                    last = nc.scalar.activation(v[:, h, :], v[:, h, :], func, bias=bnsc[:, 3, h:h + 1],
                                                scale=bnsc[:, 2, h:h + 1])
                last.then_inc(norm_done, 1)

            def turned_high(l, g):
                act.wait_ge(turned_grp, NG * (l + 1) + g + 1)
                for b in range(GB):
                    n = g * GB + b
                    last = high(parts[:, 0, n, :], ptr[g % 2][:, b * F:(b + 1) * F], scl[:, 0, n:n + 1])
                last.then_inc(parts_hi, 1)

            act.wait_ge(fcol_loaded, 48)
            def layer_out(l):
                chunks_out(l, True)
                act.wait_ge(var_ready, l + 1)
                nc.scalar.activation(bnsc[:, 1, :], bnsc[:, 0, :], ACT.Sqrt).then_inc(std_ready, 1)
                act.wait_ge(bn_ready, l + 1)
                for g in range(NG):
                    normalize(l, g, ACT.Relu)
                    if g >= 1:
                        turned_high(l, g - 1)
                turned_high(l, NG - 1)

            with act.Fori(0, LAYERS - 1) as l:
                layer_out(l)
            last_l = LAYERS - 1
            chunks_out(last_l, False)
            act.wait_ge(var_ready, LAYERS)
            nc.scalar.activation(bnsc[:, 1, :], bnsc[:, 0, :], ACT.Sqrt).then_inc(std_ready, 1)
            act.wait_ge(bn_ready, LAYERS)

            def ln_root(n, rows, nb):
                act.wait_ge(ln_var, n)
                nc.scalar.activation(ln_r[0:rows, 1, 0:nb], ln_r[0:rows, 0, 0:nb], ACT.Sqrt).then_inc(ln_std, 1)

            normalize(last_l, 0, ACT.Identity)
            for g in range(NG):
                if g + 1 < NG:
                    normalize(last_l, g + 1, ACT.Identity)
                ln_root(g + 1, P, GB)
                act.wait_ge(ln_rows, g + 1)
                for b in range(GB):
                    last = high(parts[:, 0, g * GB + b, :], xgrp[g % 2][:, b * F:(b + 1) * F], S_LN)
                last.then_inc(parts_hi, 1)

            ln_n = NG
            for ph in range(4):
                if ph:
                    for g in range(NG):
                        base_g = [64 + 48 * LAYERS + 48 * (ph - 1), 32 + 32 * LAYERS + 32 * (ph - 1)][g % 2]
                        act.wait_ge(grp_loaded[g % 2], base_g + 16 * (g // 2 + 1))
                        for b in range(GB):
                            n = g * GB + b
                            last = high(parts[:, 0, n, :], rbuf[g % 2][:, b * F:(b + 1) * F],
                                        scl[:, 1, n:n + 1] if ph < 3 else S_LN)
                        last.then_inc(parts_hi, 1)
                scale = 1.0 if ph in (1, 2) else 1.0 / S_LN

                def agg_out(c, ph=ph, scale=scale):
                    g = CH * (LAYERS + ph) + c
                    act.wait_ge(lin_done, START1 + g + 1)
                    for h in range(2):
                        act.wait_ge(spmm_done, START2 + 2 * g + h + 1)
                        nc.scalar.activation(agg[:, h, :], acc_of(c)[h], ACT.Copy, scale=scale).then_inc(agg_evac, 1)

                def acc_of(c):
                    return acc[acc_t[0]]

                acc_t = [0]
                if ph == 0:
                    act.wait_ge(x_stored, 16 * NG)
                agg_out(0)
                with act.Fori(0, CH // 2) as j:
                    for t in range(2):
                        acc_t[0] = 1 - t
                        agg_out(2 * j + t + 1)
                        if ph != 1:
                            ln_root(ln_n + 2 * j + t + 1, SW, SUBS)
                if ph != 1:
                    ln_root(ln_n + CH, SW, SUBS)
                    ln_n += CH

        @block.vector
        def _(dve):
            V = nc.vector
            link = Steps(dve, dve_step)
            for b in (fast, slow):
                dve.sem_inc(b.ring_used, GWIN)
                dve.sem_inc(b.win_kept, GWIN)
                dve.sem_inc(b.sums_kept, START1)
                dve.sem_inc(b.sums_done, CSTEP)
                dve.sem_inc(b.turned, START1)
            dve.sem_inc(fast.es_stored, START16)
            dve.sem_inc(es_free, START1)
            dve.sem_inc(hist_used, HB)
            dve.sem_inc(adj_turned_out, 2)
            dve.sem_inc(turn_even, START16)
            dve.sem_inc(turn_odd, START16)
            dve.sem_inc(sel_used, 2)
            dve.sem_inc(agg_evac, START2 + 2)
            dve.sem_inc(lin_done, START1 + 1)
            dve.sem_inc(spmm_done, START2)
            dve.sem_inc(lin_evac, START2)
            dve.sem_inc(raw_stored, START16)
            dve.sem_inc(stats_done, START1)
            V.memset(src_i, 0)
            V.memset(dst_i, 4095).then_inc(padded, 1)
            V.memset(att.rearrange("p e k -> p (e k)"), 0.0).then_inc(padded, 1)
            V.memset(ewt[:, :], 0.0)
            V.memset(sent.rearrange("p e k -> p (e k)"), 0.0)
            V.memset(ones_f, 1.0)
            V.memset(ones_h, 1.0)
            link(V.memset(zero_h, 0.0))
            V.memset(sent[:, :, 0], 4095.0)
            dve.wait_ge(consts_i, 2)
            V.tensor_copy(iot, iot_i)
            link(V.tensor_copy(pidx[:, :], pidx_i[:, :]))
            V.tensor_scalar(pidx_neg[:, :], pidx[:, :], -1.0, None, ALU.mult)
            V.tensor_scalar(ident[:, :], iot[:, 0:P], pidx[:, 0:1], None, ALU.is_equal)
            V.tensor_scalar(ident_h[:, :], iot[:, 0:P], pidx[:, 0:1], None, ALU.is_equal).then_inc(consts, 1)

            dve.wait_ge(edges_loaded, 16 * 4)
            V.tensor_scalar(slo_i, src_i, P - 1, None, ALU.bitwise_and)
            V.tensor_scalar(shi_i, src_i, 7, None, ALU.logical_shift_right)
            V.tensor_scalar(dlo_i, dst_i, P - 1, None, ALU.bitwise_and)
            link(V.tensor_scalar(dhi_i, dst_i, 7, None, ALU.logical_shift_right))
            V.tensor_copy(slo_h, slo_i).then_inc(fields_done, 1)
            V.tensor_copy(shi_h, shi_i)
            V.tensor_copy(dlo_f, dlo_i)
            link(V.tensor_copy(dhi_h, dhi_i))

            def hi_onehot(hi):
                return V.tensor_tensor(oh_hi, hi.unsqueeze(2).broadcast_to((P, EC, NB)),
                                       iot[:, 0:NB].unsqueeze(1).broadcast_to((P, EC, NB)), ALU.is_equal)

            link(hi_onehot(dhi_h))
            with dve.Fori(0, EC // (HB * EB)) as i:
                for t in range(HB):
                    dve.wait_ge(hist_used, HB * i + t + 1)
                    for k in range(EB):
                        last = V.tensor_scalar(hring[:, t * EB + k, :], iot[:, 0:P],
                                               dlo_f[:, ds(i * (HB * EB) + t * EB + k, 1)], None, ALU.is_equal)
                    last.then_inc(hist_ready, 1)

            dve.wait_ge(hist_used, HB + EC // EB + 1)
            deg = bank(6)[:, 0:NB]
            V.tensor_scalar(degs[:, 0, 0, :], deg, 1.0, None, ALU.max)
            V.tensor_scalar(degs[:, 0, 1, :], deg, 1.0, None, ALU.add)
            V.tensor_scalar(degs[:, 4, 0, :], deg, 1.0, None, ALU.min)
            link(V.memset(degs[:, 4, 1, :], 1.0))
            V.reciprocal(degs[:, 1, :, :], degs[:, 0, :, :]).then_inc(root_in, 1)
            V.scalar_tensor_tensor(tab[:, :, 0], src_i, 4096.0, dst_i, ALU.mult, ALU.add)
            dve.wait_ge(slo_loaded, 64)
            q = P * EC // 4
            for i in (2, 3):
                last = V.tensor_scalar(slo_bc[:, i * q:(i + 1) * q], slo_bc[:, i * q:(i + 1) * q], pidx[:, 0:1],
                                       None, ALU.is_equal)
            last.then_inc(onehot_t, 1)
            dve.wait_ge(root_out, 1)
            link(V.tensor_tensor(degs[:, 3, :, :], degs[:, 2, :, :], degs[:, 2, :, :], ALU.mult))
            link(V.tensor_tensor(degs[:, 3, :, :], degs[:, 3, :, :], degs[:, 0, :, :], ALU.mult))
            link(V.tensor_scalar(degs[:, 3, :, :], degs[:, 3, :, :], -0.5, 1.5, ALU.mult, ALU.add))
            link(V.tensor_tensor(degs[:, 3, :, :], degs[:, 3, :, :], degs[:, 2, :, :], ALU.mult))
            link(V.tensor_tensor(degs[:, 1, :, :], degs[:, 3, :, :], degs[:, 4, :, :], ALU.mult))
            V.tensor_scalar(degs[:, 5, :, :], degs[:, 1, :, :], 1.0 / S_BN, None, ALU.mult).then_inc(deg_done, 1)
            V.tensor_scalar(scl[:, :, :], degs[:, 1, :, :], S_BN, None, ALU.mult)
            link(V.tensor_scalar(degs[:, 2, 0, :], degs[:, 1, 0, :], S_TAB, None, ALU.mult))
            link(V.tensor_copy(dtab[:, 0, :], degs[:, 2, 0, :]))
            V.tensor_tensor(dtab[:, 1, :], degs[:, 2, 0, :], dtab[:, 0, :], ALU.subtract).then_inc(tab_ready, 1)

            link(hi_onehot(shi_h))
            n0 = link.n
            with dve.Fori(0, EC // (2 * SB)) as i:
                link.n = n0 + 4 * i
                for t in range(2):
                    e0 = i * (2 * SB) + t * SB
                    v = sel[t].rearrange("p (e b) -> p e b", b=NB)
                    dve.wait_ge(sel_ready, 2 * i + t + 1)
                    link(V.tensor_tensor(v, bank(6 + t)[:, 0:SB * NB].rearrange("p (e b) -> p e b", b=NB),
                                         oh_hi[:, ds(e0, SB), :], ALU.mult))
                    dve.sem_inc(sel_used, 1)
                    link(V.tensor_reduce(dinvs[:, ds(e0, SB)], v, AX.X, ALU.add))
            link.n = n0 + 4 * (EC // (2 * SB))
            link(V.tensor_scalar(dinvs, dinvs, S_BN / S_TAB, None, ALU.mult))
            dve.wait_ge(attr_loaded, 32)
            V.tensor_tensor(tab[:, :, 1:FLD], att, dinvs.unsqueeze(2).broadcast_to((P, EC, 4)), ALU.mult).then_inc(table_done, 1)

            link(V.tensor_scalar(dwl_i, dst_i.rearrange("p (g x) -> p g x", x=WD)[:, :, WD - 1], 4, None,
                                 ALU.logical_shift_right))
            link(V.tensor_copy(dwl_h, dwl_i))
            link(V.tensor_tensor(cmp_h, iot[:, 0:NW].unsqueeze(2).broadcast_to((P, NW, 26)),
                                 dwl_h.unsqueeze(1).broadcast_to((P, NW, 26)), ALU.is_gt))
            V.tensor_reduce(part, cmp_h, AX.X, ALU.add).then_inc(part_ready, 1)
            link(V.memset(starts[:, :, :], 0))
            dve.wait_ge(starts_ready, 1)
            V.tensor_copy(starts[:, 0, 0:1], bank(5)[:, 32:33])
            link(V.tensor_copy(starts[0:NWH[1], 1, 0:1], bank(5)[0:NWH[1], 33:34]))
            V.tensor_scalar(starts[:, :, 1], starts[:, :, 0], COPIES - 1, None, ALU.bitwise_and)
            link(V.tensor_scalar(starts[:, :, 2], starts[:, :, 0], 3, None, ALU.logical_shift_right))
            link(V.scalar_tensor_tensor(starts[:, :, 3], starts[:, :, 1], float(CPR), starts[:, :, 2], ALU.mult, ALU.add))
            for k in range(KW):
                last = V.tensor_scalar(idx[:, :].rearrange("p (h k) -> p h k", k=KW)[:, :, k], starts[:, :, 3],
                                       float(1 + k), None, ALU.add)
            last.then_inc(idx_ready, 1)

            def split(b, r, f):
                val = bank(2 * (f % 2), 2).rearrange("p (k w) -> p k w", w=2 * P)[:, 0:KW, 0:NW]
                v = [v3[:, :, 4 * a + f - 1].rearrange("p (k w) -> p k w", w=NW) for a in range(3)]
                q1, q2 = (x.rearrange("p (k w) -> p k w", w=NW) for x in (rest1, rest2))
                dve.wait_ge(b.turned, START1 + FLD * r + f + 1)
                link(V.tensor_copy(v[0], val))
                link(V.tensor_tensor(q1, val, v[0], ALU.subtract))
                dve.sem_inc(b.turned_used, 1)
                link(V.tensor_copy(v[1], q1))
                link(V.tensor_tensor(q2, q1, v[1], ALU.subtract))
                link(V.tensor_copy(v[2], q2))

            def fields(b, r):
                dve.wait_ge(b.turned, START1 + FLD * r + 1)
                k3 = [x.rearrange("p (k w) -> p k w", w=NW) for x in (key_i, fa_i, mask)]
                link(V.tensor_copy(k3[0], bank(0, 2).rearrange("p (k w) -> p k w", w=2 * P)[:, 0:KW, 0:NW]))
                dve.sem_inc(b.turned_used, 1)
                link(V.tensor_scalar(fa_i, key_i, 4, 255, ALU.logical_shift_right, ALU.bitwise_and))
                V.tensor_tensor(k3[2], k3[1], iot_i[:, 0:NW].unsqueeze(1).broadcast_to((P, KW, NW)), ALU.is_equal)
                link(V.tensor_scalar(fb_i, key_i, 19, None, ALU.logical_shift_right))
                link(V.tensor_scalar(fa_i, key_i, WD - 1, None, ALU.bitwise_and))
                V.scalar_tensor_tensor(key2, fb_i, float(WD), fa_i, ALU.mult, ALU.add)
                link(V.scalar_tensor_tensor(dlom, fa_i, 1.0, mask, ALU.add, ALU.mult))
                link(V.tensor_scalar(fb_i, key_i, 12, P - 1, ALU.logical_shift_right, ALU.bitwise_and))
                link(V.scalar_tensor_tensor(slom, fb_i, 1.0, mask, ALU.add, ALU.mult))

            def one_hots(b, r, w0, step, s):
                dve.wait_ge(b.sums_done, r * STEPS + step + 1)
                d4 = dlom.rearrange("p (k w) -> p k w", w=NW)[:, :, ds(w0, GWIN)]
                V.tensor_tensor(ringd[:, ds(s, 1), :, :, :].rearrange("p s k w c -> p (s k) w c"), d4.unsqueeze(3).broadcast_to((P, KW, GWIN, WD)),
                                iot[:, 1:WD + 1].unsqueeze(1).unsqueeze(1).broadcast_to((P, KW, GWIN, WD)), ALU.is_equal)
                for u in range(GWIN):
                    dve.wait_ge(b.ring_used, r * NW + w0 + u + 1)
                    for k in range(KW):
                        at = ds(w0 + (k * NW + u), 1)
                        if b is slow or k < KW - 1:
                            V.tensor_scalar(ring1[:, KW * u + k, :], iot[:, 1:P + 1], slom[:, at], None, ALU.is_equal)
                        last = V.tensor_scalar(ring2[:, KW * u + k, :], iot[:, 0:HC], key2[:, at], None, ALU.is_equal)
                    last.then_inc(b.ring_ready, 1)

            dve.wait_ge(zero_stored, 16 * 6)
            dve.wait_ge(table_stored, 16 * (2 * COPIES + 1))
            n0 = link.n
            fields(fast, 0)
            V.tensor_reduce(flag_f[:, 0:1], mask, AX.X, ALU.add).then_inc(captured, 1)
            dve.wait_ge(captured, 1)
            V.memset(slom_neg[:, NK:NK + GWIN], 0.0)
            link(V.tensor_scalar(slom_neg[:, 0:NK], slom, -1.0, None, ALU.mult))
            dve.sem_inc(keys_ready, 1)
            for f in range(1, FLD):
                split(fast, 0, f)
            round_steps = link.n - n0 - 1
            with dve.Fori(0, CH) as c:
                with dve.Fori(0, CSTEP) as s:
                    one_hots(fast, 0, (c * CSTEP + s) * GWIN, c * CSTEP + s, s)
            dve.wait_ge(cap_summed, 1)
            link(V.tensor_scalar(flag_f[:, 1:2], bank(7)[:, 0:1], float(E), None, ALU.is_equal))
            link(V.tensor_scalar(flag[:, :], flag_f[:, 1:2], -1.0, 1.0, ALU.mult, ALU.add))
            dve.sem_inc(flag_ready, 1)
            dve.wait_ge(fast.win_kept, GWIN + NW)
            general = dve.value_load(flag[0:1, 0:1], min_val=0, max_val=1)
            n0 = link.n
            with dve.If(general):
                dve.wait_ge(fast.es_stored, START16 + 16 * CH)
                dve.wait_ge(adj_stored, 16 * CH)
                link(V.memset(es_out, 0.0))
                dve.sem_inc(zeros_set, 1)
                for c in range(CH):
                    V.memset(adj[:, c * CF:(c + 1) * CF], 0.0)
                for h in range(2):
                    for k in range(KW):
                        last = V.memset(idx[:, KW * h + k:KW * h + k + 1], 1 + k - KW)
                link(last)
                n1 = link.n
                with dve.Fori(0, ROUNDS) as r:
                    link.n = n1 + r * (round_steps + 1)
                    dve.wait_ge(slow.turned, START1 + FLD * r)
                    link(V.tensor_scalar(idx[:, :], idx[:, :], float(KW), None, ALU.add))
                    dve.sem_inc(idx_ready, 1)
                    fields(slow, r)
                    for f in range(1, FLD):
                        split(slow, r, f)
                    settle(dve)
                    with dve.Fori(0, CH) as c:
                        with dve.Fori(0, CSTEP) as s:
                            step = c * CSTEP + s
                            one_hots(slow, r, step * GWIN, step, s)
                            for u in range(GWIN):
                                dve.wait_ge(slow.ring_used, r * NW + step * GWIN + (GWIN + u + 1))
                                v = adj_chunk(c)[:, :, ds(s * (GWIN * WD) + u * WD, WD)]
                                V.tensor_tensor(v, v, bank(u)[:, 0:HC].rearrange("p (b n) -> p b n", n=WD),
                                                ALU.add).then_inc(slow.win_kept, 1)
                        dve.wait_ge(slow.sums_done, CSTEP + r * STEPS + (c + 1) * CSTEP)
                        dve.wait_ge(es_free, START1 + r * CH + c)
                        V.tensor_copy(es_out[0:12, :], bank(4)[0:12, 0:CW]).then_inc(slow.sums_kept, 1)
                dve.wait_ge(slow.es_stored, 16 * CH * ROUNDS)
                dve.wait_ge(slow.win_kept, GWIN + NW * ROUNDS)
            with dve.Else():
                dve.nop()
            dve.sem_inc(built, 1)
            pad_link = Steps(dve, pad_step)

            def low(part_lo, rows, scale, part_hi):
                return V.scalar_tensor_tensor(part_lo, rows, scale, part_hi, ALU.mult, ALU.subtract)

            for g in range(NG):
                if g == NG - 1:
                    dve.wait_ge(turned_grp, g - 1)
                    dve.wait_ge(parts_hi, g - 1)
                    dve.wait_ge(parts_lo, g - 1)
                    pad_link(V.memset(rbuf[0][:, (GB - 1) * F:GB * F], 0.0))
                    dve.sem_inc(pad_set, 1)
                dve.wait_ge(parts_hi, g + 1)
                for b in range(GB):
                    n = g * GB + b
                    last = low(parts[:, 1, n, :], rbuf[g % 2][:, b * F:(b + 1) * F], scl[:, 0, n:n + 1], parts[:, 0, n, :])
                last.then_inc(parts_lo, 1)

            def agg_out(l, c, t):
                g = CH * l + c
                dve.wait_ge(bc_loaded, 16 * (g + 1))
                dve.wait_ge(lin_done, START1 + g + 1)
                for h in range(2):
                    dve.wait_ge(spmm_done, START2 + 2 * g + h + 1)
                    V.tensor_tensor(agg[:, h, :], acc[t][h], bc, ALU.mult).then_inc(agg_evac, 1)

            def chunk_stats(l, c, width):
                dve.wait_ge(lin_evac, START2 + 2 * (CH * l + c) + 2)
                for h in range(2):
                    last = V.bn_stats(stats[:, h, ds(c, 1), :].rearrange("p c s -> p (c s)"), nraw[:, h, 0:width])
                last.then_inc(stats_done, 1)

            def norm_factors(l, steps):
                for h in range(2):
                    last = V.bn_aggr(mv[:, h, :], stats[:, h, :, :].rearrange("p c s -> p (c s)"))
                steps(last)
                steps(V.tensor_scalar(bnsc[:, 0, :], mv[:, :, 1], EPS, None, ALU.add))
                steps(V.reciprocal(bnsc[:, 0, :], bnsc[:, 0, :]))
                dve.sem_inc(var_ready, 1)
                dve.wait_ge(std_ready, l + 1)
                g_l, b_l = (fcol[:, i, ds(l, 1), :].rearrange("p l h -> p (l h)") for i in (1, 2))
                steps(V.tensor_tensor(bnsc[:, 2, :], bnsc[:, 1, :], g_l, ALU.mult))
                steps(V.tensor_tensor(bnsc[:, 3, :], mv[:, :, 0], bnsc[:, 2, :], ALU.mult))
                steps(V.tensor_tensor(bnsc[:, 3, :], b_l, bnsc[:, 3, :], ALU.subtract))
                dve.sem_inc(bn_ready, 1)

            def row_sums(c):
                V.tensor_reduce(dop[:, ds(c, 1), :].rearrange("p c b -> p (c b)"), adj_chunk(c), AX.X, ALU.add).then_inc(dout_part, 1)

            def layer(l, degrees=False):
                agg_out(l, 0, 0)
                with dve.Fori(0, CH // 2) as j:
                    for t in range(2):
                        if degrees:
                            row_sums(2 * j + t)
                        agg_out(l, 2 * j + t + 1, 1 - t)
                        chunk_stats(l, 2 * j + t, CW)
                if degrees:
                    row_sums(CH - 1)
                chunk_stats(l, CH - 1, LASTW)
                dve.wait_ge(stats_done, START1 + CH * l + CH)
                settle(dve)
                norm_factors(l, link)

            dve.wait_ge(fcol_loaded, 48)
            link = Steps(dve, vec_step)

            def groups_low(l):
                for g in range(NG):
                    dve.wait_ge(parts_hi, NG * (l + 1) + g + 1)
                    for b in range(GB):
                        n = g * GB + b
                        last = low(parts[:, 1, n, :], ptr[g % 2][:, b * F:(b + 1) * F], scl[:, 0, n:n + 1], parts[:, 0, n, :])
                    last.then_inc(parts_lo, 1)

            layer(0, degrees=True)
            groups_low(0)
            dve.wait_ge(dout_part, CH)
            V.tensor_reduce(dop[:, CH, :], dop[:, 0:CH, :].rearrange("p c b -> p b c"), AX.X, ALU.add).then_inc(dout_ready, 1)
            per_layer = link.n
            with dve.Fori(1, LAYERS - 1) as l:
                link.n = per_layer * l
                layer(l)
                groups_low(l)
            link.n = per_layer * (LAYERS - 1)
            layer(LAYERS - 1)

            def layer_norm(v, rows, nb, n):
                for b in range(nb):
                    last = V.bn_stats(ln_st[0:rows, b, :], v[:, b, :])
                link(last)
                settle(dve)
                for b in range(nb):
                    last = V.bn_aggr(ln_mv[0:rows, b, :], ln_st[0:rows, b, :])
                link(last)
                link(V.tensor_scalar(ln_r[0:rows, 0, 0:nb], ln_mv[0:rows, 0:nb, 1], EPS, None, ALU.add))
                link(V.reciprocal(ln_r[0:rows, 0, 0:nb], ln_r[0:rows, 0, 0:nb]))
                dve.sem_inc(ln_var, 1)
                dve.wait_ge(ln_std, n)
                for b in range(nb):
                    last = V.tensor_scalar(v[:, b, :], v[:, b, :], ln_mv[0:rows, b, 0:1], ln_r[0:rows, 1, b:b + 1],
                                           ALU.subtract, ALU.mult)
                link(last)

            for g in range(NG):
                xg = xgrp[g % 2].rearrange("p (b f) -> p b f", f=F)
                if g == NG - 1:
                    dve.wait_ge(x_stored, 16 * (g - 1))
                    link(V.memset(xg[:, GB - 1, :], 0.0))
                    dve.sem_inc(pad_set, 1)
                dve.wait_ge(turned_grp, NG * LAYERS + g + 1)
                dve.wait_ge(x_loaded[g % 2], 16 * (g // 2 + 1) + 16 * (g == NG - 1))
                link(V.tensor_tensor(xgrp[g % 2], ptr[g % 2], xgrp[g % 2], ALU.add))
                layer_norm(xg, P, GB, g + 1)
                dve.sem_inc(ln_rows, 1)
                dve.wait_ge(parts_hi, NG * LAYERS + g + 1)
                for b in range(GB):
                    n = g * GB + b
                    last = low(parts[:, 1, n, :], xg[:, b, :], S_LN, parts[:, 0, n, :])
                link(last)
                dve.sem_inc(parts_lo, 1)
                dve.sem_inc(y_ready, 1)

            dve.wait_ge(rows_loaded, 32)
            link(V.tensor_scalar(nrow[:, 1, :], nrow[:, 2, :], 1.0, None, ALU.min))
            link(V.tensor_scalar(nrow[:, 0, :], nrow[:, 2, :], 1.0, None, ALU.max))
            link(V.reciprocal(nrow[:, 0, :], nrow[:, 0, :]))
            link(V.tensor_tensor(nrow[:, 0, :], nrow[:, 0, :], nrow[:, 1, :], ALU.mult))

            ln_n = NG
            for ph in range(4):
                if ph:
                    for g in range(NG):
                        dve.wait_ge(parts_hi, NG * (LAYERS + ph) + g + 1)
                        for b in range(GB):
                            n = g * GB + b
                            last = low(parts[:, 1, n, :], rbuf[g % 2][:, b * F:(b + 1) * F],
                                       scl[:, 1, n:n + 1] if ph < 3 else S_LN, parts[:, 0, n, :])
                        last.then_inc(parts_lo, 1)
                dve.wait_ge(bias_loaded, 32 * (ph + 1))
                if ph == 3:
                    dve.wait_ge(wt_done, 1)
                    link(V.tensor_copy(wd.rearrange("p h n -> p (h n)"), bank(6)))
                    dve.sem_inc(wt_kept, 1)
                row_bias = bias[0:SW, :]

                def rows_out(c, t, j, ph=ph):
                    g = CH * (LAYERS + ph) + c
                    k = [4, 3][t] * ph + j + 1
                    v = rbuf[t][0:SW, 0:SUBS * F].rearrange("p (s f) -> p s f", f=F)
                    dve.wait_ge(xr_loaded[t], 16 * k)
                    col = lambda i, s: nrow[:, i, ds(c * SUBS + s, 1)]
                    if ph in (0, 3):
                        for s in range(SUBS):
                            last = V.scalar_tensor_tensor(v[:, s, :], row_bias, col(1 if ph == 0 else 2, s), v[:, s, :], ALU.mult, ALU.add)
                        link(last)
                    dve.wait_ge(lin_done, START1 + g + 2)
                    for s in range(SUBS):
                        if ph == 0:
                            last = V.scalar_tensor_tensor(v[:, s, :], lin_s[0:SW, s, :], col(0, s), v[:, s, :], ALU.mult, ALU.add)
                        elif ph == 3:
                            last = V.tensor_tensor(v[:, s, :], lin_s[0:SW, s, :], v[:, s, :], ALU.add)
                        else:
                            last = V.scalar_tensor_tensor(tmp[0:SW, s, :], lin_s[0:SW, s, :], col(3, s), row_bias, ALU.mult, ALU.add)
                    link(last)
                    dve.sem_inc(lin_evac, 2)
                    if ph in (1, 2):
                        link(V.scalar_tensor_tensor(v, tmp[0:SW, :, :], 0.0, v, ALU.max, ALU.add))
                    if ph == 2:
                        dve.wait_ge(xr2_loaded, 16 * (c + 1))
                        link(V.tensor_tensor(v, v, xr2[0:SW, :, :], ALU.add))
                    if ph != 1:
                        layer_norm(v, SW, SUBS, ln_n + c + 1)
                    dve.sem_inc(y_ready, 1)

                per = [2 + 5, 2, 3 + 5, 2 + 5][ph]
                n0 = link.n
                with dve.Fori(0, CH // 2) as j:
                    for t in range(2):
                        link.n = n0 + per * (2 * j + t)
                        rows_out(2 * j + t, t, j)
                link.n = n0 + per * (CH - 1)
                rows_out(CH - 1, 0, CH // 2)
                assert link.n == n0 + per * CH
                if ph != 1:
                    ln_n += CH

        @block.tensor
        def _(pe):
            T = nc.tensor
            pe.wait_ge(consts, 1)
            deg = bank(6)[:, 0:NB]
            T.matmul(deg, zero_h, zero_h[:, 0:NB], start=True, stop=False)
            with pe.Fori(0, EC // (HB * EB)) as i:
                for t in range(HB):
                    pe.wait_ge(hist_ready, HB * i + t + 1)
                    for k in range(EB):
                        last = T.matmul(deg, hring[:, t * EB + k, :],
                                        oh_hi[:, ds(i * (HB * EB) + t * EB + k, 1), :].rearrange("p e b -> p (e b)"),
                                        start=False, stop=False)
                    last.then_inc(hist_used, 1)
            T.matmul(deg, zero_h, zero_h[:, 0:NB], start=False, stop=True).then_inc(hist_used, 1)
            pe.wait_ge(onehot_t, 2)
            pe.wait_ge(tab_ready, 1)
            cols = slo_bc.rearrange("q (p e) -> q p e", e=EC)
            with pe.Fori(0, EC // (2 * SB)) as i:
                for t in range(2):
                    pe.wait_ge(sel_used, 2 * i + t + 1)
                    for k in range(SB):
                        for a in range(2):
                            last = T.matmul(bank(6 + t)[:, NB * k:NB * (k + 1)],
                                            cols[:, :, ds(i * (2 * SB) + t * SB + k, 1)].rearrange("q p e -> q (p e)"),
                                            dtab[:, a, :], start=(a == 0), stop=(a == 1))
                    last.then_inc(sel_ready, 1)
            pe.wait_ge(part_ready, 1)
            T.matmul(bank(5)[:, 32:33], part[:, 0:P], ones_f[:, 0:1], start=True, stop=True)
            T.matmul(bank(5)[0:NWH[1], 33:34], part[:, P:NW], ones_f[:, 0:1], start=True, stop=True).then_inc(starts_ready, 1)

            def turn_fields(b, r):
                pe.wait_ge(b.gathered, 16 * 2 * KW * (r + 1))
                pe.wait_ge(b.win_kept, GWIN + NW * r)
                for f in range(FLD):
                    if f >= 2:
                        pe.wait_ge(b.turned_used, FLD * r + f - 1)
                    to = bank(2 * (f % 2), 2).rearrange("p (k w) -> p k w", w=2 * P)
                    for k in range(KW):
                        for h in range(2):
                            rows = win[h][0:NWH[h], k * ROWE:(k + 1) * ROWE].rearrange("w (e f) -> w e f", f=FLD)[:, :, f]
                            last = T.transpose(to[:, k, h * P:h * P + NWH[h]], rows, ident[0:NWH[h], 0:NWH[h]])
                    last.then_inc(b.turned, 1)

            def windows(b, r):
                with pe.Fori(0, CH) as c:
                    pe.wait_ge(b.sums_kept, START1 + r * CH + c)
                    settle(pe)
                    for s in range(CSTEP):
                        w0 = c * (CSTEP * GWIN) + s * GWIN
                        for u in range(GWIN):
                            pe.wait_ge(b.ring_ready, r * NW + w0 + u + 1)
                            if b is fast:
                                pe.wait_ge(onehot_act, w0 + u + 1)
                            pe.wait_ge(b.win_kept, r * NW + w0 + u + 1)
                            for k in range(KW):
                                last = T.matmul(bank(u)[:, 0:HC], ring1[:, KW * u + k, :], ring2[:, KW * u + k, :],
                                                start=(k == 0), stop=(k == KW - 1))
                            last.then_inc(b.ring_used, 1)
                        for u in range(GWIN):
                            for k in range(KW):
                                last = T.matmul(bank(4)[0:12, (s * GWIN + u) * WD:(s * GWIN + u + 1) * WD],
                                                v3[:, ds(w0 + (k * NW + u), 1), :].rearrange("p e c -> p (e c)"),
                                                ringd[:, s, k, u, :],
                                                start=(k == 0), stop=(k == KW - 1))
                        last.then_inc(b.sums_done, 1)

            turn_fields(fast, 0)
            pe.wait_ge(captured, 1)
            T.matmul(bank(7)[:, 0:1], ones_f, flag_f[:, 0:1], start=True, stop=True).then_inc(cap_summed, 1)
            windows(fast, 0)
            pe.wait_ge(flag_ready, 1)
            general = pe.value_load(flag[0:1, 0:1], min_val=0, max_val=1)
            with pe.If(general):
                with pe.Fori(0, ROUNDS) as r:
                    turn_fields(slow, r)
                    windows(slow, r)
            with pe.Else():
                pe.nop()

            def turn_input(g):
                pe.wait_ge(grp_loaded[g % 2], 16 * (g // 2 + 1) + 16 * (g == NG - 1))
                if g >= 2:
                    pe.wait_ge(xT_done, g - 1)
                for b in range(GB):
                    for h in range(2):
                        last = T.transpose(ptr[g % 2][:, h * GW + b * P:h * GW + (b + 1) * P],
                                           rbuf[g % 2][:, b * F + h * P:b * F + (h + 1) * P], ident[:, :])
                last.then_inc(turned_grp, 1)

            def turn_output(l, g):
                pe.wait_ge(norm_done, NG * l + g + 1)
                v = rbuf[g % 2].rearrange("p (h n) -> p h n", h=2)
                for b in range(GB):
                    for h in range(2):
                        last = T.transpose(ptr[g % 2][:, b * F + h * P:b * F + (h + 1) * P],
                                           v[:, h, b * P:(b + 1) * P], ident[:, :])
                last.then_inc(turned_grp, 1)

            def turn_batch(l, k, m):
                pe.wait_ge(adj_turned_out, (l * (CH - 1) + k) * TURNS + m + 1)
                for i in range(GB):
                    if m < NG:
                        rows = adj_chunk(k + 1)[:, m * GB + i, ds(l * SW, SW)]
                    else:
                        rows = adj_chunk(0)[:, ds(k * 4 + i, 1), ds(l * SW, SW)].rearrange("p b n -> p (b n)")
                    last = T.transpose(turn_ps[m % 2][:, i * P:(i + 1) * P], rows, ident_h[:, :])
                last.then_inc(adj_turned, 1)

            def blocks(c, t, bs, edges):
                for b in bs:
                    for a in range(2):
                        for h in range(2):
                            ends = not edges and b == NB - 1 and a == 1
                            last = T.matmul(acc[t][h], parts[:, a, b, h * P:(h + 1) * P], adj_chunk(c)[:, b, :],
                                            start=(b == 0 and a == 0), stop=ends)
                            if ends:
                                last.then_inc(spmm_done, 1)

            def edge_term(g, t):
                pe.wait_ge(es_loaded, 16 * (g + 1))
                for h in range(2):
                    T.matmul(acc[t][h], ewt[:, h * P:(h + 1) * P], es[0:12, :], start=False,
                             stop=True).then_inc(spmm_done, 1)

            def product(g, c, t, edges, turn_l=None):
                pe.wait_ge(agg_evac, START2 + 2 * g)
                for m in range(NG):
                    blocks(c, t, range(m * GB, (m + 1) * GB), edges)
                    if turn_l is not None:
                        turn_batch(turn_l, c - 1, m)
                if turn_l is not None:
                    turn_batch(turn_l, c - 1, NG)
                if edges:
                    edge_term(g, t)

            def first_product(g, k0, layer=None, turn_group=None):
                edges = layer is not None
                pe.wait_ge(agg_evac, START2 + 2 * g)
                if turn_group:
                    turn_group(0)
                    turn_group(1)
                for k in range(NG):
                    pe.wait_ge(parts_hi, k0 + k + 1)
                    pe.wait_ge(parts_lo, k0 + k + 1)
                    blocks(0, 0, range(k * GB, (k + 1) * GB), edges)
                    if turn_group and k + 2 < NG:
                        turn_group(k + 2)
                if turn_group is turn_input:
                    pe.wait_ge(xT_done, NG)
                if edges:
                    pe.wait_ge(w_loaded, 16 * 7 * (layer + 1))
                    edge_term(g, 0)

            def linear(l, c, t, j):
                g = CH * l + c
                pe.wait_ge(hT_loaded[t], 16 * ([4, 3][t] * l + j + 1))
                pe.wait_ge(agg_evac, START2 + 2 * g + 4)
                pe.wait_ge(lin_evac, START2 + 2 * g)
                hc = rbuf[t][:, 0:2 * CW].rearrange("p (h n) -> p h n", h=2)
                for h in range(2):
                    for k in range(4):
                        last = T.matmul(lin_h[h], wl[:, k, h * P:(h + 1) * P], hc[:, k, :] if k < 2 else agg[:, k - 2, :],
                                        start=(k == 0), stop=(k == 3))
                last.then_inc(lin_done, 1)

            def layer(l, turning, turn_group):
                turn_l = l if turning else None
                first_product(CH * l, NG * l, l, turn_group)
                with pe.Fori(0, CH // 2) as j:
                    for t in range(2):
                        product(CH * l + 2 * j + t + 1, 2 * j + t + 1, 1 - t, True, turn_l)
                        linear(l, 2 * j + t, t, j)
                linear(l, CH - 1, 0, CH // 2)

            pe.wait_ge(built, 1)
            layer(0, True, turn_input)
            with pe.Fori(1, LAYERS - 1) as l:
                layer(l, True, lambda g: turn_output(l - 1, g))
            layer(LAYERS - 1, False, lambda g: turn_output(LAYERS - 2, g))

            for ph in range(4):
                base = CH * (LAYERS + ph)
                if ph == 3:
                    pe.wait_ge(bias_loaded, 32 * 4)
                    for k in range(2):
                        for h in range(2):
                            last = T.transpose(bank(6)[:, h * F + k * P:h * F + (k + 1) * P],
                                               wt[:, k, h * P:(h + 1) * P], ident[:, :])
                    last.then_inc(wt_done, 1)

                def operator_ready(c, ph=ph):
                    if ph == 0:
                        pe.wait_ge(op_loaded, 16 * (c + 1))
                    elif ph == 1:
                        pe.wait_ge(eye_added, c + 1)
                    elif ph == 3:
                        pe.wait_ge(op_loaded, 16 * (2 * CH + c + 1))

                def chunk_product(c, t, base=base):
                    operator_ready(c)
                    product(base + c, c, t, False)

                def chunk_linear(c, base=base):
                    g = base + c
                    pe.wait_ge(agg_evac, START2 + 2 * g + 4)
                    pe.wait_ge(lin_evac, START2 + 2 * g)
                    for s in range(SUBS):
                        for h in range(2):
                            last = T.matmul(lin_s[0:SW, s, :], agg[:, h, s * SW:(s + 1) * SW], wd[:, h, :],
                                            start=(h == 0), stop=(h == 1))
                    last.then_inc(lin_done, 1)

                operator_ready(0)
                first_product(base, NG * (LAYERS + ph),
                              turn_group=(lambda g: turn_output(LAYERS - 1, g)) if ph == 0 else None)
                if ph == 3:
                    pe.wait_ge(wt_kept, 1)
                else:
                    pe.wait_ge(bias_loaded, 32 * (ph + 1))
                with pe.Fori(0, CH // 2) as j:
                    for t in range(2):
                        chunk_product(2 * j + t + 1, 1 - t)
                        chunk_linear(2 * j + t)
                chunk_linear(CH - 1)


def kernel(**inputs):
    import numpy as np
    import concourse.bacc as bacc
    from concourse.bass_utils import run_bass_kernel_spmd

    nc = bacc.Bacc("TRN2", target_bir_lowering=False, num_devices=1)
    arrays, args = {}, []
    for name in INPUTS:
        a = np.ascontiguousarray(inputs[name])
        arrays[f"in_{name}"] = a
        args.append(nc.dram_tensor(f"in_{name}", a.shape, mybir.dt.from_np(a.dtype), kind="ExternalInput").ap())
    args.append(nc.dram_tensor("out", (N, F), mybir.dt.float32, kind="ExternalOutput").ap())
    build(nc, *args)
    r = run_bass_kernel_spmd(nc, [arrays], core_ids=[0])
    return r.results[0]["out"]
```

```python
import concourse.bass as bass
from concourse import mybir
from contextlib import ExitStack

P = 128
N = 3125
F = 256
E = 53125
LAYERS = 5
EPS = 1e-5

NB = -(-N // P)
NR = NB * P
TAIL = N - (NB - 1) * P
CH = 7
CW = 448
NPAD = CH * CW
LASTW = N - (CH - 1) * CW
SUBS = 4
SW = CW // SUBS
GB = 5
NG = NB // GB
GW = GB * P
GSLOT = [1, 1, 1, 0, 1]
CF = NB * CW

EC = -(-E // P)
ELAST = E - (P - 1) * EC
EB = 8
HB = 4
SB = 16
HALF1 = 7
EH = 2 * SB * HALF1
WD = 16
NW = NPAD // WD
NWH = [P, NW - P]
KW = 3
NK = KW * NW
COPIES = 8
FLD = 5
ROWE = P * FLD
CPR = 1 + EC + 4
GAP = CPR * P - EC * P - WD
ROUNDS = -(-E // (KW * P))
TURNS = NG + 1
GWIN = 4
CSTEP = CW // (WD * GWIN)
STEPS = CH * CSTEP
HC = NB * WD

START1, START2, START16 = 1, 2, 16

S_BN = 256.0
S_LN = 2048.0
S_H = 64.0
S_W = 1024.0
S_TAB = 4096.0

INPUTS = ["x", "src", "dst", "edge_attr_4", "L0_gnn_mlp_w", "L0_gnn_mlp_b", "L0_gnn_ew1", "L0_gnn_ew2",
          "L0_gnn_bn_g", "L0_gnn_bn_b", "L1_gnn_W", "L1_gnn_b", "L2_gnn_W1", "L2_gnn_b1", "L2_gnn_W2",
          "L2_gnn_b2", "L3_gnn_W", "L3_gnn_b"]


class Steps:

    def __init__(self, eng, sem):
        self.eng, self.sem, self.n = eng, sem, 0

    def __call__(self, ins):
        ins.then_inc(self.sem, 1)
        self.n = self.n + 1
        self.eng.wait_ge(self.sem, self.n)


def build(nc, x, src, dst, attr, mlp_w, mlp_b, ew1, ew2, bn_g, bn_b, w_1, b_1, w_21, b_21, w_22, b_22,
          w_3, b_3, out):
    f32, f16, bf16, i32 = mybir.dt.float32, mybir.dt.float16, mybir.dt.bfloat16, mybir.dt.int32
    ALU = mybir.AluOpType
    ACT = mybir.ActivationFunctionType
    AX = mybir.AxisListType
    ds = bass.ds

    def flat(ap, offset, dims):
        return bass.AP(ap.tensor, offset, dims)

    ctx = ExitStack()
    with ctx:
        def sb(name, shape, dt):
            return ctx.enter_context(nc.sbuf_tensor(name, shape, dt))

        def sem(name):
            return ctx.enter_context(nc.semaphore(name))

        def dram(name, shape, dt):
            return nc.dram_tensor(name, shape, dt).ap()

        slo_row = dram("slo_row", (P, EC), f16)
        table = dram("edge_table", (COPIES * CPR, ROWE), f32)
        adj_dram = dram("adj_dram", (NR, NR), f16)
        adjT_dram = dram("adjT_dram", (NR, NR), f16)
        dinv_row = dram("dinv_row", (NR,), f32)
        dinv2_row = dram("dinv2_row", (NR,), f32)
        dout_row = dram("dout_row", (NR,), f32)
        edge_sum = dram("edge_sum", (12, NPAD), f32)
        hT = dram("hT", (4, P, NR), f16)
        rawT = dram("rawT", (2, P, NR), f32)
        xs = [dram(f"x{i}", (NR, F), f32) for i in range(1, 5)]

        adj = sb("adj", [P, CH * CF], f16)
        work = sb("work", [P, 12672], f32)
        adj32 = adj[:, :].bitcast(f32)

        def cut(base, at, n, dt=f32):
            v = base[:, at:at + n]
            return v if dt == f32 else v.bitcast(dt)

        slo_bc = cut(adj32, 0, 26624, f16)
        oh_hi = cut(adj32, 26624, 5200, f16).rearrange("p (e b) -> p e b", b=NB)
        src_i = cut(adj32, 31824, EC, i32)
        dst_i = cut(adj32, 32240, EC, i32)
        dlo_i = cut(adj32, 32656, EC, i32)
        dhi_i = cut(adj32, 33072, EC, i32)
        slo_i = cut(adj32, 33488, EC, i32)
        shi_i = cut(adj32, 33904, EC, i32)
        dlo_f = cut(adj32, 34320, EC)
        dhi_h = cut(adj32, 34736, EC // 2, f16)
        slo_h = cut(adj32, 34944, EC // 2, f16)
        shi_h = cut(adj32, 35152, EC // 2, f16)
        cmp_h = cut(adj32, 35360, NW * 26 // 2, f16).rearrange("p (w g) -> p w g", g=26)
        degs = cut(adj32, 37908, 600).rearrange("p (i t b) -> p i t b", t=2, b=NB)
        att = cut(work, 0, 4 * EC).rearrange("p (e k) -> p e k", k=4)
        tab = cut(work, 1664, FLD * EC).rearrange("p (e k) -> p e k", k=FLD)
        sent = cut(work, 3744, GAP * FLD).rearrange("p (e k) -> p e k", k=FLD)
        hring = cut(work, 6864, HB * EB * P // 2, f16).rearrange("p (s c) -> p s c", c=P)
        sel = [cut(work, 7888 + SB * NB * i, SB * NB) for i in range(2)]
        dinvs = cut(work, 8688, EC)
        part = cut(work, 9104, NW)
        dwl_i = cut(work, 9300, 26, i32)
        dwl_h = cut(work, 9326, 13, f16)
        zeros = cut(work, 9340, 800)
        win = [cut(work, 0, KW * ROWE), cut(work, 1920, KW * ROWE)]
        ring1 = cut(work, 0, 768, f16).rearrange("p (s c) -> p s c", c=P)
        ring2 = cut(work, 768, 2400, f16).rearrange("p (s c) -> p s c", c=HC)
        ringd = cut(work, 3168, CSTEP * 96, bf16).rearrange("p (s k w c) -> p s k w c", s=CSTEP, k=KW, c=WD)
        key_i = cut(work, 3840, NK, i32)
        fa_i = cut(work, 4428, NK, i32)
        fb_i = cut(work, 5016, NK, i32)
        mask = cut(work, 5604, NK)
        slom = cut(work, 6192, NK)
        key2 = cut(work, 6780, NK)
        dlom = cut(work, 7368, NK)
        v3 = cut(work, 7956, 6 * NK, bf16).rearrange("p (e c) -> p e c", c=12)
        es_out = cut(work, 5016, CW)
        rest1 = cut(work, 3840, NK)
        rest2 = cut(work, 4428, NK)
        iot_i = cut(work, 11484, HC, i32)
        iot = cut(work, 11884, HC // 2, f16)
        ones_f = cut(work, 12084, P)
        ones_h = cut(work, 12212, 64, f16)
        zero_h = cut(work, 12276, 64, f16)
        dist = cut(work, 12340, GWIN * P // 2, f16).rearrange("p (u c) -> p u c", c=P)
        slom_neg = cut(work, 5600, NK + GWIN)
        parts = cut(work, 0, 6400, f16).rearrange("p (t b f) -> p t b f", t=2, f=F)
        rbuf = [cut(work, 6400 + 1280 * i, 1280) for i in range(2)]
        agg_p = cut(work, 8960, 2 * CW, f16).rearrange("p (a h n) -> p a h n", a=2, n=CW)
        nraw = cut(work, 9856, 2 * CW).rearrange("p (h n) -> p h n", h=2)
        wl = cut(work, 10752, 4 * F, f16).rearrange("p (a k n) -> p a k n", a=2, n=F)
        w_raw = cut(work, 10240, 2 * F)
        hcut = [cut(work, at, 2 * GW, f16).rearrange("p (a h n) -> p a h n", a=2, n=GW) for at in (8960, 10752)]
        bc = cut(work, 11776, CW)
        es = cut(work, 12224, CW)
        turn = [cut(work, 6400 + 1280 * i + 2 * CW, GW // 2, f16) for i in range(2)]
        xgrp = [cut(work, 8960, GB * F), cut(work, 10752, GB * F)]
        agg = cut(work, 8960, 2 * CW).rearrange("p (h n) -> p h n", h=2)
        wd = cut(work, 9856, 2 * F).rearrange("p (h n) -> p h n", h=2)
        bias = cut(work, 10368, F)
        xr2 = cut(work, 10624, SUBS * F).rearrange("p (s f) -> p s f", f=F)
        tmp = cut(work, 11648, SUBS * F).rearrange("p (s f) -> p s f", f=F)
        wt = cut(work, 10624, 2 * F).rearrange("p (h n) -> p h n", h=2)

        pidx = sb("pidx", [P, 1], f32)
        pidx_neg = sb("pidx_neg", [P, 1], f32)
        pidx_i = sb("pidx_i", [P, 1], i32)
        ident = sb("ident", [P, P], f32)
        ident_h = sb("ident_h", [P, P], f16)
        dtab = sb("dtab", [P, 2, NB], f16)
        scl = sb("scl", [P, 2, NB], f32)
        idx = sb("idx", [P, 2 * KW], i32)
        starts = sb("starts", [P, 2, 4], i32)
        flag_f = sb("flag_f", [P, 2], f32)
        flag = sb("flag", [P, 1], i32)
        dop = sb("dop", [P, CH + 1, NB], f32)
        fcol = sb("fcol", [P, 3, LAYERS, 2], f32)
        ewt = sb("ewt", [12, F], f32)
        stats = sb("stats", [P, 2, CH, 6], f32)
        mv = sb("mv", [P, 2, 2], f32)
        bnsc = sb("bnsc", [P, 4, 2], f32)
        nrow = sb("nrow", [SW, 4, CH * SUBS], f32)
        ln_st = sb("ln_st", [P, GB, 6], f32)
        ln_mv = sb("ln_mv", [P, GB, 2], f32)
        ln_r = sb("ln_r", [P, 2, GB], f32)

        ps = ctx.enter_context(nc.psum_tensor("ps", [P, 8 * 512], f32))

        def bank(i, n=1):
            return ps[:, 512 * i:512 * (i + n)]

        acc = [[bank(2 * t + h)[:, 0:CW] for h in range(2)] for t in range(2)]
        lin = bank(4, 2)
        lin_h = [bank(4)[:, 0:CW], bank(5)[:, 0:CW]]
        lin_s = lin.rearrange("p (s f) -> p s f", f=F)
        turn_ps = [bank(6 + t)[0:SW, 0:GW // 2].bitcast(f16) for t in range(2)]
        ptr = [bank(2 + 3 * t, 3)[:, 0:GB * F] for t in range(2)]

        def adj_chunk(c):
            return adj[:, ds(c * CF, CF)].rearrange("p (b n) -> p b n", n=CW)

        (consts_i, consts, zeros_set, padded, attr_loaded, act_step, dist_ready, onehot_act, keys_ready,
         table_step, zero_stored, edges_loaded, fields_done, slo_stored, slo_loaded,
         hist_ready, hist_used, deg_done, root_in, root_out, onehot_t, tab_ready, sel_ready, sel_used,
         table_done, table_stored, part_ready, starts_ready, idx_ready, rows_stored,
         built, flag_ready, captured, cap_summed, adj_stored, adj_restored, dout_part, dout_ready, dout_stored,
         rows_loaded, dve_step, es_zeroed, vec_step, pad_step, settled, es_free, adj_turned, adj_turned_out, turn_even, turn_odd) = [sem(n) for n in (
             "consts_i consts zeros_set padded attr_loaded act_step dist_ready onehot_act keys_ready "
             "table_step zero_stored edges_loaded fields_done slo_stored slo_loaded "
             "hist_ready hist_used deg_done root_in root_out onehot_t tab_ready sel_ready sel_used "
             "table_done table_stored part_ready starts_ready idx_ready rows_stored "
             "built flag_ready captured cap_summed adj_stored adj_restored dout_part dout_ready dout_stored "
             "rows_loaded dve_step es_zeroed vec_step pad_step settled es_free adj_turned adj_turned_out turn_even turn_odd").split()]

        def settle(eng):
            eng.sem_inc(settled, 1)

        class Build:

            def __init__(self, way):
                self.gathered = sem(f"gathered_{way}")
                self.turned = sem(f"turned_{way}")
                self.turned_used = sem(f"turned_used_{way}")
                self.ring_ready = sem(f"ring_ready_{way}")
                self.ring_used = sem(f"ring_used_{way}")
                self.sums_done = sem(f"sums_done_{way}")
                self.win_kept = sem(f"win_kept_{way}")
                self.sums_kept = sem(f"sums_kept_{way}")
                self.es_stored = sem(f"es_stored_{way}")

        fast, slow = Build("fast"), Build("slow")

        (parts_hi, parts_lo, agg_evac, spmm_done, lin_done, lin_evac, hT_even, hT_odd,
         w_loaded, ew_loaded, w_high, w_low, h_high, agg_scaled, agg_high, bc_loaded,
         es_loaded, raw_stored, stats_done, var_ready, std_ready, bn_ready, grp_even, grp_odd, norm_done,
         turned_grp, in_even, in_odd, xT_done, fcol_loaded, x_even, x_odd, op_loaded, eye_added, y_ready, x_stored,
         wt_done, wt_kept, bias_loaded, xr_even, xr_odd, xr2_loaded, ln_var, ln_std, pad_set, ln_rows) = [sem(n) for n in (
             "parts_hi parts_lo agg_evac spmm_done lin_done lin_evac hT_even hT_odd "
             "w_loaded ew_loaded w_high w_low h_high agg_scaled agg_high bc_loaded "
             "es_loaded raw_stored stats_done var_ready std_ready bn_ready grp_even grp_odd norm_done "
             "turned_grp in_even in_odd xT_done fcol_loaded x_even x_odd op_loaded eye_added y_ready x_stored "
             "wt_done wt_kept bias_loaded xr_even xr_odd xr2_loaded ln_var ln_std pad_set ln_rows").split()]
        hT_stored = [in_even, in_odd]

        def input_stored(eng, layers):
            eng.wait_ge(in_even, 16 * 3 * layers)
            settle(eng)
            eng.wait_ge(in_odd, 16 * 2 * layers)

        turn_stored, x_loaded = [turn_even, turn_odd], [x_even, x_odd]
        hT_loaded, grp_loaded, xr_loaded = [hT_even, hT_odd], [grp_even, grp_odd], [xr_even, xr_odd]

        block = ctx.enter_context(nc.Block())

        @block.gpsimd
        def _(pool):
            nc.gpsimd.iota(iot_i, pattern=[[1, HC]], base=0, channel_multiplier=0).then_inc(consts_i, 1)
            nc.gpsimd.iota(pidx_i[:, :], pattern=[[0, 1]], base=0, channel_multiplier=1).then_inc(consts_i, 1)
            nc.gpsimd.memset(zeros, 0.0).then_inc(zeros_set, 1)

            def gather(b, base):
                for h in range(2):
                    for k in range(KW):
                        nc.gpsimd.indirect_dma_start(
                            win[h][0:NWH[h], k * ROWE:(k + 1) * ROWE], None, table,
                            bass.IndirectOffsetOnAxis(ap=idx[0:NWH[h], h * KW + k:h * KW + k + 1], axis=0),
                        ).then_inc(b.gathered, 16)

            pool.wait_ge(idx_ready, 1)
            pool.wait_ge(table_stored, 16 * (3 * COPIES + 1))
            gather(fast, 0)

            pool.wait_ge(flag_ready, 1)
            general = pool.value_load(flag[0:1, 0:1], min_val=0, max_val=1)
            with pool.If(general):
                pool.wait_ge(es_zeroed, 16 * CH)
                with pool.Fori(0, ROUNDS) as r:
                    pool.wait_ge(idx_ready, r + 2)
                    settle(pool)
                    gather(slow, r)
                    with pool.Fori(0, CH) as c:
                        pool.wait_ge(slow.sums_kept, START1 + (r * CH + c + 1))
                        pool.dma_start(edge_sum[:, ds(c * CW, CW)], es_out[0:12, :],
                                       accum_op=ALU.add).then_inc(slow.es_stored, 16)
                        pool.wait_ge(slow.es_stored, 16 * (r * CH + c + 1))
                        pool.sem_inc(es_free, 1)
            with pool.Else():
                pool.nop()

            def eye(c, b, at, p0, w):
                v = adj_chunk(c)[:, ds(b, 1), at:at + w].rearrange("p b n -> p (b n)")
                return nc.gpsimd.tensor_tensor(v, v, ident_h[:, p0:p0 + w], ALU.add)

            def eyes(c, j, t):
                if t == 0:
                    at = [(0, 0, P), (P, 0, P), (2 * P, 0, P), (3 * P, 0, CW - 3 * P)]
                    bs = [7 * j, 7 * j + 1, 7 * j + 2, 7 * j + 3]
                else:
                    at = [(0, 64, 64), (64, 0, P), (192, 0, P), (320, 0, P)]
                    bs = [7 * j + 3, 7 * j + 4, 7 * j + 5, 7 * j + 6]
                pool.wait_ge(op_loaded, 16 * (CH + c + 1))
                for b, (a, p0, w) in zip(bs, at):
                    last = eye(c, b, a, p0, w)
                last.then_inc(eye_added, 1)

            with pool.Fori(0, CH // 2) as j:
                for t in range(2):
                    eyes(2 * j + t, j, t)
            eyes(CH - 1, CH // 2, 0)

        @block.sync
        def _(sp):
            sp.wait_ge(padded, 1)
            full = (P - 1) * EC
            sp.dma_start(src_i[0:P - 1, :], src[0:full].rearrange("(p e) -> p e", e=EC)).then_inc(edges_loaded, 16)
            sp.dma_start(dst_i[0:P - 1, :], dst[0:full].rearrange("(p e) -> p e", e=EC)).then_inc(edges_loaded, 16)
            sp.dma_start(src_i[P - 1:P, 0:ELAST], src[full:E].rearrange("(p e) -> p e", p=1)).then_inc(edges_loaded, 16)
            sp.dma_start(dst_i[P - 1:P, 0:ELAST], dst[full:E].rearrange("(p e) -> p e", p=1)).then_inc(edges_loaded, 16)
            sp.wait_ge(padded, 2)
            sp.dma_start(att[0:P - 1, :, :], attr[0:full, :].rearrange("(p e) k -> p e k", e=EC)).then_inc(attr_loaded, 16)
            sp.dma_start(att[P - 1:P, 0:ELAST, :], attr[full:E, :].rearrange("(p e) k -> p e k", p=1)).then_inc(attr_loaded, 16)
            sp.wait_ge(zeros_set, 1)
            sp.wait_ge(fields_done, 1)
            sp.dma_start(slo_row, slo_h).then_inc(slo_stored, 16)
            sp.wait_ge(slo_stored, 16)
            q = P * EC // 4
            for i in range(4):
                sp.dma_start(slo_bc[:, i * q:(i + 1) * q], flat(slo_row, i * q, [[0, P], [1, q]])).then_inc(slo_loaded, 16)
            zh = zeros.bitcast(f16).rearrange("p (b n) -> p b n", b=NB)
            zf = zeros[:, 0:F]
            sp.dma_start(adj_dram[:, NPAD:NR].rearrange("(b p) n -> p b n", p=P), zh[:, :, 0:NR - NPAD]).then_inc(zero_stored, 16)
            sp.dma_start(rawT[:, :, NPAD:NR].rearrange("h p n -> p h n"),
                         zf[:, 0:128].rearrange("p (h n) -> p h n", h=2)).then_inc(zero_stored, 16)
            sp.dma_start(adjT_dram[NPAD:NR, :].rearrange("r (x c) -> (r x) c", x=2),
                         zeros.bitcast(f16)).then_inc(zero_stored, 16)
            for t in xs[1:]:
                sp.dma_start(t[NPAD:NR, :], zf[0:NR - NPAD, :]).then_inc(zero_stored, 16)
            sp.dma_start(fcol[:, 0, :, :], mlp_b.rearrange("l (h p) -> p (l h)", p=P), allow_slow_non_contiguous=True).then_inc(fcol_loaded, 16)
            sp.dma_start(fcol[:, 1, :, :], bn_g.rearrange("l (h p) -> p (l h)", p=P), allow_slow_non_contiguous=True).then_inc(fcol_loaded, 16)
            sp.dma_start(fcol[:, 2, :, :], bn_b.rearrange("l (h p) -> p (l h)", p=P), allow_slow_non_contiguous=True).then_inc(fcol_loaded, 16)
            sp.wait_ge(deg_done, 1)
            for t, row in enumerate((dinv_row, dinv2_row)):
                sp.dma_start(row.rearrange("(b p) -> p b", p=P), degs[:, 5, t, :], allow_slow_non_contiguous=True).then_inc(rows_stored, 16)
            sp.dma_start(table[0:1, :], sent[0:1, 0:P, :].rearrange("p e k -> p (e k)")).then_inc(table_stored, 16)
            for j in range(COPIES):
                at = (j * CPR * P + P - WD * j + P * EC) * FLD
                sp.dma_start(flat(table, at, [[GAP * FLD, 1], [1, GAP * FLD]]),
                             sent[0:1, :, :].rearrange("p e k -> p (e k)")).then_inc(table_stored, 16)
            for half, (lo, hi) in enumerate(((0, EH), (EH, EC))):
                sp.wait_ge(table_done, half + 1)
                for j in range(COPIES):
                    at = (j * CPR * P + P - WD * j + lo) * FLD
                    sp.dma_start(flat(table, at, [[EC * FLD, P], [1, (hi - lo) * FLD]]),
                                 tab[:, lo:hi, :].rearrange("p e k -> p (e k)")).then_inc(table_stored, 16)
            def store_adj(c, done):
                sp.dma_start(adj_dram[:, c * CW:(c + 1) * CW].rearrange("(b p) n -> p b n", p=P),
                             adj_chunk(c)).then_inc(done, 16)

            for c in range(CH):
                sp.wait_ge(fast.sums_kept, START1 + c + 1)
                sp.dma_start(edge_sum[:, c * CW:(c + 1) * CW], es_out[0:12, :]).then_inc(fast.es_stored, 16)
                if c < CH - 1:
                    sp.wait_ge(fast.win_kept, GWIN + (c + 1) * CSTEP * GWIN)
                    store_adj(c, adj_stored)
            sp.wait_ge(flag_ready, 1)
            general = sp.value_load(flag[0:1, 0:1], min_val=0, max_val=1)
            with sp.If(general):
                sp.wait_ge(fast.es_stored, START16 + 16 * CH)
                sp.wait_ge(zeros_set, 2)
                for c in range(CH):
                    sp.dma_start(edge_sum[:, c * CW:(c + 1) * CW], es_out[0:12, :]).then_inc(es_zeroed, 16)
                sp.wait_ge(built, 1)
                sp.wait_ge(adj_stored, 16 * (CH - 1))
                for c in range(CH - 1):
                    store_adj(c, adj_restored)
                sp.wait_ge(adj_restored, 16 * (CH - 1))
            with sp.Else():
                sp.nop()

            sp.wait_ge(built, 1)
            sp.wait_ge(fast.es_stored, START16 + 16 * CH)
            sp.wait_ge(rows_stored, 32)
            sp.wait_ge(zero_stored, 16 * 6)

            def store_input(g):
                sp.dma_start(hT[:, :, g * GW:(g + 1) * GW].rearrange("h p n -> p h n"),
                             hcut[g % 2].rearrange("p a h n -> p (a h) n")).then_inc(hT_stored[g % 2], 16)

            def load_half(l, i):
                sp.dma_start(w_raw.rearrange("p (k n) -> p k n", k=2),
                             mlp_w[ds(l, 1), i * F:(i + 1) * F, :].rearrange("l (k p) n -> p (l k) n", p=P)).then_inc(w_loaded, 16)

            def load_weights(l):
                sp.wait_ge(lin_done, START1 + CH * l + 1)
                settle(sp)
                sp.wait_ge(stats_done, START1 + CH * l)
                for i in range(3):
                    sp.dma_start(ewt[4 * i:4 * i + 3, P:F], ew2[ds(l, 1), :, :].rearrange("l k n -> (l k) n")).then_inc(ew_loaded, 16)
                    sp.dma_start(ewt[4 * i + 3:4 * i + 4, 0:P], ew1[ds(l, 1), :, :].rearrange("l k n -> (l k) n")).then_inc(ew_loaded, 16)
                load_half(l, 0)

            for g in range(NG):
                if g >= 2:
                    sp.wait_ge(turned_grp, g - 1)
                    sp.wait_ge(parts_hi, g - 1)
                    sp.wait_ge(parts_lo, g - 1)
                v = rbuf[g % 2].rearrange("p (b f) -> p b f", f=F)
                if g < NG - 1:
                    sp.dma_start(v, x[g * GW:(g + 1) * GW, :].rearrange("(b p) f -> p b f", p=P)).then_inc(grp_loaded[g % 2], 16)
                else:
                    sp.wait_ge(pad_set, 1)
                    sp.dma_start(v[:, 0:GB - 1, :], x[g * GW:(NB - 1) * P, :].rearrange("(b p) f -> p b f", p=P)).then_inc(grp_loaded[0], 16)
                    sp.dma_start(v[0:TAIL, GB - 1, :], x[(NB - 1) * P:N, :]).then_inc(grp_loaded[0], 16)
                if g == 1:
                    store_adj(CH - 1, adj_stored)
                    load_weights(0)
                if g >= 1:
                    sp.wait_ge(xT_done, g)
                    store_input(g - 1)
            sp.wait_ge(xT_done, NG)
            store_input(NG - 1)

            LAST = LAYERS - 1

            sp.wait_ge(adj_stored, 16 * CH)

            def store_raw(g, c):
                sp.wait_ge(lin_evac, START2 + 2 * g + 2)
                sp.dma_start(rawT[:, :, ds(c * CW, CW)].rearrange("h p n -> p h n"), nraw).then_inc(raw_stored, 16)

            def load_reverse(c):
                if c:
                    sp.wait_ge(op_loaded, 16 * c)
                sp.dma_start(adj_chunk(c), adjT_dram[:, ds(c * CW, CW)].rearrange("(b p) n -> p b n", p=P)).then_inc(op_loaded, 16)

            def chunk(l, c, t, j, first):
                g = CH * l + c
                sp.wait_ge(agg_evac, START2 + 2 * g + 2)
                sp.dma_start(bc, flat(dinv_row, c * CW, [[0, P], [1, CW]])).then_inc(bc_loaded, 16)
                sp.wait_ge(spmm_done, START2 + 2 * g)
                sp.dma_start(es[0:12, :], edge_sum[:, ds(c * CW, CW)]).then_inc(es_loaded, 16)
                sp.wait_ge(lin_done, START1 + g)
                settle(sp)
                sp.dma_start(rbuf[t][:, 0:2 * CW].bitcast(f16).rearrange("p (h n) -> p h n", n=CW),
                             hT[:, :, ds(c * CW, CW)].rearrange("h p n -> p h n")).then_inc(hT_loaded[t], 16)
                if not first:
                    store_raw(g - 1, c - 1)
                    if l is LAST and c >= 2:
                        load_reverse(c - 2)

            def load_raw_group(l, g):
                if g >= 2:
                    sp.wait_ge(turned_grp, NG * (l + 1) + g - 1)
                    if l is not LAST:
                        settle(sp)
                        sp.wait_ge(xT_done, NG * (l + 1) + g - 1)
                sp.dma_start(rbuf[g % 2].rearrange("p (h n) -> p h n", h=2),
                             rawT[:, :, g * GW:(g + 1) * GW].rearrange("h p n -> p h n")).then_inc(grp_loaded[g % 2], 16)

            def products(l):
                input_stored(sp, l + 1)
                settle(sp)
                sp.wait_ge(parts_lo, NG * (l + 1))
                sp.wait_ge(parts_hi, NG * (l + 1))
                chunk(l, 0, 0, 0, True)
                sp.wait_ge(w_high, 2 * l + 1)
                settle(sp)
                sp.wait_ge(w_low, 2 * l + 1)
                load_half(l, 1)
                if l is LAST:
                    for c in range(1, CH):
                        chunk(l, c, c % 2, c // 2, False)
                else:
                    with sp.Fori(0, CH // 2) as j:
                        chunk(l, 2 * j + 1, 1, j, False)
                        chunk(l, 2 * j + 2, 0, j + 1, False)
                sp.wait_ge(raw_stored, START16 + 16 * (CH * l + CH - 1))
                if l is not LAST:
                    for t in range(2):
                        settle(sp)
                        sp.wait_ge(turn_stored[t], START16 + 16 * (CH - 1) * (TURNS // 2) * (l + 1))
                for t in (1, 0):
                    settle(sp)
                    sp.wait_ge(lin_done, START1 + CH * l + (CH + 1 - t))
                    load_raw_group(l, t)
                store_raw(CH * l + CH - 1, CH - 1)
                sp.wait_ge(raw_stored, START16 + 16 * CH * (l + 1))

            with sp.Fori(0, LAYERS - 1) as l:
                products(l)
                load_weights(l + 1)
                for g in range(NG):
                    if g + 2 < NG:
                        load_raw_group(l, g + 2)
                    sp.wait_ge(xT_done, NG * (l + 1) + g + 1)
                    store_input(g)
            sp.wait_ge(dout_ready, 1)
            sp.dma_start(dout_row.rearrange("(b p) -> p b", p=P), dop[:, CH, :], allow_slow_non_contiguous=True).then_inc(dout_stored, 16)
            sp.wait_ge(dout_stored, 16)
            sp.dma_start(nrow[:, 2, :], dout_row[0:NPAD].rearrange("(s p) -> p s", p=SW), allow_slow_non_contiguous=True).then_inc(rows_loaded, 16)
            sp.dma_start(nrow[:, 3, :], dinv2_row[0:NPAD].rearrange("(s p) -> p s", p=SW), allow_slow_non_contiguous=True).then_inc(rows_loaded, 16)
            products(LAST)

            sp.wait_ge(stats_done, START1 + CH * LAYERS)
            def load_x_group(g):
                v = xgrp[g % 2].rearrange("p (b f) -> p b f", f=F)
                if g < NG - 1:
                    sp.dma_start(v, x[g * GW:(g + 1) * GW, :].rearrange("(b p) f -> p b f", p=P)).then_inc(x_loaded[g % 2], 16)
                else:
                    sp.wait_ge(pad_set, 2)
                    sp.dma_start(v[:, 0:GB - 1, :], x[g * GW:(NB - 1) * P, :].rearrange("(b p) f -> p b f", p=P)).then_inc(x_loaded[g % 2], 16)
                    sp.dma_start(v[0:TAIL, GB - 1, :], x[(NB - 1) * P:N, :]).then_inc(x_loaded[g % 2], 16)

            for g in range(2):
                load_x_group(g)
            for g in range(NG):
                if g + 2 < NG:
                    load_raw_group(LAST, g + 2)
                sp.wait_ge(ln_rows, g + 1)
                sp.dma_start(xs[0][g * GW:(g + 1) * GW, :].rearrange("(b p) f -> p b f", p=P),
                             xgrp[g % 2].rearrange("p (b f) -> p b f", f=F)).then_inc(x_stored, 16)
                sp.wait_ge(x_stored, 16 * (g + 1))
                if g + 2 < NG:
                    sp.wait_ge(parts_hi, NG * LAYERS + g + 1)
                    sp.wait_ge(parts_lo, NG * LAYERS + g + 1)
                    load_x_group(g + 2)

            def load_rows(ph, g):
                sp.dma_start(rbuf[GSLOT[g]].rearrange("p (b f) -> p b f", f=F),
                             xs[ph][g * GW:(g + 1) * GW, :].rearrange("(b p) f -> p b f", p=P)).then_inc(grp_loaded[GSLOT[g]], 16)

            def rows_cut(ph, g):
                sp.wait_ge(parts_hi, NG * (LAYERS + ph) + g + 1)
                sp.wait_ge(parts_lo, NG * (LAYERS + ph) + g + 1)

            def load_operator(ph, c):
                sp.wait_ge(spmm_done, START2 + 2 * (CH * (LAYERS + ph) + c) + 2)
                op = adj_dram if ph == 0 else adjT_dram
                sp.dma_start(adj_chunk(c), op[:, ds(c * CW, CW)].rearrange("(b p) n -> p b n", p=P)).then_inc(op_loaded, 16)
                sp.wait_ge(op_loaded, 16 * (CH * (1 if ph == 0 else 2) + c + 1))
                settle(sp)

            for ph, (w, b) in enumerate(((w_1, b_1), (w_21, b_21), (w_22, b_22), (w_3, b_3))):
                base = CH * (LAYERS + ph)
                if ph:
                    sp.wait_ge(x_stored, 16 * (NG + CH * ph))
                    load_rows(ph, 3)
                    rows_cut(ph, 2)
                    load_rows(ph, 4)
                else:
                    rows_cut(ph, NG - 1)
                sp.wait_ge(lin_done, START1 + base + 1)
                if ph:
                    sp.wait_ge(y_ready, CH * ph)
                sp.dma_start(wt if ph == 3 else wd, w.rearrange("(h p) n -> p h n", p=P)).then_inc(bias_loaded, 16)
                sp.dma_start(bias[0:SW, :], flat(b, 0, [[0, SW], [1, F]])).then_inc(bias_loaded, 16)
                rows_cut(ph, NG - 1)

                def load_x(c, t, ph=ph):
                    sp.dma_start(rbuf[t][0:SW, 0:SUBS * F].rearrange("p (s f) -> p s f", f=F),
                                 xs[ph][ds(c * CW, CW), :].rearrange("(s p) f -> p s f", p=SW)).then_inc(xr_loaded[t], 16)

                def store_y(c, t, ph=ph, base=base):
                    sp.wait_ge(y_ready, CH * ph + c + 1)
                    v = rbuf[t][0:SW, 0:SUBS * F].rearrange("p (s f) -> p s f", f=F)
                    if ph < 3:
                        sp.dma_start(xs[ph + 1][ds(c * CW, CW), :].rearrange("(s p) f -> p s f", p=SW), v).then_inc(x_stored, 16)
                    elif isinstance(c, int) and c == CH - 1:
                        at = c * CW + (SUBS - 1) * SW
                        sp.dma_start(out[c * CW:at, :].rearrange("(s p) f -> p s f", p=SW), v[:, 0:SUBS - 1, :]).then_inc(x_stored, 16)
                        sp.dma_start(out[at:N, :], v[0:N - at, SUBS - 1, :]).then_inc(x_stored, 16)
                    else:
                        sp.dma_start(out[ds(c * CW, CW), :].rearrange("(s p) f -> p s f", p=SW), v).then_inc(x_stored, 16)

                def dense(c, t, first, ph=ph, base=base):
                    if ph == 2:
                        sp.wait_ge(y_ready, CH * ph + c)
                        sp.dma_start(xr2[0:SW, :, :], xs[1][ds(c * CW, CW), :].rearrange("(s p) f -> p s f", p=SW)).then_inc(xr2_loaded, 16)
                    if not first:
                        store_y(c - 1, 1 - t)
                        sp.wait_ge(x_stored, 16 * (NG + CH * ph) + 16 * c)
                    if not (isinstance(c, int) and c == CH - 1):
                        load_x(c + 1, 1 - t)
                    if ph in (0, 2) and not (isinstance(c, int) and c == CH - 1):
                        load_operator(ph, c)

                load_x(0, 0)
                if ph == 0:
                    for c in (CH - 2, CH - 1):
                        load_reverse(c)
                if ph in (1, 3):
                    load_operator(ph - 1, CH - 1)
                dense(0, 0, True)
                with sp.Fori(0, CH // 2 - 1) as j:
                    dense(2 * j + 1, 1, False)
                    dense(2 * j + 2, 0, False)
                dense(CH - 2, 1, False)
                dense(CH - 1, 0, False)
                if ph < 3:
                    load_rows(ph + 1, 0)
                    rows_cut(ph + 1, 0)
                    load_rows(ph + 1, 1)
                store_y(CH - 1, 0)
                if ph < 3:
                    rows_cut(ph + 1, 1)
                    load_rows(ph + 1, 2)
            sp.wait_ge(x_stored, 16 * (NG + 4 * CH + 1))

        @block.scalar
        def _(act):
            act.wait_ge(consts, 1)
            act.wait_ge(slo_loaded, 64)
            q = P * EC // 4
            quarters = [slo_bc[:, i * q:(i + 1) * q] for i in range(2)]
            for v in quarters:
                nc.scalar.activation(v, v, ACT.Abs, bias=pidx_neg[:, 0:1]).then_inc(act_step, 1)
            for i, v in enumerate(quarters):
                act.wait_ge(act_step, i + 1)
                last = nc.scalar.activation(v, v, ACT.Relu, bias=ones_f[:, 0:1], scale=-1.0)
            last.then_inc(onehot_t, 1)

            act.wait_ge(root_in, 1)
            nc.scalar.activation(degs[:, 2, :, :], degs[:, 1, :, :], ACT.Sqrt).then_inc(root_out, 1)

            def last_block(w, u):
                nc.scalar.activation(dist[:, u, :], iot[:, 1:P + 1], ACT.Abs,
                                     bias=slom_neg[:, ds(w + (KW - 1) * NW, 1)]).then_inc(dist_ready, 1)
                act.wait_ge(dist_ready, w + 1)
                nc.scalar.activation(ring1[:, KW * u + KW - 1, :], dist[:, u, :], ACT.Relu,
                                     bias=ones_f[:, 0:1], scale=-1.0).then_inc(onehot_act, 1)

            act.wait_ge(keys_ready, 1)
            act.wait_ge(fast.turned, START1 + FLD)
            for u in range(GWIN):
                last_block(u, u)
            with act.Fori(0, CH) as c:
                with act.Fori(0, CSTEP) as s:
                    w0 = (c * CSTEP + s) * GWIN
                    for u in range(GWIN):
                        act.wait_ge(fast.ring_used, GWIN + w0 + u + 1)
                        nc.scalar.activation(adj_chunk(c)[:, :, ds(s * (GWIN * WD) + u * WD, WD)],
                                             bank(u)[:, 0:HC].rearrange("p (b n) -> p b n", n=WD),
                                             ACT.Copy).then_inc(fast.win_kept, 1)
                        last_block(w0 + (GWIN + u), u)
                act.wait_ge(fast.sums_done, CSTEP + (c + 1) * CSTEP)
                act.wait_ge(fast.es_stored, START16 + 16 * c)
                nc.scalar.activation(es_out[0:12, :], bank(4)[0:12, 0:CW], ACT.Copy).then_inc(fast.sums_kept, 1)

            def high(dst_part, src_rows, scale):
                return nc.scalar.activation(dst_part, src_rows, ACT.Identity, scale=scale)

            for g in range(NG):
                act.wait_ge(grp_loaded[g % 2], 16 * (g // 2 + 1) + 16 * (g == NG - 1))
                v = rbuf[g % 2].rearrange("p (b f) -> p b f", f=F)
                for b in range(GB):
                    last = high(parts[:, 0, g * GB + b, :], v[:, b, :], scl[:, 0, g * GB + b:g * GB + b + 1])
                last.then_inc(parts_hi, 1)
                act.wait_ge(turned_grp, g + 1)
                if g >= 2:
                    act.wait_ge(hT_stored[g % 2], 16 * (g // 2))
                nc.scalar.activation(hcut[g % 2][:, 0, :, :].rearrange("p h n -> p (h n)"), ptr[g % 2], ACT.Copy,
                                     scale=S_H).then_inc(h_high, 1)

            def weights_high(l):
                for i in range(2):
                    act.wait_ge(w_loaded, 16 * (2 * l + i + 1))
                    settle(act)
                    nc.scalar.activation(wl[:, 0, 2 * i:2 * i + 2, :].rearrange("p k n -> p (k n)"), w_raw, ACT.Copy,
                                         scale=S_W).then_inc(w_high, 1)

            def agg_high_out(l, c, t):
                g = CH * l + c
                act.wait_ge(lin_done, START1 + g + 1)
                for h in range(2):
                    act.wait_ge(agg_scaled, 2 * g + h + 1)
                    settle(act)
                    nc.scalar.activation(agg_p[:, 0, h, :], acc[t][h], ACT.Copy, scale=S_H).then_inc(agg_high, 1)

            def lin_out(l, c):
                g = CH * l + c
                act.wait_ge(lin_done, START1 + g + 2)
                act.wait_ge(raw_stored, START16 + 16 * g)
                act.wait_ge(stats_done, START1 + g)
                settle(act)
                for h in range(2):
                    nc.scalar.activation(nraw[:, h, :], lin_h[h], ACT.Relu,
                                         bias=fcol[:, 0, ds(l, 1), h], scale=1.0 / (S_H * S_W)).then_inc(lin_evac, 1)

            def turn_out(l, k):
                for m in range(TURNS):
                    n, slot = (l * (CH - 1) + k) * TURNS + m, m % 2
                    act.wait_ge(adj_turned, n + 1)
                    act.wait_ge(turn_stored[slot], START16 + 16 * ((l * (CH - 1) + k) * (TURNS // 2) + m // 2))
                    nc.scalar.activation(turn[slot][0:SW, :], turn_ps[slot], ACT.Copy).then_inc(adj_turned_out, 1)
                    act.wait_ge(adj_turned_out, 2 + n + 1)
                    if m < NG:
                        to = adjT_dram[ds((k + 1) * CW + l * SW, SW), m * GW:(m + 1) * GW]
                    else:
                        to = adjT_dram[ds(l * SW, SW), ds(k * (4 * P), GW)]
                    act.dma_start(to, turn[slot][0:SW, :]).then_inc(turn_stored[slot], 16)

            def chunks_out(l, turning):
                if turning:
                    act.wait_ge(parts_hi, NG * (l + 1))
                    act.wait_ge(parts_lo, NG * (l + 1))
                    input_stored(act, l + 1)
                    settle(act)
                if not turning:
                    input_stored(act, l + 1)
                weights_high(l)
                agg_high_out(l, 0, 0)
                with act.Fori(0, CH // 2) as j:
                    for t in range(2):
                        if turning:
                            turn_out(l, 2 * j + t)
                        lin_out(l, 2 * j + t)
                        agg_high_out(l, 2 * j + t + 1, 1 - t)
                lin_out(l, CH - 1)

            def normalize(l, g, func):
                k = g // 2 + 1
                act.wait_ge(grp_loaded[g % 2], 64 + 48 * l + 16 * k if g % 2 == 0 else 32 + 32 * l + 16 * k)
                v = rbuf[g % 2].rearrange("p (h n) -> p h n", h=2)
                for h in range(2):
                    last = nc.scalar.activation(v[:, h, :], v[:, h, :], func, bias=bnsc[:, 3, h:h + 1],
                                                scale=bnsc[:, 2, h:h + 1])
                last.then_inc(norm_done, 1)

            def turned_high(l, g):
                act.wait_ge(turned_grp, NG * (l + 1) + g + 1)
                for b in range(GB):
                    n = g * GB + b
                    last = high(parts[:, 0, n, :], ptr[g % 2][:, b * F:(b + 1) * F], scl[:, 0, n:n + 1])
                last.then_inc(parts_hi, 1)

            act.wait_ge(fcol_loaded, 48)
            def layer_out(l):
                chunks_out(l, True)
                act.wait_ge(var_ready, l + 1)
                nc.scalar.activation(bnsc[:, 1, :], bnsc[:, 0, :], ACT.Sqrt).then_inc(std_ready, 1)
                act.wait_ge(bn_ready, l + 1)
                for g in range(NG):
                    normalize(l, g, ACT.Relu)
                    if g >= 1:
                        turned_high(l, g - 1)
                    act.wait_ge(norm_done, NG * l + g + 1)
                    if g == 0:
                        settle(act)
                        act.wait_ge(raw_stored, START16 + 16 * CH * (l + 1))
                        settle(act)
                        act.wait_ge(stats_done, START1 + CH * (l + 1))
                    if g >= 2:
                        act.wait_ge(hT_stored[g % 2], 16 * ([3, 2][g % 2] * (l + 1) + g // 2))
                    settle(act)
                    nc.scalar.activation(hcut[g % 2][:, 0, :, :].rearrange("p h n -> p (h n)"), rbuf[g % 2], ACT.Copy,
                                         scale=S_H).then_inc(h_high, 1)
                turned_high(l, NG - 1)

            with act.Fori(0, LAYERS - 1) as l:
                layer_out(l)
            last_l = LAYERS - 1
            chunks_out(last_l, False)
            act.wait_ge(var_ready, LAYERS)
            nc.scalar.activation(bnsc[:, 1, :], bnsc[:, 0, :], ACT.Sqrt).then_inc(std_ready, 1)
            act.wait_ge(bn_ready, LAYERS)

            def ln_root(n, rows, nb):
                act.wait_ge(ln_var, n)
                nc.scalar.activation(ln_r[0:rows, 1, 0:nb], ln_r[0:rows, 0, 0:nb], ACT.Sqrt).then_inc(ln_std, 1)

            normalize(last_l, 0, ACT.Identity)
            for g in range(NG):
                if g + 1 < NG:
                    normalize(last_l, g + 1, ACT.Identity)
                ln_root(g + 1, P, GB)
                act.wait_ge(ln_rows, g + 1)
                for b in range(GB):
                    last = high(parts[:, 0, g * GB + b, :], xgrp[g % 2][:, b * F:(b + 1) * F], S_LN)
                last.then_inc(parts_hi, 1)

            def rows_high(ph, g):
                t = GSLOT[g]
                n = [64 + 48 * LAYERS + 16 * (ph - 1), 32 + 32 * LAYERS + 64 * (ph - 1)][t]
                act.wait_ge(grp_loaded[t], n + 16 * GSLOT[0:g + 1].count(t))
                for b in range(GB):
                    n = g * GB + b
                    last = high(parts[:, 0, n, :], rbuf[t][:, b * F:(b + 1) * F],
                                scl[:, 1, n:n + 1] if ph < 3 else S_LN)
                last.then_inc(parts_hi, 1)

            ln_n = NG
            for ph in range(4):
                if ph:
                    for g in range(1, NG):
                        rows_high(ph, g)
                scale = 1.0 if ph in (1, 2) else 1.0 / S_LN

                def agg_out(c, ph=ph, scale=scale):
                    g = CH * (LAYERS + ph) + c
                    act.wait_ge(lin_done, START1 + g + 1)
                    for h in range(2):
                        act.wait_ge(spmm_done, START2 + 2 * g + h + 1)
                        nc.scalar.activation(agg[:, h, :], acc_of(c)[h], ACT.Copy, scale=scale).then_inc(agg_evac, 1)

                def acc_of(c):
                    return acc[acc_t[0]]

                acc_t = [0]
                if ph == 0:
                    act.wait_ge(x_stored, 16 * NG)
                agg_out(0)
                with act.Fori(0, CH // 2) as j:
                    for t in range(2):
                        acc_t[0] = 1 - t
                        agg_out(2 * j + t + 1)
                        if ph != 1:
                            ln_root(ln_n + 2 * j + t + 1, SW, SUBS)
                if ph < 3:
                    rows_high(ph + 1, 0)
                if ph != 1:
                    ln_root(ln_n + CH, SW, SUBS)
                    ln_n += CH

        @block.vector
        def _(dve):
            V = nc.vector
            link = Steps(dve, dve_step)
            for b in (fast, slow):
                dve.sem_inc(b.ring_used, GWIN)
                dve.sem_inc(b.win_kept, GWIN)
                dve.sem_inc(b.sums_kept, START1)
                dve.sem_inc(b.sums_done, CSTEP)
                dve.sem_inc(b.turned, START1)
            dve.sem_inc(fast.es_stored, START16)
            dve.sem_inc(es_free, START1)
            dve.sem_inc(hist_used, HB)
            dve.sem_inc(adj_turned_out, 2)
            dve.sem_inc(turn_even, START16)
            dve.sem_inc(turn_odd, START16)
            dve.sem_inc(sel_used, 2)
            dve.sem_inc(agg_evac, START2 + 2)
            dve.sem_inc(lin_done, START1 + 1)
            dve.sem_inc(spmm_done, START2)
            dve.sem_inc(lin_evac, START2)
            dve.sem_inc(raw_stored, START16)
            dve.sem_inc(stats_done, START1)
            V.memset(src_i, 0)
            V.memset(dst_i, 4095).then_inc(padded, 1)
            V.memset(att.rearrange("p e k -> p (e k)"), 0.0).then_inc(padded, 1)
            V.memset(ewt[:, :], 0.0)
            V.memset(sent.rearrange("p e k -> p (e k)"), 0.0)
            V.memset(ones_f, 1.0)
            V.memset(ones_h, 1.0)
            link(V.memset(zero_h, 0.0))
            V.memset(sent[:, :, 0], 4095.0)
            dve.wait_ge(consts_i, 2)
            V.tensor_copy(iot, iot_i)
            link(V.tensor_copy(pidx[:, :], pidx_i[:, :]))
            V.tensor_scalar(pidx_neg[:, :], pidx[:, :], -1.0, None, ALU.mult)
            V.tensor_scalar(ident[:, :], iot[:, 0:P], pidx[:, 0:1], None, ALU.is_equal)
            V.tensor_scalar(ident_h[:, :], iot[:, 0:P], pidx[:, 0:1], None, ALU.is_equal).then_inc(consts, 1)

            dve.wait_ge(edges_loaded, 16 * 4)
            V.tensor_scalar(slo_i, src_i, P - 1, None, ALU.bitwise_and)
            V.tensor_scalar(shi_i, src_i, 7, None, ALU.logical_shift_right)
            V.tensor_scalar(dlo_i, dst_i, P - 1, None, ALU.bitwise_and)
            link(V.tensor_scalar(dhi_i, dst_i, 7, None, ALU.logical_shift_right))
            V.tensor_copy(slo_h, slo_i).then_inc(fields_done, 1)
            V.tensor_copy(shi_h, shi_i)
            V.tensor_copy(dlo_f, dlo_i)
            link(V.tensor_copy(dhi_h, dhi_i))

            def hi_onehot(hi):
                return V.tensor_tensor(oh_hi, hi.unsqueeze(2).broadcast_to((P, EC, NB)),
                                       iot[:, 0:NB].unsqueeze(1).broadcast_to((P, EC, NB)), ALU.is_equal)

            link(hi_onehot(dhi_h))
            with dve.Fori(0, EC // (HB * EB)) as i:
                for t in range(HB):
                    dve.wait_ge(hist_used, HB * i + t + 1)
                    for k in range(EB):
                        last = V.tensor_scalar(hring[:, t * EB + k, :], iot[:, 0:P],
                                               dlo_f[:, ds(i * (HB * EB) + t * EB + k, 1)], None, ALU.is_equal)
                    last.then_inc(hist_ready, 1)

            dve.wait_ge(hist_used, HB + EC // EB + 1)
            deg = bank(6)[:, 0:NB]
            V.tensor_scalar(degs[:, 0, 0, :], deg, 1.0, None, ALU.max)
            V.tensor_scalar(degs[:, 0, 1, :], deg, 1.0, None, ALU.add)
            V.tensor_scalar(degs[:, 4, 0, :], deg, 1.0, None, ALU.min)
            link(V.memset(degs[:, 4, 1, :], 1.0))
            V.reciprocal(degs[:, 1, :, :], degs[:, 0, :, :]).then_inc(root_in, 1)
            V.scalar_tensor_tensor(tab[:, :, 0], src_i, 4096.0, dst_i, ALU.mult, ALU.add)
            dve.wait_ge(slo_loaded, 64)
            q = P * EC // 4
            for i in (2, 3):
                last = V.tensor_scalar(slo_bc[:, i * q:(i + 1) * q], slo_bc[:, i * q:(i + 1) * q], pidx[:, 0:1],
                                       None, ALU.is_equal)
            last.then_inc(onehot_t, 1)
            dve.wait_ge(root_out, 1)
            link(V.tensor_tensor(degs[:, 3, :, :], degs[:, 2, :, :], degs[:, 2, :, :], ALU.mult))
            link(V.tensor_tensor(degs[:, 3, :, :], degs[:, 3, :, :], degs[:, 0, :, :], ALU.mult))
            link(V.tensor_scalar(degs[:, 3, :, :], degs[:, 3, :, :], -0.5, 1.5, ALU.mult, ALU.add))
            link(V.tensor_tensor(degs[:, 3, :, :], degs[:, 3, :, :], degs[:, 2, :, :], ALU.mult))
            link(V.tensor_tensor(degs[:, 1, :, :], degs[:, 3, :, :], degs[:, 4, :, :], ALU.mult))
            V.tensor_scalar(degs[:, 5, :, :], degs[:, 1, :, :], 1.0 / S_BN, None, ALU.mult).then_inc(deg_done, 1)
            V.tensor_scalar(scl[:, :, :], degs[:, 1, :, :], S_BN, None, ALU.mult)
            link(V.tensor_scalar(degs[:, 2, 0, :], degs[:, 1, 0, :], S_TAB, None, ALU.mult))
            link(V.tensor_copy(dtab[:, 0, :], degs[:, 2, 0, :]))
            V.tensor_tensor(dtab[:, 1, :], degs[:, 2, 0, :], dtab[:, 0, :], ALU.subtract).then_inc(tab_ready, 1)

            link(hi_onehot(shi_h))
            n0 = link.n

            def lookup(i):
                link.n = n0 + 4 * i
                for t in range(2):
                    e0 = i * (2 * SB) + t * SB
                    v = sel[t].rearrange("p (e b) -> p e b", b=NB)
                    dve.wait_ge(sel_ready, 2 * i + t + 1)
                    link(V.tensor_tensor(v, bank(6 + t)[:, 0:SB * NB].rearrange("p (e b) -> p e b", b=NB),
                                         oh_hi[:, ds(e0, SB), :], ALU.mult))
                    dve.sem_inc(sel_used, 1)
                    link(V.tensor_reduce(dinvs[:, ds(e0, SB)], v, AX.X, ALU.add))

            def values(lo, hi):
                d = dinvs[:, lo:hi]
                steps(V.tensor_scalar(d, d, S_BN / S_TAB, None, ALU.mult))
                V.tensor_tensor(tab[:, lo:hi, 1:FLD], att[:, lo:hi, :], d.unsqueeze(2).broadcast_to((P, hi - lo, 4)),
                                ALU.mult).then_inc(table_done, 1)

            dve.wait_ge(attr_loaded, 32)
            steps = Steps(dve, table_step)
            with dve.Fori(0, HALF1) as i:
                lookup(i)
            link.n = n0 + 4 * HALF1
            values(0, EH)
            with dve.Fori(HALF1, EC // (2 * SB)) as i:
                lookup(i)
            link.n = n0 + 4 * (EC // (2 * SB))
            values(EH, EC)

            link(V.tensor_scalar(dwl_i, dst_i.rearrange("p (g x) -> p g x", x=WD)[:, :, WD - 1], 4, None,
                                 ALU.logical_shift_right))
            link(V.tensor_copy(dwl_h, dwl_i))
            link(V.tensor_tensor(cmp_h, iot[:, 0:NW].unsqueeze(2).broadcast_to((P, NW, 26)),
                                 dwl_h.unsqueeze(1).broadcast_to((P, NW, 26)), ALU.is_gt))
            V.tensor_reduce(part, cmp_h, AX.X, ALU.add).then_inc(part_ready, 1)
            link(V.memset(starts[:, :, :], 0))
            dve.wait_ge(starts_ready, 1)
            V.tensor_copy(starts[:, 0, 0:1], bank(5)[:, 32:33])
            link(V.tensor_copy(starts[0:NWH[1], 1, 0:1], bank(5)[0:NWH[1], 33:34]))
            V.tensor_scalar(starts[:, :, 1], starts[:, :, 0], COPIES - 1, None, ALU.bitwise_and)
            link(V.tensor_scalar(starts[:, :, 2], starts[:, :, 0], 3, None, ALU.logical_shift_right))
            link(V.scalar_tensor_tensor(starts[:, :, 3], starts[:, :, 1], float(CPR), starts[:, :, 2], ALU.mult, ALU.add))
            for k in range(KW):
                last = V.tensor_scalar(idx[:, :].rearrange("p (h k) -> p h k", k=KW)[:, :, k], starts[:, :, 3],
                                       float(1 + k), None, ALU.add)
            last.then_inc(idx_ready, 1)

            def split(b, r, f):
                val = bank(2 * (f % 2), 2).rearrange("p (k w) -> p k w", w=2 * P)[:, 0:KW, 0:NW]
                v = [v3[:, :, 4 * a + f - 1].rearrange("p (k w) -> p k w", w=NW) for a in range(3)]
                q1, q2 = (x.rearrange("p (k w) -> p k w", w=NW) for x in (rest1, rest2))
                dve.wait_ge(b.turned, START1 + FLD * r + f + 1)
                link(V.tensor_copy(v[0], val))
                link(V.tensor_tensor(q1, val, v[0], ALU.subtract))
                dve.sem_inc(b.turned_used, 1)
                link(V.tensor_copy(v[1], q1))
                link(V.tensor_tensor(q2, q1, v[1], ALU.subtract))
                link(V.tensor_copy(v[2], q2))

            def fields(b, r):
                dve.wait_ge(b.turned, START1 + FLD * r + 1)
                k3 = [x.rearrange("p (k w) -> p k w", w=NW) for x in (key_i, fa_i, mask)]
                link(V.tensor_copy(k3[0], bank(0, 2).rearrange("p (k w) -> p k w", w=2 * P)[:, 0:KW, 0:NW]))
                dve.sem_inc(b.turned_used, 1)
                link(V.tensor_scalar(fa_i, key_i, 4, 255, ALU.logical_shift_right, ALU.bitwise_and))
                V.tensor_tensor(k3[2], k3[1], iot_i[:, 0:NW].unsqueeze(1).broadcast_to((P, KW, NW)), ALU.is_equal)
                link(V.tensor_scalar(fb_i, key_i, 19, None, ALU.logical_shift_right))
                link(V.tensor_scalar(fa_i, key_i, WD - 1, None, ALU.bitwise_and))
                V.scalar_tensor_tensor(key2, fb_i, float(WD), fa_i, ALU.mult, ALU.add)
                link(V.scalar_tensor_tensor(dlom, fa_i, 1.0, mask, ALU.add, ALU.mult))
                link(V.tensor_scalar(fb_i, key_i, 12, P - 1, ALU.logical_shift_right, ALU.bitwise_and))
                link(V.scalar_tensor_tensor(slom, fb_i, 1.0, mask, ALU.add, ALU.mult))

            def one_hots(b, r, w0, step, s):
                dve.wait_ge(b.sums_done, r * STEPS + step + 1)
                d4 = dlom.rearrange("p (k w) -> p k w", w=NW)[:, :, ds(w0, GWIN)]
                V.tensor_tensor(ringd[:, ds(s, 1), :, :, :].rearrange("p s k w c -> p (s k) w c"), d4.unsqueeze(3).broadcast_to((P, KW, GWIN, WD)),
                                iot[:, 1:WD + 1].unsqueeze(1).unsqueeze(1).broadcast_to((P, KW, GWIN, WD)), ALU.is_equal)
                for u in range(GWIN):
                    dve.wait_ge(b.ring_used, r * NW + w0 + u + 1)
                    for k in range(KW):
                        at = ds(w0 + (k * NW + u), 1)
                        if b is slow or k < KW - 1:
                            V.tensor_scalar(ring1[:, KW * u + k, :], iot[:, 1:P + 1], slom[:, at], None, ALU.is_equal)
                        last = V.tensor_scalar(ring2[:, KW * u + k, :], iot[:, 0:HC], key2[:, at], None, ALU.is_equal)
                    last.then_inc(b.ring_ready, 1)

            dve.wait_ge(zero_stored, 16 * 6)
            dve.wait_ge(table_stored, 16 * (3 * COPIES + 1))
            n0 = link.n
            fields(fast, 0)
            V.tensor_reduce(flag_f[:, 0:1], mask, AX.X, ALU.add).then_inc(captured, 1)
            dve.wait_ge(captured, 1)
            V.memset(slom_neg[:, NK:NK + GWIN], 0.0)
            link(V.tensor_scalar(slom_neg[:, 0:NK], slom, -1.0, None, ALU.mult))
            dve.sem_inc(keys_ready, 1)
            for f in range(1, FLD):
                split(fast, 0, f)
            round_steps = link.n - n0 - 1
            with dve.Fori(0, CH) as c:
                with dve.Fori(0, CSTEP) as s:
                    one_hots(fast, 0, (c * CSTEP + s) * GWIN, c * CSTEP + s, s)
            dve.wait_ge(cap_summed, 1)
            link(V.tensor_scalar(flag_f[:, 1:2], bank(7)[:, 0:1], float(E), None, ALU.is_equal))
            link(V.tensor_scalar(flag[:, :], flag_f[:, 1:2], -1.0, 1.0, ALU.mult, ALU.add))
            dve.sem_inc(flag_ready, 1)
            dve.wait_ge(fast.win_kept, GWIN + NW)
            general = dve.value_load(flag[0:1, 0:1], min_val=0, max_val=1)
            n0 = link.n
            with dve.If(general):
                dve.wait_ge(fast.es_stored, START16 + 16 * CH)
                dve.wait_ge(adj_stored, 16 * (CH - 1))
                link(V.memset(es_out, 0.0))
                dve.sem_inc(zeros_set, 1)
                for c in range(CH):
                    V.memset(adj[:, c * CF:(c + 1) * CF], 0.0)
                for h in range(2):
                    for k in range(KW):
                        last = V.memset(idx[:, KW * h + k:KW * h + k + 1], 1 + k - KW)
                link(last)
                n1 = link.n
                with dve.Fori(0, ROUNDS) as r:
                    link.n = n1 + r * (round_steps + 1)
                    dve.wait_ge(slow.turned, START1 + FLD * r)
                    link(V.tensor_scalar(idx[:, :], idx[:, :], float(KW), None, ALU.add))
                    dve.sem_inc(idx_ready, 1)
                    fields(slow, r)
                    for f in range(1, FLD):
                        split(slow, r, f)
                    settle(dve)
                    with dve.Fori(0, CH) as c:
                        with dve.Fori(0, CSTEP) as s:
                            step = c * CSTEP + s
                            one_hots(slow, r, step * GWIN, step, s)
                            for u in range(GWIN):
                                dve.wait_ge(slow.ring_used, r * NW + step * GWIN + (GWIN + u + 1))
                                v = adj_chunk(c)[:, :, ds(s * (GWIN * WD) + u * WD, WD)]
                                V.tensor_tensor(v, v, bank(u)[:, 0:HC].rearrange("p (b n) -> p b n", n=WD),
                                                ALU.add).then_inc(slow.win_kept, 1)
                        dve.wait_ge(slow.sums_done, CSTEP + r * STEPS + (c + 1) * CSTEP)
                        dve.wait_ge(es_free, START1 + r * CH + c)
                        V.tensor_copy(es_out[0:12, :], bank(4)[0:12, 0:CW]).then_inc(slow.sums_kept, 1)
                dve.wait_ge(slow.es_stored, 16 * CH * ROUNDS)
                dve.wait_ge(slow.win_kept, GWIN + NW * ROUNDS)
            with dve.Else():
                dve.nop()
            dve.sem_inc(built, 1)
            pad_link = Steps(dve, pad_step)

            def low(part_lo, rows, scale, part_hi):
                return V.scalar_tensor_tensor(part_lo, rows, scale, part_hi, ALU.mult, ALU.subtract)

            for g in range(NG):
                if g == NG - 1:
                    dve.wait_ge(turned_grp, g - 1)
                    dve.wait_ge(parts_hi, g - 1)
                    dve.wait_ge(parts_lo, g - 1)
                    pad_link(V.memset(rbuf[0][:, (GB - 1) * F:GB * F], 0.0))
                    dve.sem_inc(pad_set, 1)
                dve.wait_ge(parts_hi, g + 1)
                for b in range(GB):
                    n = g * GB + b
                    last = low(parts[:, 1, n, :], rbuf[g % 2][:, b * F:(b + 1) * F], scl[:, 0, n:n + 1], parts[:, 0, n, :])
                last.then_inc(parts_lo, 1)
                dve.wait_ge(h_high, g + 1)
                low(hcut[g % 2][:, 1, :, :].rearrange("p h n -> p (h n)"), ptr[g % 2], S_H,
                    hcut[g % 2][:, 0, :, :].rearrange("p h n -> p (h n)")).then_inc(xT_done, 1)

            def weights_low(l):
                for i in range(2):
                    dve.wait_ge(w_high, 2 * l + i + 1)
                    settle(dve)
                    low(wl[:, 1, 2 * i:2 * i + 2, :].rearrange("p k n -> p (k n)"), w_raw, S_W,
                        wl[:, 0, 2 * i:2 * i + 2, :].rearrange("p k n -> p (k n)")).then_inc(w_low, 1)

            def agg_out(l, c, t):
                g = CH * l + c
                dve.wait_ge(bc_loaded, 16 * (g + 1))
                for h in range(2):
                    dve.wait_ge(spmm_done, START2 + 2 * g + h + 1)
                    settle(dve)
                    V.tensor_tensor(acc[t][h], acc[t][h], bc, ALU.mult).then_inc(agg_scaled, 1)
                for h in range(2):
                    dve.wait_ge(agg_high, 2 * g + h + 1)
                    low(agg_p[:, 1, h, :], acc[t][h], S_H, agg_p[:, 0, h, :]).then_inc(agg_evac, 1)

            def chunk_stats(l, c, width):
                dve.wait_ge(lin_evac, START2 + 2 * (CH * l + c) + 2)
                for h in range(2):
                    last = V.bn_stats(stats[:, h, ds(c, 1), :].rearrange("p c s -> p (c s)"), nraw[:, h, 0:width])
                last.then_inc(stats_done, 1)

            def norm_factors(l, steps):
                for h in range(2):
                    last = V.bn_aggr(mv[:, h, :], stats[:, h, :, :].rearrange("p c s -> p (c s)"))
                steps(last)
                steps(V.tensor_scalar(bnsc[:, 0, :], mv[:, :, 1], EPS, None, ALU.add))
                steps(V.reciprocal(bnsc[:, 0, :], bnsc[:, 0, :]))
                dve.sem_inc(var_ready, 1)
                dve.wait_ge(std_ready, l + 1)
                g_l, b_l = (fcol[:, i, ds(l, 1), :].rearrange("p l h -> p (l h)") for i in (1, 2))
                steps(V.tensor_tensor(bnsc[:, 2, :], bnsc[:, 1, :], g_l, ALU.mult))
                steps(V.tensor_tensor(bnsc[:, 3, :], mv[:, :, 0], bnsc[:, 2, :], ALU.mult))
                steps(V.tensor_tensor(bnsc[:, 3, :], b_l, bnsc[:, 3, :], ALU.subtract))
                dve.sem_inc(bn_ready, 1)

            def row_sums(c):
                V.tensor_reduce(dop[:, ds(c, 1), :].rearrange("p c b -> p (c b)"), adj_chunk(c), AX.X, ALU.add).then_inc(dout_part, 1)

            def layer(l, degrees=False):
                weights_low(l)
                agg_out(l, 0, 0)
                if degrees:
                    row_sums(0)
                with dve.Fori(0, CH // 2) as j:
                    for t in range(2):
                        if degrees:
                            row_sums(2 * j + t + 1)
                        agg_out(l, 2 * j + t + 1, 1 - t)
                        chunk_stats(l, 2 * j + t, CW)
                chunk_stats(l, CH - 1, LASTW)
                dve.wait_ge(stats_done, START1 + CH * l + CH)
                settle(dve)
                norm_factors(l, link)

            dve.wait_ge(fcol_loaded, 48)
            link = Steps(dve, vec_step)

            def groups_low(l):
                for g in range(NG):
                    dve.wait_ge(h_high, NG * (l + 1) + g + 1)
                    settle(dve)
                    low(hcut[g % 2][:, 1, :, :].rearrange("p h n -> p (h n)"), rbuf[g % 2], S_H,
                        hcut[g % 2][:, 0, :, :].rearrange("p h n -> p (h n)")).then_inc(xT_done, 1)
                    dve.wait_ge(parts_hi, NG * (l + 1) + g + 1)
                    for b in range(GB):
                        n = g * GB + b
                        last = low(parts[:, 1, n, :], ptr[g % 2][:, b * F:(b + 1) * F], scl[:, 0, n:n + 1], parts[:, 0, n, :])
                    last.then_inc(parts_lo, 1)

            layer(0, degrees=True)
            groups_low(0)
            dve.wait_ge(dout_part, CH)
            V.tensor_reduce(dop[:, CH, :], dop[:, 0:CH, :].rearrange("p c b -> p b c"), AX.X, ALU.add).then_inc(dout_ready, 1)
            per_layer = link.n
            with dve.Fori(1, LAYERS - 1) as l:
                link.n = per_layer * l
                layer(l)
                groups_low(l)
            link.n = per_layer * (LAYERS - 1)
            layer(LAYERS - 1)

            def layer_norm(v, rows, nb, n, meanwhile=None):
                for b in range(nb):
                    last = V.bn_stats(ln_st[0:rows, b, :], v[:, b, :])
                link(last)
                settle(dve)
                for b in range(nb):
                    last = V.bn_aggr(ln_mv[0:rows, b, :], ln_st[0:rows, b, :])
                link(last)
                link(V.tensor_scalar(ln_r[0:rows, 0, 0:nb], ln_mv[0:rows, 0:nb, 1], EPS, None, ALU.add))
                link(V.reciprocal(ln_r[0:rows, 0, 0:nb], ln_r[0:rows, 0, 0:nb]))
                dve.sem_inc(ln_var, 1)
                if meanwhile:
                    meanwhile()
                dve.wait_ge(ln_std, n)
                for b in range(nb):
                    last = V.tensor_scalar(v[:, b, :], v[:, b, :], ln_mv[0:rows, b, 0:1], ln_r[0:rows, 1, b:b + 1],
                                           ALU.subtract, ALU.mult)
                link(last)

            def first_low(g):
                dve.wait_ge(parts_hi, NG * LAYERS + g + 1)
                for b in range(GB):
                    last = low(parts[:, 1, g * GB + b, :], xgrp[g % 2][:, b * F:(b + 1) * F], S_LN,
                               parts[:, 0, g * GB + b, :])
                last.then_inc(parts_lo, 1)

            for g in range(NG):
                xg = xgrp[g % 2].rearrange("p (b f) -> p b f", f=F)
                if g == NG - 1:
                    dve.wait_ge(x_stored, 16 * (g - 1))
                    dve.wait_ge(parts_hi, NG * LAYERS + g - 1)
                    dve.wait_ge(parts_lo, NG * LAYERS + g - 1)
                    link(V.memset(xg[:, GB - 1, :], 0.0))
                    dve.sem_inc(pad_set, 1)
                dve.wait_ge(turned_grp, NG * LAYERS + g + 1)
                dve.wait_ge(x_loaded[g % 2], 16 * (g // 2 + 1) + 16 * (g == NG - 1))
                link(V.tensor_tensor(xgrp[g % 2], ptr[g % 2], xgrp[g % 2], ALU.add))
                layer_norm(xg, P, GB, g + 1, (lambda: first_low(g - 1)) if g else None)
                dve.sem_inc(ln_rows, 1)
            first_low(NG - 1)

            dve.wait_ge(rows_loaded, 32)
            link(V.tensor_scalar(nrow[:, 1, :], nrow[:, 2, :], 1.0, None, ALU.min))
            link(V.tensor_scalar(nrow[:, 0, :], nrow[:, 2, :], 1.0, None, ALU.max))
            link(V.reciprocal(nrow[:, 0, :], nrow[:, 0, :]))
            link(V.tensor_tensor(nrow[:, 0, :], nrow[:, 0, :], nrow[:, 1, :], ALU.mult))

            def rows_low(ph, g):
                dve.wait_ge(parts_hi, NG * (LAYERS + ph) + g + 1)
                for b in range(GB):
                    n = g * GB + b
                    last = low(parts[:, 1, n, :], rbuf[GSLOT[g]][:, b * F:(b + 1) * F],
                               scl[:, 1, n:n + 1] if ph < 3 else S_LN, parts[:, 0, n, :])
                last.then_inc(parts_lo, 1)

            ln_n = NG
            for ph in range(4):
                if ph:
                    for g in range(1, NG):
                        rows_low(ph, g)
                dve.wait_ge(bias_loaded, 32 * (ph + 1))
                if ph == 3:
                    dve.wait_ge(wt_done, 1)
                    link(V.tensor_copy(wd.rearrange("p h n -> p (h n)"), bank(6)))
                    dve.sem_inc(wt_kept, 1)
                row_bias = bias[0:SW, :]

                def rows_out(c, t, j, ph=ph):
                    g = CH * (LAYERS + ph) + c
                    k = [4, 3][t] * ph + j + 1
                    v = rbuf[t][0:SW, 0:SUBS * F].rearrange("p (s f) -> p s f", f=F)
                    dve.wait_ge(xr_loaded[t], 16 * k)
                    col = lambda i, s: nrow[:, i, ds(c * SUBS + s, 1)]
                    if ph in (0, 3):
                        for s in range(SUBS):
                            last = V.scalar_tensor_tensor(v[:, s, :], row_bias, col(1 if ph == 0 else 2, s), v[:, s, :], ALU.mult, ALU.add)
                        link(last)
                    dve.wait_ge(lin_done, START1 + g + 2)
                    for s in range(SUBS):
                        if ph == 0:
                            last = V.scalar_tensor_tensor(v[:, s, :], lin_s[0:SW, s, :], col(0, s), v[:, s, :], ALU.mult, ALU.add)
                        elif ph == 3:
                            last = V.tensor_tensor(v[:, s, :], lin_s[0:SW, s, :], v[:, s, :], ALU.add)
                        else:
                            last = V.scalar_tensor_tensor(tmp[0:SW, s, :], lin_s[0:SW, s, :], col(3, s), row_bias, ALU.mult, ALU.add)
                    link(last)
                    dve.sem_inc(lin_evac, 2)
                    if ph in (1, 2):
                        link(V.scalar_tensor_tensor(v, tmp[0:SW, :, :], 0.0, v, ALU.max, ALU.add))
                    if ph == 2:
                        dve.wait_ge(xr2_loaded, 16 * (c + 1))
                        link(V.tensor_tensor(v, v, xr2[0:SW, :, :], ALU.add))
                    if ph != 1:
                        layer_norm(v, SW, SUBS, ln_n + c + 1)
                    dve.sem_inc(y_ready, 1)

                per = [2 + 5, 2, 3 + 5, 2 + 5][ph]
                n0 = link.n
                with dve.Fori(0, CH // 2) as j:
                    for t in range(2):
                        link.n = n0 + per * (2 * j + t)
                        rows_out(2 * j + t, t, j)
                link.n = n0 + per * (CH - 1)
                if ph < 3:
                    rows_low(ph + 1, 0)
                rows_out(CH - 1, 0, CH // 2)
                assert link.n == n0 + per * CH
                if ph != 1:
                    ln_n += CH

        @block.tensor
        def _(pe):
            T = nc.tensor
            pe.wait_ge(consts, 1)
            deg = bank(6)[:, 0:NB]
            T.matmul(deg, zero_h, zero_h[:, 0:NB], start=True, stop=False)
            with pe.Fori(0, EC // (HB * EB)) as i:
                for t in range(HB):
                    pe.wait_ge(hist_ready, HB * i + t + 1)
                    for k in range(EB):
                        last = T.matmul(deg, hring[:, t * EB + k, :],
                                        oh_hi[:, ds(i * (HB * EB) + t * EB + k, 1), :].rearrange("p e b -> p (e b)"),
                                        start=False, stop=False)
                    last.then_inc(hist_used, 1)
            T.matmul(deg, zero_h, zero_h[:, 0:NB], start=False, stop=True).then_inc(hist_used, 1)
            pe.wait_ge(onehot_t, 2)
            pe.wait_ge(tab_ready, 1)
            cols = slo_bc.rearrange("q (p e) -> q p e", e=EC)
            with pe.Fori(0, EC // (2 * SB)) as i:
                for t in range(2):
                    pe.wait_ge(sel_used, 2 * i + t + 1)
                    for k in range(SB):
                        for a in range(2):
                            last = T.matmul(bank(6 + t)[:, NB * k:NB * (k + 1)],
                                            cols[:, :, ds(i * (2 * SB) + t * SB + k, 1)].rearrange("q p e -> q (p e)"),
                                            dtab[:, a, :], start=(a == 0), stop=(a == 1))
                    last.then_inc(sel_ready, 1)
            pe.wait_ge(part_ready, 1)
            T.matmul(bank(5)[:, 32:33], part[:, 0:P], ones_f[:, 0:1], start=True, stop=True)
            T.matmul(bank(5)[0:NWH[1], 33:34], part[:, P:NW], ones_f[:, 0:1], start=True, stop=True).then_inc(starts_ready, 1)

            def turn_fields(b, r):
                pe.wait_ge(b.gathered, 16 * 2 * KW * (r + 1))
                pe.wait_ge(b.win_kept, GWIN + NW * r)
                for f in range(FLD):
                    if f >= 2:
                        pe.wait_ge(b.turned_used, FLD * r + f - 1)
                    to = bank(2 * (f % 2), 2).rearrange("p (k w) -> p k w", w=2 * P)
                    for k in range(KW):
                        for h in range(2):
                            rows = win[h][0:NWH[h], k * ROWE:(k + 1) * ROWE].rearrange("w (e f) -> w e f", f=FLD)[:, :, f]
                            last = T.transpose(to[:, k, h * P:h * P + NWH[h]], rows, ident[0:NWH[h], 0:NWH[h]])
                    last.then_inc(b.turned, 1)

            def windows(b, r):
                with pe.Fori(0, CH) as c:
                    for s in range(CSTEP):
                        w0 = c * (CSTEP * GWIN) + s * GWIN
                        for u in range(GWIN):
                            pe.wait_ge(b.ring_ready, r * NW + w0 + u + 1)
                            if b is fast:
                                pe.wait_ge(onehot_act, w0 + u + 1)
                            pe.wait_ge(b.win_kept, r * NW + w0 + u + 1)
                            for k in range(KW):
                                last = T.matmul(bank(u)[:, 0:HC], ring1[:, KW * u + k, :], ring2[:, KW * u + k, :],
                                                start=(k == 0), stop=(k == KW - 1))
                            last.then_inc(b.ring_used, 1)
                        if s == 0:
                            pe.wait_ge(b.sums_kept, START1 + r * CH + c)
                        for u in range(GWIN):
                            for k in range(KW):
                                last = T.matmul(bank(4)[0:12, (s * GWIN + u) * WD:(s * GWIN + u + 1) * WD],
                                                v3[:, ds(w0 + (k * NW + u), 1), :].rearrange("p e c -> p (e c)"),
                                                ringd[:, s, k, u, :],
                                                start=(k == 0), stop=(k == KW - 1))
                        last.then_inc(b.sums_done, 1)

            turn_fields(fast, 0)
            pe.wait_ge(captured, 1)
            T.matmul(bank(7)[:, 0:1], ones_f, flag_f[:, 0:1], start=True, stop=True).then_inc(cap_summed, 1)
            windows(fast, 0)
            pe.wait_ge(flag_ready, 1)
            general = pe.value_load(flag[0:1, 0:1], min_val=0, max_val=1)
            with pe.If(general):
                with pe.Fori(0, ROUNDS) as r:
                    turn_fields(slow, r)
                    windows(slow, r)
            with pe.Else():
                pe.nop()

            def turn_input(g):
                pe.wait_ge(grp_loaded[g % 2], 16 * (g // 2 + 1) + 16 * (g == NG - 1))
                if g >= 2:
                    pe.wait_ge(xT_done, g - 1)
                for b in range(GB):
                    for h in range(2):
                        last = T.transpose(ptr[g % 2][:, h * GW + b * P:h * GW + (b + 1) * P],
                                           rbuf[g % 2][:, b * F + h * P:b * F + (h + 1) * P], ident[:, :])
                last.then_inc(turned_grp, 1)

            def turn_output(l, g):
                pe.wait_ge(norm_done, NG * l + g + 1)
                v = rbuf[g % 2].rearrange("p (h n) -> p h n", h=2)
                for b in range(GB):
                    for h in range(2):
                        last = T.transpose(ptr[g % 2][:, b * F + h * P:b * F + (h + 1) * P],
                                           v[:, h, b * P:(b + 1) * P], ident[:, :])
                last.then_inc(turned_grp, 1)

            def turn_batch(l, k, m):
                pe.wait_ge(adj_turned_out, (l * (CH - 1) + k) * TURNS + m + 1)
                for i in range(GB):
                    if m < NG:
                        rows = adj_chunk(k + 1)[:, m * GB + i, ds(l * SW, SW)]
                    else:
                        rows = adj_chunk(0)[:, ds(k * 4 + i, 1), ds(l * SW, SW)].rearrange("p b n -> p (b n)")
                    last = T.transpose(turn_ps[m % 2][:, i * P:(i + 1) * P], rows, ident_h[:, :])
                last.then_inc(adj_turned, 1)

            def blocks(c, t, bs, edges):
                for b in bs:
                    for a in range(2):
                        for h in range(2):
                            ends = not edges and b == NB - 1 and a == 1
                            last = T.matmul(acc[t][h], parts[:, a, b, h * P:(h + 1) * P], adj_chunk(c)[:, b, :],
                                            start=(b == 0 and a == 0), stop=ends)
                            if ends:
                                last.then_inc(spmm_done, 1)

            def edge_term(g, t):
                pe.wait_ge(es_loaded, 16 * (g + 1))
                for h in range(2):
                    T.matmul(acc[t][h], ewt[:, h * P:(h + 1) * P], es[0:12, :], start=False,
                             stop=True).then_inc(spmm_done, 1)

            def product(g, c, t, edges, turn_l=None):
                pe.wait_ge(agg_evac, START2 + 2 * g)
                for m in range(NG):
                    blocks(c, t, range(m * GB, (m + 1) * GB), edges)
                    if turn_l is not None:
                        turn_batch(turn_l, c - 1, m)
                if turn_l is not None:
                    turn_batch(turn_l, c - 1, NG)
                if edges:
                    edge_term(g, t)

            def first_product(g, k0, layer=None, turn_group=None):
                edges = layer is not None
                pe.wait_ge(agg_evac, START2 + 2 * g)
                if turn_group:
                    turn_group(0)
                    turn_group(1)
                for k in range(NG):
                    pe.wait_ge(parts_hi, k0 + k + 1)
                    pe.wait_ge(parts_lo, k0 + k + 1)
                    if turn_group and k + 2 < NG and not edges:
                        turn_group(k + 2)
                    blocks(0, 0, range(k * GB, (k + 1) * GB), edges)
                    if turn_group and k + 2 < NG and edges:
                        turn_group(k + 2)
                if turn_group is turn_input:
                    pe.wait_ge(xT_done, NG)
                if edges:
                    pe.wait_ge(ew_loaded, 16 * 6 * (layer + 1))
                    edge_term(g, 0)

            def linear(l, c, t, j):
                g = CH * l + c
                pe.wait_ge(w_low, 2 * (l + 1))
                pe.wait_ge(hT_loaded[t], 16 * ([4, 3][t] * l + j + 1))
                pe.wait_ge(agg_evac, START2 + 2 * g + 4)
                pe.wait_ge(lin_evac, START2 + 2 * g)
                hc = rbuf[t][:, 0:2 * CW].bitcast(f16).rearrange("p (a h n) -> p a h n", a=2, n=CW)
                for h in range(2):
                    for k in range(4):
                        for a, b in ((0, 0), (0, 1), (1, 0)):
                            last = T.matmul(lin_h[h], wl[:, a, k, h * P:(h + 1) * P],
                                            hc[:, b, k, :] if k < 2 else agg_p[:, b, k - 2, :],
                                            start=(k == 0 and a == 0 and b == 0), stop=(k == 3 and a == 1))
                last.then_inc(lin_done, 1)

            def layer(l, turning, turn_group):
                turn_l = l if turning else None
                first_product(CH * l, NG * l, l, turn_group)
                with pe.Fori(0, CH // 2) as j:
                    for t in range(2):
                        product(CH * l + 2 * j + t + 1, 2 * j + t + 1, 1 - t, True, turn_l)
                        linear(l, 2 * j + t, t, j)
                linear(l, CH - 1, 0, CH // 2)

            pe.wait_ge(built, 1)
            layer(0, True, turn_input)
            with pe.Fori(1, LAYERS - 1) as l:
                layer(l, True, lambda g: turn_output(l - 1, g))
            layer(LAYERS - 1, False, lambda g: turn_output(LAYERS - 2, g))

            for ph in range(4):
                base = CH * (LAYERS + ph)
                def operator_ready(c, ph=ph):
                    if ph == 0:
                        pe.wait_ge(op_loaded, 16 * (c + 1))
                    elif ph == 1:
                        pe.wait_ge(eye_added, c + 1)
                    elif ph == 3:
                        pe.wait_ge(op_loaded, 16 * (2 * CH + c + 1))

                def chunk_product(c, t, base=base):
                    operator_ready(c)
                    product(base + c, c, t, False)

                def chunk_linear(c, base=base):
                    g = base + c
                    pe.wait_ge(agg_evac, START2 + 2 * g + 4)
                    pe.wait_ge(lin_evac, START2 + 2 * g)
                    for s in range(SUBS):
                        for h in range(2):
                            last = T.matmul(lin_s[0:SW, s, :], agg[:, h, s * SW:(s + 1) * SW], wd[:, h, :],
                                            start=(h == 0), stop=(h == 1))
                    last.then_inc(lin_done, 1)

                operator_ready(0)
                first_product(base, NG * (LAYERS + ph),
                              turn_group=(lambda g: turn_output(LAYERS - 1, g)) if ph == 0 else None)
                if ph == 3:
                    pe.wait_ge(bias_loaded, 32 * 4)
                    for k in range(2):
                        for h in range(2):
                            last = T.transpose(bank(6)[:, h * F + k * P:h * F + (k + 1) * P],
                                               wt[:, k, h * P:(h + 1) * P], ident[:, :])
                    last.then_inc(wt_done, 1)
                    pe.wait_ge(wt_kept, 1)
                else:
                    pe.wait_ge(bias_loaded, 32 * (ph + 1))
                with pe.Fori(0, CH // 2) as j:
                    for t in range(2):
                        chunk_product(2 * j + t + 1, 1 - t)
                        chunk_linear(2 * j + t)
                chunk_linear(CH - 1)


def kernel(**inputs):
    import numpy as np
    import concourse.bacc as bacc
    from concourse.bass_utils import run_bass_kernel_spmd

    nc = bacc.Bacc("TRN2", target_bir_lowering=False, num_devices=1)
    arrays, args = {}, []
    for name in INPUTS:
        a = np.ascontiguousarray(inputs[name])
        arrays[f"in_{name}"] = a
        args.append(nc.dram_tensor(f"in_{name}", a.shape, mybir.dt.from_np(a.dtype), kind="ExternalInput").ap())
    args.append(nc.dram_tensor("out", (N, F), mybir.dt.float32, kind="ExternalOutput").ap())
    build(nc, *args)
    r = run_bass_kernel_spmd(nc, [arrays], core_ids=[0])
    return r.results[0]["out"]
```
